# Optimizing a Trainium2 kernel written in Bass

```python
import numpy as np
import jax
import jax.numpy as jnp

def _softmax(x, axis=-1):
    return jax.nn.softmax(x, axis=axis)

def _gelu(x):
    return jax.nn.gelu(x, approximate=True)

def _silu(x):
    return jax.nn.silu(x)

def _sigmoid(x):
    return jax.nn.sigmoid(x)

def _layernorm(x, axis=-1, eps=1e-05):
    m = jnp.mean(x, axis=axis, keepdims=True)
    v = jnp.var(x, axis=axis, keepdims=True)
    return (x - m) / jnp.sqrt(v + eps)

def _scatter_add(tgt, idx, src, axis=0):
    return tgt.at[idx].add(src)

def _segment_sum(src, seg, n):
    return jax.ops.segment_sum(src, seg, n)
kernel_name = 'mk_decoder_preln_d1_seqx_r4_92a573'

def setup_inputs(seed: int=0):
    np.random.seed(seed)
    _w = jnp.asarray

    def _rec_inputs():
        import jax
        import jax.numpy as jnp
        _rk = jax.random.key(seed)
        x = 7.22e-05 + 1 * jax.random.normal(jax.random.fold_in(_rk, 1), (1, 2048, 256), jnp.float32)
        _lenS = 2048 - jax.random.randint(jax.random.fold_in(_rk, 7), (1,), 0, max(1, 2048 // 4) + 1, jnp.int32)
        _lenS2 = 1601 - jax.random.randint(jax.random.fold_in(_rk, 8), (1,), 0, max(1, 1601 // 4) + 1, jnp.int32)
        _ctx_768P = jax.random.normal(jax.random.fold_in(_rk, 11), (1, 16, 192), jnp.float32)
        _ctx_768c = jax.random.dirichlet(jax.random.fold_in(_rk, 511), 0.3 * jnp.ones((16,), jnp.float32), (1, 1601))
        _ctx_768t = jnp.einsum('bsk,bkd->bsd', _ctx_768c, _ctx_768P)
        _ctx_768t = _ctx_768t * jax.lax.rsqrt(jnp.mean(jnp.square(_ctx_768t)) + 1e-12) * 0.953939
        ctx_768 = -0.000191848 + 0.999787 * (_ctx_768t + 0.3 * jax.random.normal(jax.random.fold_in(_rk, 611), (1, 1601, 192), jnp.float32))
        return (x, ctx_768)
    x, ctx_768 = _rec_inputs()

    def _L0_attn_setup():
        import jax, jax.numpy as jnp
        import numpy as np
        import math
        DIM_EMB = 256
        KSQRT = math.sqrt(DIM_EMB)
        key = jax.random.key(seed)
        ks = jax.random.split(key, 7)
        b, t, e, d = (4, 1024, DIM_EMB, 256)
        s = 1.0 / math.sqrt(e)
        return {'x': jax.random.normal(ks[0], (b, t, e), dtype=jnp.float32), 'Wq': jax.random.normal(ks[1], (d, e), dtype=jnp.float32) * s, 'bq': jax.random.normal(ks[2], (d,), dtype=jnp.float32) * s, 'Wk': jax.random.normal(ks[3], (d, e), dtype=jnp.float32) * s, 'bk': jax.random.normal(ks[4], (d,), dtype=jnp.float32) * s, 'Wv': jax.random.normal(ks[5], (d, e), dtype=jnp.float32) * s, 'bv': jax.random.normal(ks[6], (d,), dtype=jnp.float32) * s}
    _L0_attn_all = _L0_attn_setup()
    _L0_attn_in = {k: v for k, v in _L0_attn_all.items() if k in ('Wq', 'bq', 'Wk', 'bk', 'Wv', 'bv')}
    del _L0_attn_all

    def _L0_xattn_setup():
        import jax, jax.numpy as jnp
        import numpy as np
        N_HEADS = 16
        key = jax.random.key(seed)
        ks = jax.random.split(key, 8)
        b, l, m = (8, 256, 256)
        d_embed, d_cross = (256, 192)
        s_q = 1.0 / np.sqrt(d_embed)
        s_kv = 1.0 / np.sqrt(d_cross)
        return {'x': jax.random.normal(ks[0], (b, l, d_embed), jnp.float32), 'y': jax.random.normal(ks[1], (b, m, d_cross), jnp.float32), 'Wq': jax.random.normal(ks[2], (d_embed, d_embed), jnp.float32) * s_q, 'bq': jax.random.normal(ks[3], (d_embed,), jnp.float32) * 0.01, 'Wkv': jax.random.normal(ks[4], (2 * d_embed, d_cross), jnp.float32) * s_kv, 'bkv': jax.random.normal(ks[5], (2 * d_embed,), jnp.float32) * 0.01, 'Wo': jax.random.normal(ks[6], (d_embed, d_embed), jnp.float32) * s_q, 'bo': jax.random.normal(ks[7], (d_embed,), jnp.float32) * 0.01}
    _L0_xattn_all = _L0_xattn_setup()
    _L0_xattn_in = {k: v for k, v in _L0_xattn_all.items() if k in ('Wq', 'bq', 'Wkv', 'bkv', 'Wo', 'bo')}
    del _L0_xattn_all

    def _L0_ffn_setup():
        import jax, jax.numpy as jnp
        import numpy as np
        H = 16
        EPS = 1e-05

        def layernorm(x, g, b):
            m = jnp.mean(x, axis=-1, keepdims=True)
            v = jnp.mean((x - m) ** 2, axis=-1, keepdims=True)
            return (x - m) * jax.lax.rsqrt(v + EPS) * g + b
        key = jax.random.key(seed)
        B, S, D, E = (4, 512, 256, 8)
        ks = jax.random.split(key, 16)
        s = 0.02
        inp = {'x': jax.random.normal(ks[0], (B, S, D), jnp.float32), 'Wq': jax.random.normal(ks[1], (D, D), jnp.float32) * s, 'bq': jnp.zeros((D,), jnp.float32), 'Wk': jax.random.normal(ks[2], (D, D), jnp.float32) * s, 'bk': jnp.zeros((D,), jnp.float32), 'Wv': jax.random.normal(ks[3], (D, D), jnp.float32) * s, 'bv': jnp.zeros((D,), jnp.float32), 'Wo': jax.random.normal(ks[4], (D, D), jnp.float32) * s, 'bo': jnp.zeros((D,), jnp.float32), 'g1': jnp.ones((D,), jnp.float32), 'be1': jnp.zeros((D,), jnp.float32), 'g2': jnp.ones((D,), jnp.float32), 'be2': jnp.zeros((D,), jnp.float32), 'Wg': jax.random.normal(ks[5], (D, E), jnp.float32) * s, 'bg': jnp.zeros((E,), jnp.float32), 'We': jax.random.normal(ks[6], (E, D, D), jnp.float32) * s, 'bexp': jnp.zeros((E, D), jnp.float32)}
        return inp
    _L0_ffn_all = _L0_ffn_setup()
    _L0_ffn_in = {k: v for k, v in _L0_ffn_all.items() if k in ('Wq', 'bq', 'Wk', 'bk', 'Wv', 'bv', 'Wo', 'bo', 'g1', 'be1', 'g2', 'be2', 'Wg', 'bg', 'We', 'bexp')}
    del _L0_ffn_all
    return {'x': x, 'ctx_768': ctx_768, 'L0_attn_Wq': _L0_attn_in['Wq'], 'L0_attn_bq': _L0_attn_in['bq'], 'L0_attn_Wk': _L0_attn_in['Wk'], 'L0_attn_bk': _L0_attn_in['bk'], 'L0_attn_Wv': _L0_attn_in['Wv'], 'L0_attn_bv': _L0_attn_in['bv'], 'L0_xattn_Wq': _L0_xattn_in['Wq'], 'L0_xattn_bq': _L0_xattn_in['bq'], 'L0_xattn_Wkv': _L0_xattn_in['Wkv'], 'L0_xattn_bkv': _L0_xattn_in['bkv'], 'L0_xattn_Wo': _L0_xattn_in['Wo'], 'L0_xattn_bo': _L0_xattn_in['bo'], 'L0_ffn_Wq': _L0_ffn_in['Wq'], 'L0_ffn_bq': _L0_ffn_in['bq'], 'L0_ffn_Wk': _L0_ffn_in['Wk'], 'L0_ffn_bk': _L0_ffn_in['bk'], 'L0_ffn_Wv': _L0_ffn_in['Wv'], 'L0_ffn_bv': _L0_ffn_in['bv'], 'L0_ffn_Wo': _L0_ffn_in['Wo'], 'L0_ffn_bo': _L0_ffn_in['bo'], 'L0_ffn_g1': _L0_ffn_in['g1'], 'L0_ffn_be1': _L0_ffn_in['be1'], 'L0_ffn_g2': _L0_ffn_in['g2'], 'L0_ffn_be2': _L0_ffn_in['be2'], 'L0_ffn_Wg': _L0_ffn_in['Wg'], 'L0_ffn_bg': _L0_ffn_in['bg'], 'L0_ffn_We': _L0_ffn_in['We'], 'L0_ffn_bexp': _L0_ffn_in['bexp']}

def reference(x, ctx_768, L0_attn_Wq, L0_attn_bq, L0_attn_Wk, L0_attn_bk, L0_attn_Wv, L0_attn_bv, L0_xattn_Wq, L0_xattn_bq, L0_xattn_Wkv, L0_xattn_bkv, L0_xattn_Wo, L0_xattn_bo, L0_ffn_Wq, L0_ffn_bq, L0_ffn_Wk, L0_ffn_bk, L0_ffn_Wv, L0_ffn_bv, L0_ffn_Wo, L0_ffn_bo, L0_ffn_g1, L0_ffn_be1, L0_ffn_g2, L0_ffn_be2, L0_ffn_Wg, L0_ffn_bg, L0_ffn_We, L0_ffn_bexp):
    import jax
    import jax.numpy as jnp

    def _L0_attn_ref(x, Wq, bq, Wk, bk, Wv, bv):
        import jax, jax.numpy as jnp
        import numpy as np
        import math
        DIM_EMB = 256
        KSQRT = math.sqrt(DIM_EMB)
        q = jnp.einsum('bte,de->btd', x, Wq) + bq
        k = jnp.einsum('bte,de->btd', x, Wk) + bk
        v = jnp.einsum('bte,de->btd', x, Wv) + bv
        dot = jnp.einsum('bqd,bkd->bqk', q, k) / KSQRT
        p = jax.nn.softmax(dot, axis=-1)
        z = jnp.einsum('bqk,bkd->bqd', p, v)
        return z

    def _L0_xattn_ref(x, y, Wq, bq, Wkv, bkv, Wo, bo):
        import jax, jax.numpy as jnp
        import numpy as np
        N_HEADS = 16
        b, l, d = x.shape
        m = y.shape[1]
        h = N_HEADS
        dh = d // h
        q = (jnp.einsum('bld,ed->ble', x, Wq) + bq).reshape(b, l, h, dh)
        kv = (jnp.einsum('bmc,ec->bme', y, Wkv) + bkv).reshape(b, m, h, 2 * dh)
        k, v = (kv[..., :dh], kv[..., dh:])
        scale = 1.0 / jnp.sqrt(jnp.asarray(dh, x.dtype))
        att = jax.nn.softmax(jnp.einsum('blhd,bmhd->blmh', q, k) * scale, axis=2)
        out = jnp.einsum('blmh,bmhd->blhd', att, v).reshape(b, l, d)
        return jnp.einsum('bld,ed->ble', out, Wo) + bo

    def _L0_ffn_ref(x, Wq, bq, Wk, bk, Wv, bv, Wo, bo, g1, be1, g2, be2, Wg, bg, We, bexp):
        import jax, jax.numpy as jnp
        import numpy as np
        H = 16
        EPS = 1e-05

        def layernorm(x, g, b):
            m = jnp.mean(x, axis=-1, keepdims=True)
            v = jnp.mean((x - m) ** 2, axis=-1, keepdims=True)
            return (x - m) * jax.lax.rsqrt(v + EPS) * g + b
        B, S, D = x.shape
        Dh = D // H
        TOP_K = 2
        q = (x @ Wq + bq).reshape(B, S, H, Dh)
        k = (x @ Wk + bk).reshape(B, S, H, Dh)
        v = (x @ Wv + bv).reshape(B, S, H, Dh)
        scores = jnp.einsum('bqhd,bkhd->bhqk', q, k) / jnp.sqrt(jnp.float32(Dh))
        attn = jax.nn.softmax(scores, axis=-1)
        ctx = jnp.einsum('bhqk,bkhd->bqhd', attn, v).reshape(B, S, D)
        attn_out = ctx @ Wo + bo
        x = x + layernorm(attn_out, g1, be1)
        gate_probs = jax.nn.softmax(x @ Wg + bg, axis=-1)
        top_vals, top_idx = jax.lax.top_k(gate_probs, TOP_K)
        all_out = jnp.einsum('bsd,edf->bsef', x, We) + bexp
        picked = jnp.take_along_axis(all_out, top_idx[..., None], axis=2)
        moe_out = jnp.sum(top_vals[..., None] * picked, axis=2)
        return x + layernorm(moe_out, g2, be2)
    x = x + _L0_attn_ref(_layernorm(x, axis=-1), L0_attn_Wq, L0_attn_bq, L0_attn_Wk, L0_attn_bk, L0_attn_Wv, L0_attn_bv)
    x = x + _L0_xattn_ref(_layernorm(x, axis=-1), ctx_768, L0_xattn_Wq, L0_xattn_bq, L0_xattn_Wkv, L0_xattn_bkv, L0_xattn_Wo, L0_xattn_bo)
    x = x + _L0_ffn_ref(_layernorm(x, axis=-1), L0_ffn_Wq, L0_ffn_bq, L0_ffn_Wk, L0_ffn_bk, L0_ffn_Wv, L0_ffn_bv, L0_ffn_Wo, L0_ffn_bo, L0_ffn_g1, L0_ffn_be1, L0_ffn_g2, L0_ffn_be2, L0_ffn_Wg, L0_ffn_bg, L0_ffn_We, L0_ffn_bexp)
    return x

_drawn_inputs = setup_inputs


def setup_inputs(seed=0):
    import zlib

    import numpy as np

    out = dict(_drawn_inputs(seed))
    spreads = {'L0_ffn_bq': (0.0, 0.8),
     'L0_ffn_bk': (0.0, 2.0),
     'L0_ffn_bv': (0.0, 0.1),
     'L0_ffn_bo': (0.0, 0.1),
     'L0_ffn_g1': (1.0, 0.2),
     'L0_ffn_be1': (0.0, 0.1),
     'L0_ffn_g2': (1.0, 0.2),
     'L0_ffn_be2': (0.0, 0.1),
     'L0_ffn_bg': (0.0, 0.1),
     'L0_ffn_bexp': (0.0, 0.1)}
    factors = {'L0_attn_bk': 64.0,
     'L0_xattn_bq': 7.368,
     'L0_ffn_Wq': 3.793,
     'L0_ffn_Wk': 3.683,
     'L0_attn_bq': 2.847}
    for name, (base, spread) in spreads.items():
        noise = np.random.default_rng([zlib.crc32(name.encode()), seed]).standard_normal(out[name].shape)
        drawn = base * np.exp(spread * noise) if base else spread * noise
        out[name] = jnp.asarray(drawn.astype(out[name].dtype))
    for name, factor in factors.items():
        out[name] = (out[name] * factor).astype(out[name].dtype)
    return out
```

```python
from contextlib import ExitStack

import concourse.bass as bass
from concourse import mybir

F32 = mybir.dt.float32
BF16 = mybir.dt.bfloat16
ALU = mybir.AluOpType
ACT = mybir.ActivationFunctionType
AX = mybir.AxisListType
ds = bass.ds

P = 128
D = 256
DC = D // P
N = 2048
NT = N // P
CH = 512
NCH = N // CH
H = 16
DH = D // H
HG = 4
NG = H // HG
CTX = 1601
CW = 192
NE = 8
EPS = 1e-5
BANK = 512
ROWS = 6 * DH
MROWS = 3
Q_PARTS = (0, 0, 0, 1, 1, 2)
K_PARTS = (0, 1, 2, 0, 1, 0)
W1Q, W1K, W1V, W2Q, W2O, W3Q, W3K, W3V, W3O = range(9)
B1Q, B1K, B2Q, B2K, B3Q, B3K = range(6)
R1V, R2V, R2O, R3V, R3O, RG1, RBE1, RG2, RBE2 = range(9)


def build(nc, x, ctxT, wpack, wkv, we, wg, bcols, brows, bg, bexp, out):
    with ExitStack() as ctx:
        def sb(name, shape, dt=F32):
            return ctx.enter_context(nc.sbuf_tensor(name, shape, dt))

        def sem(name):
            return ctx.enter_context(nc.semaphore(name))

        PS = ctx.enter_context(nc.psum_tensor("PS", [P, 8, BANK], F32))
        xres = sb("xres", [P, NT, D])
        hA = sb("hA", [P, NT, D])
        hT = sb("hT", [P, DC, N])
        W = sb("W", [P, 9, DC, D])
        Wkv = sb("Wkv", [P, 2, 2 * D])
        Wg = sb("Wg", [P, DC, NE])
        bcol = sb("bcol", [P, 12])
        brow = sb("brow", [P, 9, D])
        bgrow = sb("bgrow", [P, NE])
        bexp_sb = sb("bexp_sb", [NE, D])
        ident = sb("ident", [P, P])
        identb = sb("identb", [P, P], BF16)
        stats = sb("stats", [P, NT, 6])
        mv = sb("mv", [P, NT, 2])
        vareps = sb("vareps", [P, NT])
        mhalf = sb("mhalf", [P, NT])
        rstd = sb("rstd", [P, NT])
        ARENA = 26500
        arena = sb("arena", [P, ARENA])

        def carve(at, shape, dt=F32):
            n = 1
            for d in shape:
                n *= d
            words = n * (2 if dt == BF16 else 4) // 4
            assert at + words <= ARENA, (at, words)
            v = arena[:, at:at + words]
            if dt == BF16:
                v = v.bitcast(BF16)
            names = "abcd"[:len(shape)]
            if len(shape) > 1:
                v = v.rearrange(f"p ({' '.join(names)}) -> p {' '.join(names)}",
                                **dict(zip(names[1:], shape[1:])))
            return v, at + words

        x_in = [sem(f"x_in{g}") for g in range(NCH)]
        w_in = sem("w_in")
        ctx_in = sem("ctx_in")
        late_in = sem("late_in")
        const_rdy = sem("const_rdy")

        xt = x.rearrange("(t p) d -> p t d", p=P)

        qT, a = carve(0, [DC, N])
        kT, a = carve(a, [DC, N])
        V1, a = carve(a, [NT, D])
        qs, a = carve(a, [2, DC, P])
        P1, a = carve(a, [2, N])
        PT, a = carve(a, [2, NT, P])
        rs = sb("rs", [P, 2])
        nmax = sb("nmax", [P, 2])
        nbias = sb("nbias", [P, 2])
        rr = sb("rr", [P, 2])

        sems = {n: sem("a_" + n) for n in (
            "stat", "mv", "var", "rstd", "h", "pe", "act", "dve", "qs", "s", "mx", "nb", "exp", "tr", "pta",
            "ptd", "z", "rr", "x")}
        var_s = sems["var"]
        stat_s, mv_s, rstd_s, h_s, pe_s, act_s, dve_s = (sems[n] for n in (
            "stat", "mv", "rstd", "h", "pe", "act", "dve"))
        qs_s, s_s, mx_s, nb_s, exp_s, tr_s, pta_s, ptd_s, z_s, rr_s, x_s = (sems[n] for n in (
            "qs", "s", "mx", "nb", "exp", "tr", "pta", "ptd", "z", "rr", "x"))

        units = [("T", n, c, True) for n in range(NCH) for c in range(DC)]
        units += [("K", n, m, True) for n in range(NCH) for m in range(DC)]
        units += [("V", v, 0, False) for v in range(NT // 2)]
        units += [("Q", n, m, m == 0) for n in range(NCH) for m in range(DC)]

        def emptied(u):
            same = sum(1 for w in units[:u + 1] if w[3] == units[u][3])
            return (act_s if units[u][3] else dve_s), same

        LATE = 16 * 11
        with nc.Block() as block:
            @block.sync
            def _(sp):
                for g in range(NCH):
                    sp.dma_start(xres[:, 4 * g:4 * g + 4, :], xt[:, 4 * g:4 * g + 4, :]).then_inc(x_in[g], 16)
                    if g == 0:
                        sp.dma_start(W[:, 0:3], wpack[0:3].rearrange("w (c p) d -> p w c d", p=P)).then_inc(w_in, 16)
                        sp.dma_start(bcol[:, :], bcols).then_inc(w_in, 16)
                        sp.dma_start(brow[:, :, :], brows.partition_broadcast(P)).then_inc(w_in, 16)
                for w in range(3, 9):
                    sp.dma_start(W[:, w], wpack[w].rearrange("(c p) d -> p c d", p=P)).then_inc(late_in, 16)
                sp.dma_start(Wkv[:, 0, :], wkv[0:P, :]).then_inc(late_in, 16)
                sp.dma_start(Wkv[0:CW - P, 1, :], wkv[P:CW, :]).then_inc(late_in, 16)
                sp.dma_start(Wg[:, :, :], wg.rearrange("(c p) e -> p c e", p=P)).then_inc(late_in, 16)
                sp.dma_start(bgrow[:, :], bg.partition_broadcast(P)).then_inc(late_in, 16)
                sp.dma_start(bexp_sb[:, :], bexp).then_inc(late_in, 16)

            @block.gpsimd
            def _(pool):
                pool.memset(ident[:, :], 0.0).then_inc(const_rdy, 1)
                pool.memset(identb[:, :], 0.0).then_inc(const_rdy, 1)
                pool.memset(mhalf[:, :], -0.5).then_inc(const_rdy, 1)
                pool.wait_ge(const_rdy, 3)
                for m in (ident, identb):
                    pool.affine_select(out=m[:, :], in_=m[:, :], compare_op=ALU.not_equal, fill=1.0,
                                       base=0, pattern=[[-1, P]], channel_multiplier=1).then_inc(const_rdy, 1)
                for g in range(NCH):
                    r = slice(4 * g, 4 * g + 4)
                    pool.wait_ge(mv_s, 4 * g + 4)
                    pool.tensor_scalar(vareps[:, r], mv[:, r, 1], EPS, None, ALU.add).then_inc(var_s, 1)
                    pool.wait_ge(var_s, g + 1)
                    pool.tensor_tensor(rstd[:, r], vareps[:, r], mhalf[:, r], ALU.pow).then_inc(rstd_s, 1)
                pool.wait_ge(act_s, sum(1 for w in units if w[3]))
                pool.wait_ge(dve_s, sum(1 for w in units if not w[3]))

                def q_tile(t, par, first):
                    if not first:
                        pool.wait_ge(s_s, t - 1)
                    pool.tensor_copy(qs[:, par], qT[:, :, ds(t * P, P)]).then_inc(qs_s, 1)

                q_tile(0, 0, True)
                q_tile(1, 1, True)
                with pool.Fori(1, NT // 2) as i:
                    t = 2 * i
                    q_tile(t, 0, False)
                    q_tile(t + 1, 1, False)

            @block.vector
            def _(dve):
                def statistics(g):
                    dve.wait_ge(x_in[g], 16)
                    for t in range(4 * g, 4 * g + 4):
                        dve.bn_stats(stats[:, t, :], xres[:, t, :]).then_inc(stat_s, 1)
                    for t in range(4 * g, 4 * g + 4):
                        dve.wait_ge(stat_s, t + 1)
                        dve.bn_aggr(mv[:, t, :], stats[:, t, :]).then_inc(mv_s, 1)

                def normalize(g):
                    dve.wait_ge(rstd_s, g + 1)
                    for t in range(4 * g, 4 * g + 4):
                        dve.tensor_scalar(hA[:, t, :], xres[:, t, :], mv[:, t, 0:1], rstd[:, t:t + 1],
                                          ALU.subtract, ALU.mult).then_inc(h_s, 1)

                statistics(0)
                for g in range(NCH):
                    if g + 1 < NCH:
                        statistics(g + 1)
                    normalize(g)
                dve.wait_ge(w_in, 48)
                for u, (what, i, m, by_act) in enumerate(units):
                    if by_act:
                        continue
                    dve.wait_ge(pe_s, u + 1)
                    if what == "V":
                        bias = brow[:, R1V, :].unsqueeze(1).to_broadcast([P, 2, D])
                        dve.tensor_tensor(V1[:, 2 * i:2 * i + 2, :],
                                          PS[:, u % 8, :].rearrange("p (t d) -> p t d", t=2), bias,
                                          ALU.add).then_inc(dve_s, 1)
                    else:
                        dve.tensor_scalar(qT[:, m, i * CH:(i + 1) * CH], PS[:, u % 8, :],
                                          bcol[:, 2 * B1Q + m:2 * B1Q + m + 1], None, ALU.add).then_inc(dve_s, 1)

                S = PS[:, 0:4, :].rearrange("p a b -> p (a b)")

                def softmax_max(t, par):
                    dve.wait_ge(s_s, t + 1)
                    dve.tensor_reduce(nmax[:, par:par + 1], S, AX.X, ALU.max, negate=True).then_inc(mx_s, 1)
                    dve.wait_ge(mx_s, t + 1)
                    dve.tensor_scalar(nbias[:, par:par + 1], nmax[:, par:par + 1], D ** -0.5, None,
                                      ALU.mult).then_inc(nb_s, 1)

                def tile(t, par, last):
                    for j in (1, 3):
                        dve.wait_ge(tr_s, 4 * t + j + 1)
                        dve.tensor_copy(PT[:, par, 4 * j:4 * j + 4, :],
                                        PS[:, 4 + j % 2, :].rearrange("p (a b) -> p a b", a=4)).then_inc(ptd_s, 1)
                    if not last:
                        softmax_max(t + 1, 1 - par)
                    dve.wait_ge(exp_s, t + 1)
                    dve.reciprocal(rr[:, par:par + 1], rs[:, par:par + 1]).then_inc(rr_s, 1)
                    dve.wait_ge(rr_s, t + 1)
                    dve.wait_ge(z_s, t + 1)
                    xt_ = xres[:, ds(t, 1), :].rearrange("p a d -> p (a d)")
                    dve.scalar_tensor_tensor(xt_, PS[:, 6 + par, 0:D], rr[:, par:par + 1], xt_,
                                             ALU.mult, ALU.add).then_inc(x_s, 1)

                softmax_max(0, 0)
                tile(0, 0, False)
                tile(1, 1, False)
                with dve.Fori(1, NT // 2 - 1) as i:
                    t = 2 * i
                    tile(t, 0, False)
                    tile(t + 1, 1, False)
                tile(NT - 2, 0, False)
                tile(NT - 1, 1, True)

            @block.scalar
            def _(act):
                act.wait_ge(w_in, 48)
                for u, (what, i, m, by_act) in enumerate(units):
                    if not by_act:
                        continue
                    act.wait_ge(pe_s, u + 1)
                    if what == "T":
                        act.activation(hT[:, m, i * CH:(i + 1) * CH], PS[:, u % 8, :], ACT.Copy).then_inc(act_s, 1)
                    else:
                        to, b = (kT, B1K) if what == "K" else (qT, B1Q)
                        act.activation(to[:, m, i * CH:(i + 1) * CH], PS[:, u % 8, :], ACT.Identity,
                                       bias=bcol[:, 2 * b + m:2 * b + m + 1]).then_inc(act_s, 1)

                S = PS[:, 0:4, :].rearrange("p a b -> p (a b)")

                def exps(t, par, first):
                    act.wait_ge(nb_s, t + 1)
                    if not first:
                        act.wait_ge(tr_s, 4 * t - 4)
                        act.wait_ge(rr_s, t - 1)
                    act.activation(P1[:, par, :], S, ACT.Exp, bias=nbias[:, par:par + 1], scale=D ** -0.5,
                                   accum_out=rs[:, par:par + 1]).then_inc(exp_s, 1)

                def tile(t, par, first, last):
                    for j in (0, 2):
                        act.wait_ge(tr_s, 4 * t + j + 1)
                        act.activation(PT[:, par, 4 * j:4 * j + 4, :],
                                       PS[:, 4 + j % 2, :].rearrange("p (a b) -> p a b", a=4),
                                       ACT.Copy).then_inc(pta_s, 1)
                    if not last:
                        exps(t + 1, 1 - par, first)

                exps(0, 0, True)
                tile(0, 0, True, False)
                tile(1, 1, False, False)
                with act.Fori(1, NT // 2 - 1) as i:
                    t = 2 * i
                    tile(t, 0, False, False)
                    tile(t + 1, 1, False, False)
                tile(NT - 2, 0, False, False)
                tile(NT - 1, 1, False, True)

            @block.tensor
            def _(pe):
                pe.wait_ge(const_rdy, 5)
                pe.wait_ge(w_in, 48)
                for u, (what, i, m, _) in enumerate(units):
                    if u >= 8:
                        pe.wait_ge(*emptied(u - 8))
                    bank = PS[:, u % 8, :]
                    if what == "T":
                        pe.wait_ge(h_s, 4 * i + 4)
                        for j in range(4):
                            mm = pe.transpose(bank[:, j * P:(j + 1) * P], hA[:, 4 * i + j, m * P:(m + 1) * P],
                                              ident[:, :])
                    elif what == "V":
                        for j in range(2):
                            t = 2 * i + j
                            for c in range(DC):
                                mm = pe.matmul(bank[:, j * D:(j + 1) * D], hT[:, c, t * P:(t + 1) * P],
                                               W[:, W1V, c, :], start=(c == 0), stop=(c == DC - 1))
                    else:
                        w = W1K if what == "K" else W1Q
                        pe.wait_ge(*emptied(2 * i + 1))
                        for c in range(DC):
                            mm = pe.matmul(bank, W[:, w, c, m * P:(m + 1) * P], hT[:, c, i * CH:(i + 1) * CH],
                                           start=(c == 0), stop=(c == DC - 1))
                    mm.then_inc(pe_s, 1)
                for u in range(len(units) - 8, len(units)):
                    pe.wait_ge(*emptied(u))

                def scores(t, par, n):
                    if n == 0:
                        pe.wait_ge(qs_s, t + 1)
                    for c in range(DC):
                        mm = pe.matmul(PS[:, n, :], qs[:, par, c, :], kT[:, c, n * CH:(n + 1) * CH],
                                       start=(c == 0), stop=(c == DC - 1))
                    if n == 3:
                        mm.then_inc(s_s, 1)

                def transposes(t, par, j, first):
                    if j == 0:
                        pe.wait_ge(exp_s, t + 1)
                    if j >= 2 or not first:
                        pe.wait_ge(pta_s if j % 2 == 0 else ptd_s, 2 * t + j // 2)
                    for i in range(4):
                        k = 4 * j + i
                        mm = pe.transpose(PS[:, 4 + j % 2, i * P:(i + 1) * P], P1[:, par, k * P:(k + 1) * P],
                                          ident[:, :])
                    mm.then_inc(tr_s, 1)

                def products(t, par, j, first):
                    if j == 0 and not first:
                        pe.wait_ge(x_s, t - 1)
                    pe.wait_ge(pta_s if j % 2 == 0 else ptd_s, 2 * t + j // 2 + 1)
                    for k in range(4 * j, 4 * j + 4):
                        mm = pe.matmul(PS[:, 6 + par, 0:D], PT[:, par, k, :], V1[:, k, :],
                                       start=(k == 0), stop=(k == NT - 1))
                    if j == 3:
                        mm.then_inc(z_s, 1)

                def tile(t, par, first, second, last):
                    for j in range(4):
                        transposes(t, par, j, first)
                        if not last:
                            scores(t + 1, 1 - par, j)
                    for j in range(4):
                        products(t, par, j, first or second)

                for n in range(4):
                    scores(0, 0, n)
                tile(0, 0, True, False, False)
                tile(1, 1, False, True, False)
                with pe.Fori(1, NT // 2 - 1) as i:
                    t = 2 * i
                    tile(t, 0, False, False, False)
                    tile(t + 1, 1, False, False, False)
                tile(NT - 2, 0, False, False, False)
                tile(NT - 1, 1, False, False, True)

        KA, a = carve(0, [HG, N], BF16)
        KB, a = carve(a, [HG, N], BF16)
        Q, a = carve(a, [NCH, HG, CH], BF16)
        V, a = carve(a, [NT, D])
        VG, a = carve(a, [NT, HG, 2 * DH])
        p_at = a
        PX, a = carve(a, [2, HG, CH])
        U, a = carve(a, [CH])
        small_at = a
        mxs, a = carve(a, [2, 16, 4])
        nm, a = carve(a, [16])
        nr, a = carve(a, [16])
        mparts, a = carve(a, [8, 16], BF16)
        rc, a = carve(a, [4, HG])
        mrow, a = carve(a, [P], BF16)
        warm, a = carve(a, [2])
        F, b = carve(p_at, [2, CH])
        R, b = carve(b, [2, CH])
        PRT, b = carve(b, [4, 3, CH], BF16)
        assert b <= ARENA
        ctxT_sb, _ = carve(HG * N // 2, [2, CTX])

        def heads_layer(tag, keys, wq, wo, bq, bk, rv, ro, w_prev):
            cross = keys == CTX
            KT = -(-keys // P)
            sname = lambda n: sem(f"{tag}_{n}")
            qscr = nc.dram_tensor(f"{tag}_q_stack", [ROWS, H, N], BF16).ap()
            kscr = nc.dram_tensor(f"{tag}_k_stack", [ROWS, H, keys], BF16).ap()
            kch = [(n * CH, min(CH, keys - n * CH)) for n in range(-(-keys // CH))]

            units = []
            if w_prev is not None:
                units += [("C", n, c, "act") for n in range(NCH) for c in range(DC)]
                units += [("O", v, 0, "dve") for v in range(NT // 2)]
            kv_units = [("K", n, m, "act") for n in range(len(kch)) for m in range(DC)]
            kv_units += [("V", v, 0, "dve") for v in range(-(-KT // 2))]
            t_units = [("T", n, c, "act") for n in range(NCH) for c in range(DC)]
            q_units = [("Q", n, m, "act") for n in range(NCH) for m in range(DC)]
            units += (kv_units + t_units if cross else t_units + kv_units) + q_units
            split = [u for u in units if u[0] in "KQ"]
            pe_s, act_s, dve_s, stat_s, mv_s, var_s, rstd_s, h_s, p1_s, r1_s, p2_s, p3_s, one_s = (
                sname(n) for n in ("pe", "act", "dve", "stat", "mv", "var", "rstd", "h", "p1", "r1",
                                   "p2", "p3", "one"))
            st_s = [sname(f"st{i}") for i in range(4)]
            kin = sname("ctx") if cross else None

            def emptied(u):
                same = sum(1 for w in units[:u + 1] if w[3] == units[u][3])
                return (act_s if units[u][3] == "act" else dve_s), same

            def index(what, i, m):
                return next(n for n, w in enumerate(units) if w[:3] == (what, i, m))

            with nc.Block() as block:
                @block.sync
                def _(sp):
                    if cross:
                        sp.wait_ge(late_in, LATE)
                        sp.dma_start(ctxT_sb[:, 0, :], ctxT[0:P, :]).then_inc(kin, 16)
                        sp.dma_start(ctxT_sb[0:CW - P, 1, :], ctxT[P:CW, :]).then_inc(kin, 16)
                    for j, (what, n, m, _) in enumerate(split):
                        scr, parts = (kscr, K_PARTS) if what == "K" else (qscr, Q_PARTS)
                        at, size = kch[n] if what == "K" else (n * CH, CH)
                        sp.wait_ge(p3_s, j + 1)
                        for b, part in enumerate(parts):
                            to = scr[b * DH:(b + 1) * DH, 8 * m:8 * m + 8, at:at + size].rearrange("d h t -> h d t")
                            sp.dma_start(to, PRT[:, j % 4, part, 0:size]).then_inc(st_s[j % 4], 16)
                    for j in range(len(split) - 4, len(split)):
                        sp.wait_ge(st_s[j % 4], 96 * (j // 4 + 1))

                @block.gpsimd
                def _(pool):
                    for g in range(NCH):
                        r = slice(4 * g, 4 * g + 4)
                        pool.wait_ge(mv_s, 4 * g + 4)
                        pool.tensor_scalar(vareps[:, r], mv[:, r, 1], EPS, None, ALU.add).then_inc(var_s, 1)
                        pool.wait_ge(var_s, g + 1)
                        pool.tensor_tensor(rstd[:, r], vareps[:, r], mhalf[:, r], ALU.pow).then_inc(rstd_s, 1)
                    pool.memset(VG[:, :, :, DH:2 * DH], 1.0).then_inc(one_s, 1)
                    pool.wait_ge(one_s, 1)
                    pool.memset(KA[ROWS:ROWS + MROWS, :, :], 1.0).then_inc(one_s, 1)

                @block.vector
                def _(dve):
                    dve.wait_ge(late_in, LATE)

                    def statistics(g):
                        if w_prev is not None:
                            dve.wait_ge(dve_s, 2 * g + 2)
                        for t in range(4 * g, 4 * g + 4):
                            dve.bn_stats(stats[:, t, :], xres[:, t, :]).then_inc(stat_s, 1)
                        for t in range(4 * g, 4 * g + 4):
                            dve.wait_ge(stat_s, t + 1)
                            dve.bn_aggr(mv[:, t, :], stats[:, t, :]).then_inc(mv_s, 1)

                    def normalize(g):
                        dve.wait_ge(rstd_s, g + 1)
                        for t in range(4 * g, 4 * g + 4):
                            dve.tensor_scalar(hA[:, t, :], xres[:, t, :], mv[:, t, 0:1], rstd[:, t:t + 1],
                                              ALU.subtract, ALU.mult).then_inc(h_s, 1)

                    def layernorm():
                        statistics(0)
                        for g in range(NCH):
                            if g + 1 < NCH:
                                statistics(g + 1)
                            normalize(g)

                    def second_part(j):
                        size = kch[split[j][1]][1] if split[j][0] == "K" else CH
                        dve.wait_ge(p2_s, j + 1)
                        dve.tensor_tensor(PRT[:, j % 4, 2, 0:size], R[:, j % 2, 0:size],
                                          PRT[:, j % 4, 1, 0:size], ALU.subtract).then_inc(p3_s, 1)

                    if cross:
                        layernorm()
                    j = 0
                    for u, (what, i, m, by) in enumerate(units):
                        if not cross and what == "T" and (i, m) == (0, 0):
                            layernorm()
                        if what in "KQ":
                            size = kch[i][1] if what == "K" else CH
                            dve.wait_ge(p1_s, j + 1)
                            if j >= 2:
                                dve.wait_ge(p3_s, j - 1)
                            dve.tensor_tensor(R[:, j % 2, 0:size], F[:, j % 2, 0:size],
                                              PRT[:, j % 4, 0, 0:size], ALU.subtract).then_inc(r1_s, 1)
                            if j:
                                second_part(j - 1)
                            j += 1
                        elif what == "O":
                            dve.wait_ge(pe_s, u + 1)
                            x2 = xres[:, 2 * i:2 * i + 2, :]
                            dve.tensor_tensor(x2, PS[:, u % 8, :].rearrange("p (t d) -> p t d", t=2), x2,
                                              ALU.add).then_inc(dve_s, 1)
                        elif what == "V":
                            dve.wait_ge(pe_s, u + 1)
                            for k in range(2):
                                t = 2 * i + k
                                rows = min(P, keys - t * P)
                                if rows <= 0:
                                    continue
                                last = dve.tensor_tensor(V[0:rows, t, :], PS[0:rows, u % 8, k * D:(k + 1) * D],
                                                         brow[0:rows, rv, :], ALU.add)
                            last.then_inc(dve_s, 1)
                    second_part(len(split) - 1)

                @block.scalar
                def _(act):
                    def first_cut(j):
                        size = kch[split[j][1]][1] if split[j][0] == "K" else CH
                        act.wait_ge(r1_s, j + 1)
                        act.activation(PRT[:, j % 4, 1, 0:size], R[:, j % 2, 0:size], ACT.Copy).then_inc(p2_s, 1)

                    j = 0
                    for u, (what, i, m, by) in enumerate(units):
                        if by != "act":
                            continue
                        act.wait_ge(pe_s, u + 1)
                        if what in "TC":
                            act.activation(hT[:, m, i * CH:(i + 1) * CH], PS[:, u % 8, :], ACT.Copy).then_inc(act_s, 1)
                            continue
                        size = kch[i][1] if what == "K" else CH
                        col = 2 * (bk if what == "K" else bq) + m
                        if j >= 2:
                            act.wait_ge(r1_s, j - 1)
                        if j >= 4:
                            act.wait_ge(st_s[j % 4], 96 * (j // 4))
                        act.activation(F[:, j % 2, 0:size], PS[:, u % 8, 0:size], ACT.Identity,
                                       bias=bcol[:, col:col + 1]).then_inc(act_s, 1)
                        act.wait_ge(*emptied(u))
                        act.activation(PRT[:, j % 4, 0, 0:size], F[:, j % 2, 0:size], ACT.Copy).then_inc(p1_s, 1)
                        if j:
                            first_cut(j - 1)
                        j += 1
                    first_cut(j - 1)

                @block.tensor
                def _(pe):
                    if cross:
                        pe.wait_ge(late_in, LATE)
                        pe.wait_ge(kin, 32)
                    for u, (what, i, m, _) in enumerate(units):
                        if u >= 8:
                            pe.wait_ge(*emptied(u - 8))
                        bank = PS[:, u % 8, :]
                        if what in "TC":
                            if what == "T":
                                pe.wait_ge(h_s, 4 * i + 4)
                            source = hA if what == "T" else CTXO
                            for j in range(4):
                                mm = pe.transpose(bank[:, j * P:(j + 1) * P],
                                                  source[:, 4 * i + j, m * P:(m + 1) * P], ident[:, :])
                        elif what == "O":
                            pe.wait_ge(*emptied(index("C", i // 2, 1)))
                            for j in range(2):
                                t = 2 * i + j
                                for c in range(DC):
                                    mm = pe.matmul(bank[:, j * D:(j + 1) * D], hT[:, c, t * P:(t + 1) * P],
                                                   W[:, w_prev, c, :], start=(c == 0), stop=(c == DC - 1))
                        elif what == "V":
                            if not cross:
                                pe.wait_ge(*emptied(index("T", i // 2, 1)))
                            for j in range(2):
                                t = 2 * i + j
                                rows = min(P, keys - t * P)
                                if rows <= 0:
                                    continue
                                for c in range(DC):
                                    k = P if c == 0 or not cross else CW - P
                                    lhs = (ctxT_sb if cross else hT)[0:k, c, t * P:t * P + rows]
                                    rhs = Wkv[0:k, c, D:2 * D] if cross else W[:, W3V, c, :]
                                    mm = pe.matmul(bank[0:rows, j * D:(j + 1) * D], lhs, rhs,
                                                   start=(c == 0), stop=(c == DC - 1))
                        elif what == "K" and cross:
                            at, size = kch[i]
                            for c in range(DC):
                                k = P if c == 0 else CW - P
                                mm = pe.matmul(bank[:, 0:size], Wkv[0:k, c, m * P:(m + 1) * P],
                                               ctxT_sb[0:k, c, at:at + size], start=(c == 0), stop=(c == DC - 1))
                        else:
                            w = W3K if what == "K" else wq
                            pe.wait_ge(*emptied(index("T", i, 1)))
                            for c in range(DC):
                                mm = pe.matmul(bank, W[:, w, c, m * P:(m + 1) * P], hT[:, c, i * CH:(i + 1) * CH],
                                               start=(c == 0), stop=(c == DC - 1))
                        mm.then_inc(pe_s, 1)

            SLOTS = NCH * KT
            UNITS = 64
            AHEAD = 96
            quarter = [keys * i // 4 for i in range(5)]
            aq = [(n * 4, min(4 * n + 4, KT)) for n in range(-(-KT // 4))]

            def until(i):
                return i // KT * UNITS + (i % KT) * UNITS // KT

            s_s, exp_s, mx_s, md_s, nm_s, mp_s, mt_s, mc_s, pv_s, u_s, ut_s, un_s, rc_s, vg_s, xb_s = (
                sname(n) for n in ("s", "exp", "mx", "md", "nm", "mp", "mt", "mc", "pv", "u", "ut", "un",
                                   "rc", "vg", "xb"))
            ka_in = [sname(f"ka{i}") for i in range(len(aq))]
            kb_in = sname("kb")
            q_in = [sname(f"q{i}") for i in range(NCH)]
            mrow_in = sname("mrow")
            zero_s = sname("zero")
            def turn_slot(q):
                return next(i for i in range(SLOTS + 1) if until(i) + AHEAD >= (q + 1) * UNITS + 8) - 1

            turns = {turn_slot(q): q for q in range(1, 5)}
            OUTPUT_SLOTS = [c * KT + 2 for c in range(1, NCH)]

            with nc.Block() as block:
                @block.sync
                def _(sp):
                    def load_a(g, n):
                        lo, hi = aq[n][0] * P, min(aq[n][1] * P, keys)
                        sp.dma_start(KA[0:ROWS, :, lo:hi], kscr[:, HG * g:HG * g + HG, lo:hi]).then_inc(ka_in[n], 16)

                    def load_b(g):
                        sp.dma_start(KB[0:ROWS, :, 0:keys], kscr[:, HG * g:HG * g + HG, :]).then_inc(kb_in, 16)

                    def load_q(g, c):
                        sp.dma_start(Q[0:ROWS, c], qscr[:, HG * g:HG * g + HG, c * CH:(c + 1) * CH]).then_inc(q_in[c], 16)

                    def minus_max(n):
                        sp.wait_ge(mc_s, n + 1)
                        if n >= NCH:
                            sp.wait_ge(s_s, 2 * KT * (n - NCH + 1))
                        for r in range(MROWS):
                            sp.dma_start(Q[ROWS + r:ROWS + r + 1, n % NCH].rearrange("p h (t q) -> p (h t) q", t=4),
                                         mrow[16 * r:16 * r + 16, :]).then_inc(mrow_in, 16)

                    load_b(0)
                    load_q(0, 0)
                    for n in range(len(aq)):
                        load_a(0, n)
                    for c in range(1, NCH):
                        load_q(0, c)
                    minus_max(0)
                    for g in range(NG):
                        more = g + 1 < NG
                        minus_max(NCH * g + 1)
                        if more:
                            sp.wait_ge(mx_s, g * 256 + 2 * UNITS)
                            load_b(g + 1)
                            sp.wait_ge(s_s, 2 * KT * (NCH * g + 1))
                            load_q(g + 1, 0)
                        minus_max(NCH * g + 2)
                        if more:
                            sp.wait_ge(s_s, 2 * KT * (NCH * g + 2))
                            load_q(g + 1, 1)
                        minus_max(NCH * g + 3)
                        if more:
                            sp.wait_ge(s_s, 2 * KT * (NCH * g + 3))
                            load_q(g + 1, 2)
                            for n, (lo, hi) in enumerate(aq):
                                if n == len(aq) // 2:
                                    minus_max(NCH * g + 4)
                                sp.wait_ge(s_s, 2 * KT * (NCH * g + 3) + 2 * hi)
                                load_a(g + 1, n)
                            load_q(g + 1, 3)

                @block.gpsimd
                def _(pool):
                    base = xres if cross else hA
                    for t in range(NT):
                        pool.tensor_tensor(base[:, t, :], base[:, t, :], brow[:, ro, :], ALU.add).then_inc(xb_s, 1)

                    def v_group(g, n, first):
                        lo, hi = aq[n]
                        if not first:
                            pool.wait_ge(pv_s, KT * (NCH * g - 1) + hi)
                        whole = min(hi, keys // P)
                        last = None
                        for a_, b_, rows in ((lo, whole, P), (whole, hi, keys % P)):
                            if b_ > a_:
                                last = pool.tensor_copy(
                                    VG[0:rows, a_:b_, :, 0:DH],
                                    V[0:rows, a_:b_, ds(g * HG * DH, HG * DH)].rearrange("p t (h d) -> p t h d", h=HG))
                                last.then_inc(vg_s, 1)

                    for n in range(len(aq)):
                        v_group(0, n, True)
                    with pool.Fori(1, NG) as g:
                        for n in range(len(aq)):
                            v_group(g, n, False)

                def copies(n):
                    return sum((min(hi, keys // P) > lo) + (hi > keys // P) for lo, hi in aq[:n])

                @block.vector
                def _(dve):
                    def unit(base, n):
                        size = quarter[n % 4 + 1] - quarter[n % 4]
                        slot = n // UNITS % 2
                        dve.wait_ge(mx_s, base + n + 1)
                        dve.tensor_reduce(mxs[:, slot, n % UNITS // 4, n % 4:n % 4 + 1], PS[:, 4 + n % 2, 0:size],
                                          AX.X, ALU.max).then_inc(md_s, 1)

                    def minus(base, chunks, q):
                        n = chunks + q
                        dve.wait_ge(md_s, base + (q + 1) * UNITS)
                        dve.tensor_reduce(nm[:, :], mxs[:, q % 2], AX.X, ALU.max, negate=True).then_inc(nm_s, 1)
                        dve.wait_ge(nm_s, 4 * n + 1)
                        dve.tensor_copy(mparts[:, 0, :], nm[:, :]).then_inc(nm_s, 1)
                        dve.wait_ge(nm_s, 4 * n + 2)
                        dve.tensor_tensor(nr[:, :], nm[:, :], mparts[:, 0, :], ALU.subtract).then_inc(nm_s, 1)
                        dve.wait_ge(nm_s, 4 * n + 3)
                        dve.tensor_copy(mparts[:, 1, :], nr[:, :]).then_inc(nm_s, 1)
                        dve.wait_ge(nm_s, 4 * n + 4)
                        dve.tensor_tensor(mparts[:, 2, :], nr[:, :], mparts[:, 1, :], ALU.subtract).then_inc(mp_s, 1)

                    def divide(g, n, c):
                        t4 = PS[:, 7, :].rearrange("p (t h e) -> p t h e", t=4, h=HG)
                        dve.wait_ge(ut_s, n + 1)
                        dve.reciprocal(rc[:, :, :], t4[:, :, :, DH]).then_inc(rc_s, 1)
                        dve.wait_ge(rc_s, n + 1)
                        to = CTXO[:, 4 * c:4 * c + 4, ds(g * HG * DH, HG * DH)].rearrange("p t (h d) -> p t h d", h=HG)
                        dve.tensor_tensor(to, t4[:, :, :, 0:DH], rc[:, :, :].unsqueeze(3).to_broadcast([P, 4, HG, DH]),
                                          ALU.mult).then_inc(un_s, 1)

                    def group(g, last):
                        base, chunks = g * 256, g * NCH
                        for i in range(SLOTS):
                            for n in range(until(i) + AHEAD, until(i + 1) + AHEAD):
                                if last and n >= 256:
                                    break
                                unit(base, n)
                                if n % UNITS == UNITS - 1:
                                    minus(base, chunks, n // UNITS)
                            if i in OUTPUT_SLOTS:
                                divide(g, chunks + i // KT - 1, i // KT - 1)
                        divide(g, chunks + NCH - 1, NCH - 1)

                    dve.memset(mparts[:, :, :], 0.0).then_inc(zero_s, 1)
                    dve.wait_ge(zero_s, 1)
                    dve.memset(rc[:, :, :], 0.0).then_inc(un_s, 1)
                    for n in range(AHEAD):
                        unit(0, n)
                        if n == UNITS - 1:
                            minus(0, 0, 0)
                    with dve.Fori(0, NG - 1) as g:
                        group(g, False)
                    group(NG - 1, True)

                @block.scalar
                def _(act):
                    act.activation(warm[:, 0:1], ident[:, 0:1], ACT.Exp).then_inc(exp_s, 1)
                    act.activation(warm[:, 1:2], ident[:, 0:1], ACT.Exp).then_inc(exp_s, 1)

                    def turned(n):
                        act.wait_ge(mt_s, n + 1)
                        act.activation(mrow[0:16 * MROWS, :], PS[0:16 * MROWS, 7, 0:P // 2].bitcast(BF16),
                                       ACT.Copy).then_inc(mc_s, 1)

                    def sums(n):
                        act.wait_ge(pv_s, KT * (n + 1))
                        act.activation(U[:, :], PS[:, 6, :], ACT.Copy).then_inc(u_s, 1)

                    def group(g, last):
                        chunks = g * NCH
                        for i in range(SLOTS):
                            kt = i % KT
                            rows = min(P, keys - kt * P)
                            for pair in range(2):
                                act.wait_ge(s_s, chunks * 2 * KT + 2 * i + pair + 1)
                                act.activation(PX[0:rows, i % 2, 2 * pair:2 * pair + 2, :],
                                               PS[0:rows, 2 * pair:2 * pair + 2, :], ACT.Exp,
                                               scale=DH ** -0.5).then_inc(exp_s, 1)
                            if i in turns and not (last and turns[i] >= NCH):
                                turned(chunks + turns[i])
                            if i >= KT and kt == 0:
                                sums(chunks + i // KT - 1)
                        sums(chunks + NCH - 1)

                    turned(0)
                    with act.Fori(0, NG - 1) as g:
                        group(g, False)
                    group(NG - 1, True)

                @block.tensor
                def _(pe):
                    def unit(base, g, n, first):
                        q = n // UNITS
                        head, tile, k = n % UNITS // 16, n % 16 // 4, n % 4
                        source = KA if q in (2, 3) else KB
                        if n % UNITS == 0:
                            pe.wait_ge(q_in[q % NCH], (g + 1 + q // NCH) * 16)
                            if q % NCH == 0:
                                pe.wait_ge(kb_in, (g + 1 + q // NCH) * 16)
                            if q == 2:
                                for m in ka_in:
                                    pe.wait_ge(m, (g + 1) * 16)
                        if not first:
                            pe.wait_ge(md_s, base + n - 1)
                        lo, hi = quarter[k], quarter[k + 1]
                        pe.matmul(PS[:, 4 + n % 2, 0:hi - lo], Q[0:ROWS, q % NCH, head, tile * P:(tile + 1) * P],
                                  source[0:ROWS, head, lo:hi], start=True, stop=True).then_inc(mx_s, 1)

                    def turn(n):
                        pe.wait_ge(mp_s, n + 1)
                        pe.transpose(PS[:, 7, 0:P // 2].bitcast(BF16),
                                     mparts[:, :, :].rearrange("p a b -> p (a b)"), identb[:, :]).then_inc(mt_s, 1)

                    def scores(g, chunks, i, pair):
                        c, kt = divmod(i, KT)
                        rows = min(P, keys - kt * P)
                        if kt == 0 and pair == 0:
                            pe.wait_ge(mrow_in, 16 * MROWS * (chunks + c + 1))
                        if c == 0 and pair == 0:
                            for n, (lo, _) in enumerate(aq):
                                if kt == lo:
                                    pe.wait_ge(ka_in[n], (g + 1) * 16)
                        pe.wait_ge(exp_s, chunks * 2 * KT + 2 * i + pair + 1)
                        for h in (2 * pair, 2 * pair + 1):
                            mm = pe.matmul(PS[0:rows, h, :], KA[0:ROWS + MROWS, h, kt * P:kt * P + rows],
                                           Q[0:ROWS + MROWS, c, h, :], start=True, stop=True)
                        mm.then_inc(s_s, 1)

                    def products(g, chunks, i):
                        c, kt = divmod(i, KT)
                        rows = min(P, keys - kt * P)
                        if c == 0:
                            for n, (lo, _) in enumerate(aq):
                                if kt == lo:
                                    pe.wait_ge(vg_s, g * copies(len(aq)) + copies(n + 1))
                        if kt == 0 and c > 0:
                            pe.wait_ge(u_s, chunks + c)
                        pe.wait_ge(exp_s, chunks * 2 * KT + 2 * i + 4)
                        for h in range(HG):
                            mm = pe.matmul(PS[32 * h:32 * h + 32, 6, :], VG[0:rows, kt, h, :],
                                           PX[0:rows, i % 2, h, :], start=(kt == 0), stop=(kt == KT - 1))
                        mm.then_inc(pv_s, 1)

                    def outputs(n):
                        pe.wait_ge(u_s, n + 1)
                        pe.wait_ge(un_s, n + 1)
                        for t in range(4):
                            mm = pe.transpose(PS[:, 7, t * P:(t + 1) * P], U[:, t * P:(t + 1) * P], ident[:, :])
                        mm.then_inc(ut_s, 1)

                    def group(g, last):
                        base, chunks = g * 256, g * NCH
                        for i in range(SLOTS):
                            units = [n for n in range(until(i) + AHEAD, until(i + 1) + AHEAD)
                                     if not (last and n >= 256)]
                            half = len(units) // 2
                            scores(g, chunks, i, 0)
                            for n in units[:1]:
                                unit(base, g, n, False)
                            scores(g, chunks, i, 1)
                            for n in units[1:half]:
                                unit(base, g, n, False)
                            if i:
                                products(g, chunks, i - 1)
                            for n in units[max(half, 1):]:
                                unit(base, g, n, False)
                            if i in turns and not (last and turns[i] >= NCH):
                                pe.wait_ge(un_s, chunks + 1 + sum(1 for o in OUTPUT_SLOTS if o < i))
                                turn(chunks + turns[i])
                            if i in OUTPUT_SLOTS:
                                pe.wait_ge(mc_s, chunks + 1 + sum(1 for s in turns if s <= i))
                                outputs(chunks + i // KT - 1)
                        products(g, chunks, SLOTS - 1)
                        pe.wait_ge(mc_s, chunks + 1 + (NCH if not last else NCH - 1))
                        outputs(chunks + NCH - 1)

                    pe.wait_ge(one_s, 2)
                    for n in range(AHEAD):
                        unit(0, 0, n, n < 2)
                        if n == UNITS + 8:
                            turn(0)
                    with pe.Fori(0, NG - 1) as g:
                        group(g, False)
                    group(NG - 1, True)
            return un_s

        CTXO = sb("CTXO", [P, NT, D])
        heads_layer("c", CTX, W2Q, W2O, B2Q, B2K, R2V, R2O, None)
        heads_layer("s", N, W3Q, W3O, B3Q, B3K, R3V, RBE1, W2O)

        We, a = carve(0, [DC, NE, D])
        AO, a = carve(a, [NT, D])
        YT, a = carve(a, [DC, N])
        MO, a = carve(a, [NT, D])
        wT, a = carve(a, [NCH, CH])
        small = {}
        for name in ("lg", "sh", "ex", "pr", "q1", "o1", "p2", "q2", "o2", "wt", "oo"):
            small[name], a = carve(a, [NT, NE])
        for name in ("mx", "sm", "rc", "m1", "a1", "m2", "a2"):
            small[name], a = carve(a, [NT])
        rev, a = carve(a, [NE])
        stats2, a = carve(a, [NT, 6])
        mv2, a = carve(a, [NT, 2])
        rstd2, a = carve(a, [NT])
        units = [("C", n, c, "act") for n in range(NCH) for c in range(DC)]
        units += [("O", v, 0, "dve") for v in range(NT // 2)]
        for n in range(NCH):
            units += [("T", n, c, "act") for c in range(DC)] + [("G", n, 0, "dve")]
        for n in range(NCH):
            units += [("R", n, 0, "act")] + [("B", v, 0, "act") for v in (2 * n, 2 * n + 1)]
            units += [("M", t, e, "dve") for t in range(4 * n, 4 * n + 4) for e in range(NE // 2)]
        fsem = {n: sem("f_" + n) for n in (
            "we", "pe", "act", "dve", "stat", "mv", "var", "rstd", "n", "ng", "y", "g", "ex", "w", "mo", "stat2",
            "mv2", "rstd2", "n2", "ng2", "res", "o", "out", "rev")}
        pe_s, act_s, dve_s = fsem["pe"], fsem["act"], fsem["dve"]

        def emptied(u):
            same = sum(1 for w in units[:u + 1] if w[3] == units[u][3])
            return (act_s if units[u][3] == "act" else dve_s), same

        def index(what, i, m=0):
            return next(n for n, w in enumerate(units) if w[:3] == (what, i, m))

        def brows4(r):
            return brow[:, r, :].unsqueeze(1).to_broadcast([P, 4, D])

        with nc.Block() as block:
            @block.sync
            def _(sp):
                sp.dma_start(We[:, 0, :, :], we[:, 0:P, :].rearrange("e p f -> p e f")).then_inc(fsem["we"], 16)
                sp.dma_start(We[:, 1, :, :], we[:, P:D, :].rearrange("e p f -> p e f")).then_inc(fsem["we"], 16)
                o = out.rearrange("(t p) d -> p t d", p=P)
                for g in range(NCH):
                    sp.wait_ge(fsem["o"], g + 1)
                    sp.dma_start(o[:, 4 * g:4 * g + 4, :], MO[:, 4 * g:4 * g + 4, :]).then_inc(fsem["out"], 16)
                sp.wait_ge(fsem["out"], 16 * NCH)

            @block.gpsimd
            def _(pool):
                for e in range(NE):
                    pool.memset(rev[:, e:e + 1], float(NE - e)).then_inc(fsem["rev"], 1)
                def reciprocal_std(n, g, mvs, src, to):
                    r = slice(4 * g, 4 * g + 4)
                    pool.wait_ge(mvs, 4 * g + 4)
                    pool.tensor_scalar(vareps[:, r], src[:, r, 1], EPS, None, ALU.add).then_inc(fsem["var"], 1)
                    pool.wait_ge(fsem["var"], n + 1)
                    pool.tensor_tensor(to[:, r], vareps[:, r], mhalf[:, r], ALU.pow).then_inc(fsem["rstd"], 1)

                def gain(g, to, row, normalized, done):
                    r = slice(4 * g, 4 * g + 4)
                    pool.wait_ge(normalized, 4 * g + 4)
                    pool.tensor_tensor(to[:, r, :], to[:, r, :], brows4(row), ALU.mult).then_inc(done, 1)

                for g in range(NCH):
                    reciprocal_std(g, g, fsem["mv"], mv, rstd)
                    if g:
                        gain(g - 1, AO, RG1, fsem["n"], fsem["ng"])
                gain(NCH - 1, AO, RG1, fsem["n"], fsem["ng"])
                for g in range(NCH):
                    r = slice(4 * g, 4 * g + 4)
                    pool.wait_ge(fsem["y"], g + 1)
                    pool.tensor_tensor(xres[:, r, :], xres[:, r, :], hA[:, r, :], ALU.add).then_inc(fsem["res"], 1)
                    pool.wait_ge(fsem["res"], 2 * g + 1)
                    pool.tensor_tensor(xres[:, r, :], xres[:, r, :], brows4(RBE2), ALU.add).then_inc(fsem["res"], 1)
                for g in range(NCH):
                    pool.wait_ge(fsem["rstd"], NCH + g)
                    reciprocal_std(NCH + g, g, fsem["mv2"], mv2, rstd2)
                    gain(g, MO, RG2, fsem["n2"], fsem["ng2"])

            @block.vector
            def _(dve):
                def attention_output(g):
                    for v in (2 * g, 2 * g + 1):
                        u = index("O", v)
                        dve.wait_ge(pe_s, u + 1)
                        bias = brow[:, R3O, :].unsqueeze(1).to_broadcast([P, 2, D])
                        dve.tensor_tensor(AO[:, 2 * v:2 * v + 2, :], PS[:, u % 8, :].rearrange("p (t d) -> p t d", t=2),
                                          bias, ALU.add).then_inc(dve_s, 1)
                    dve.wait_ge(dve_s, 2 * g + 2)
                    for t in range(4 * g, 4 * g + 4):
                        dve.bn_stats(stats[:, t, :], AO[:, t, :]).then_inc(fsem["stat"], 1)
                    for t in range(4 * g, 4 * g + 4):
                        dve.wait_ge(fsem["stat"], t + 1)
                        dve.bn_aggr(mv[:, t, :], stats[:, t, :]).then_inc(fsem["mv"], 1)

                def normalize(g, to, m, r, rdy, s):
                    dve.wait_ge(fsem["rstd"], rdy)
                    for t in range(4 * g, 4 * g + 4):
                        dve.tensor_scalar(to[:, t, :], to[:, t, :], m[:, t, 0:1], r[:, t:t + 1],
                                          ALU.subtract, ALU.mult).then_inc(s, 1)

                def experts_input(g):
                    r = slice(4 * g, 4 * g + 4)
                    dve.wait_ge(fsem["ng"], g + 1)
                    dve.tensor_tensor(hA[:, r, :], hA[:, r, :], AO[:, r, :], ALU.add).then_inc(fsem["y"], 1)

                def gate(g):
                    r = slice(4 * g, 4 * g + 4)
                    u = index("G", g)
                    n = [16 * g]
                    gs = fsem["g"]

                    def chain(ins):
                        ins.then_inc(gs, 1)
                        n[0] += 1
                        dve.wait_ge(gs, n[0])

                    def b(name):
                        return small[name][:, r].unsqueeze(2).to_broadcast([P, 4, NE])

                    s = {k: v[:, r] for k, v in small.items()}
                    revb = rev[:, :].unsqueeze(1).to_broadcast([P, 4, NE])
                    dve.wait_ge(pe_s, u + 1)
                    dve.tensor_tensor(s["lg"], PS[:, u % 8, 0:4 * NE].rearrange("p (t e) -> p t e", t=4),
                                      bgrow[:, :].unsqueeze(1).to_broadcast([P, 4, NE]), ALU.add).then_inc(dve_s, 1)
                    dve.wait_ge(*emptied(u))
                    chain(dve.tensor_reduce(s["mx"], s["lg"], AX.X, ALU.max))
                    chain(dve.tensor_tensor(s["sh"], s["lg"], b("mx"), ALU.subtract))
                    dve.wait_ge(fsem["ex"], g + 1)
                    chain(dve.tensor_reduce(s["sm"], s["ex"], AX.X, ALU.add))
                    chain(dve.reciprocal(s["rc"], s["sm"]))
                    chain(dve.tensor_tensor(s["pr"], s["ex"], b("rc"), ALU.mult))
                    chain(dve.tensor_reduce(s["m1"], s["pr"], AX.X, ALU.max))
                    chain(dve.tensor_tensor(s["q1"], s["pr"], b("m1"), ALU.is_equal))
                    chain(dve.tensor_tensor(s["o2"], s["q1"], revb, ALU.mult))
                    chain(dve.tensor_reduce(s["a1"], s["o2"], AX.X, ALU.max))
                    chain(dve.tensor_tensor(s["o1"], s["o2"], b("a1"), ALU.is_equal))
                    chain(dve.scalar_tensor_tensor(s["p2"], s["o1"], -2.0, s["pr"], ALU.mult, ALU.add))
                    chain(dve.tensor_reduce(s["m2"], s["p2"], AX.X, ALU.max))
                    chain(dve.tensor_tensor(s["q2"], s["p2"], b("m2"), ALU.is_equal))
                    chain(dve.tensor_tensor(s["oo"], s["q2"], revb, ALU.mult))
                    chain(dve.tensor_reduce(s["a2"], s["oo"], AX.X, ALU.max))
                    chain(dve.tensor_tensor(s["q1"], s["oo"], b("a2"), ALU.is_equal))
                    assert n[0] == 16 * g + 16
                    dve.tensor_tensor(s["q2"], s["q1"], s["o1"], ALU.add).then_inc(fsem["w"], 1)
                    dve.wait_ge(fsem["w"], 2 * g + 1)
                    dve.tensor_tensor(s["wt"], s["q2"], s["pr"], ALU.mult).then_inc(fsem["w"], 1)

                mo = [0]

                def experts(t):
                    for e in range(NE // 2):
                        u = index("M", t, e)
                        dve.wait_ge(pe_s, u + 1)
                        if e == 0:
                            dve.wait_ge(*emptied(index("B", t // 2)))
                        for k in range(2):
                            if e or k:
                                dve.wait_ge(fsem["mo"], mo[0])
                            ins = dve.scalar_tensor_tensor(MO[:, t, :], PS[:, u % 8, k * D:(k + 1) * D],
                                                           small["wt"][:, t, 2 * e + k:2 * e + k + 1], MO[:, t, :],
                                                           ALU.mult, ALU.add)
                            if k == 0:
                                ins.then_inc(fsem["mo"], 1)
                                mo[0] += 1
                            else:
                                ins.then_inc(dve_s, 1)
                                dve.wait_ge(*emptied(u))

                def experts_stats(g):
                    for t in range(4 * g, 4 * g + 4):
                        dve.bn_stats(stats2[:, t, :], MO[:, t, :]).then_inc(fsem["stat2"], 1)
                    for t in range(4 * g, 4 * g + 4):
                        dve.wait_ge(fsem["stat2"], t + 1)
                        dve.bn_aggr(mv2[:, t, :], stats2[:, t, :]).then_inc(fsem["mv2"], 1)

                def finish(g):
                    r = slice(4 * g, 4 * g + 4)
                    dve.wait_ge(fsem["ng2"], g + 1)
                    dve.wait_ge(fsem["res"], 2 * g + 2)
                    dve.tensor_tensor(MO[:, r, :], MO[:, r, :], xres[:, r, :], ALU.add).then_inc(fsem["o"], 1)

                for g in range(NCH):
                    attention_output(g)
                    if g:
                        normalize(g - 1, AO, mv, rstd, g, fsem["n"])
                    if g > 1:
                        experts_input(g - 2)
                normalize(NCH - 1, AO, mv, rstd, NCH, fsem["n"])
                experts_input(NCH - 2)
                experts_input(NCH - 1)
                dve.wait_ge(fsem["rev"], NE)
                for g in range(NCH):
                    gate(g)
                for g in range(NCH):
                    dve.wait_ge(fsem["w"], 2 * g + 2)
                    for t in range(4 * g, 4 * g + 4):
                        experts(t)
                    experts_stats(g)
                    if g:
                        finish(g - 1)
                    normalize(g, MO, mv2, rstd2, NCH + g + 1, fsem["n2"])
                finish(NCH - 1)

            @block.scalar
            def _(act):
                for u, (what, i, m, by) in enumerate(units):
                    if what == "G":
                        act.wait_ge(fsem["g"], 16 * i + 2)
                        act.activation(small["ex"][:, 4 * i:4 * i + 4], small["sh"][:, 4 * i:4 * i + 4],
                                       ACT.Exp).then_inc(fsem["ex"], 1)
                    if by != "act":
                        continue
                    act.wait_ge(pe_s, u + 1)
                    if what == "C":
                        act.activation(hT[:, m, i * CH:(i + 1) * CH], PS[:, u % 8, :], ACT.Copy).then_inc(act_s, 1)
                    elif what == "T":
                        act.activation(YT[:, m, i * CH:(i + 1) * CH], PS[:, u % 8, :], ACT.Copy).then_inc(act_s, 1)
                    elif what == "R":
                        act.activation(wT[0:NE, i, :], PS[0:NE, u % 8, :], ACT.Copy).then_inc(act_s, 1)
                    else:
                        act.activation(MO[:, 2 * i:2 * i + 2, :], PS[:, u % 8, :].rearrange("p (t d) -> p t d", t=2),
                                       ACT.Copy).then_inc(act_s, 1)

            @block.tensor
            def _(pe):
                for u, (what, i, m, _) in enumerate(units):
                    if u >= 8:
                        pe.wait_ge(*emptied(u - 8))
                    bank = PS[:, u % 8, :]
                    if what in "CT":
                        if what == "T":
                            pe.wait_ge(fsem["y"], i + 1)
                        source = hA if what == "T" else CTXO
                        for j in range(4):
                            mm = pe.transpose(bank[:, j * P:(j + 1) * P], source[:, 4 * i + j, m * P:(m + 1) * P],
                                              ident[:, :])
                    elif what == "O":
                        pe.wait_ge(*emptied(index("C", i // 2, 1)))
                        for j in range(2):
                            t = 2 * i + j
                            for c in range(DC):
                                mm = pe.matmul(bank[:, j * D:(j + 1) * D], hT[:, c, t * P:(t + 1) * P],
                                               W[:, W3O, c, :], start=(c == 0), stop=(c == DC - 1))
                    elif what == "G":
                        pe.wait_ge(*emptied(index("T", i, 1)))
                        for j in range(4):
                            t = 4 * i + j
                            for c in range(DC):
                                mm = pe.matmul(bank[:, j * NE:(j + 1) * NE], YT[:, c, t * P:(t + 1) * P],
                                               Wg[:, c, :], start=(c == 0), stop=(c == DC - 1))
                    elif what == "R":
                        pe.wait_ge(fsem["w"], 2 * i + 2)
                        for j in range(4):
                            mm = pe.transpose(bank[0:NE, j * P:(j + 1) * P], small["wt"][:, 4 * i + j, :], ident[:, :])
                    elif what == "B":
                        pe.wait_ge(*emptied(index("R", i // 2)))
                        for j in range(2):
                            t = 2 * i + j
                            mm = pe.matmul(bank[:, j * D:(j + 1) * D], wT[0:NE, t // 4, t % 4 * P:(t % 4 + 1) * P],
                                           bexp_sb[:, :], start=True, stop=True)
                    else:
                        if (i, m) == (0, 0):
                            pe.wait_ge(fsem["we"], 32)
                        for c in range(DC):
                            mm = pe.matmul(bank, YT[:, c, i * P:(i + 1) * P],
                                           We[:, c, 2 * m:2 * m + 2, :].rearrange("p e f -> p (e f)"),
                                           start=(c == 0), stop=(c == DC - 1))
                    mm.then_inc(pe_s, 1)


def kernel(**inputs):
    import numpy as np
    import concourse.bacc as bacc
    from concourse.bass_utils import run_bass_kernel_spmd

    i = {k: np.asarray(v) for k, v in inputs.items()}
    t = np.ascontiguousarray
    kv = i["L0_xattn_Wkv"].reshape(H, 2, DH, CW)
    bkv = i["L0_xattn_bkv"].reshape(H, 2, DH)
    columns = [i["L0_attn_bq"], i["L0_attn_bk"], i["L0_xattn_bq"], bkv[:, 0].reshape(D), i["L0_ffn_bq"],
               i["L0_ffn_bk"]]
    arrays = {
        "x": t(i["x"][0]),
        "ctxT": t(i["ctx_768"][0].T),
        "wpack": t(np.stack([i["L0_attn_Wq"].T, i["L0_attn_Wk"].T, i["L0_attn_Wv"].T, i["L0_xattn_Wq"].T,
                             i["L0_xattn_Wo"].T, i["L0_ffn_Wq"], i["L0_ffn_Wk"], i["L0_ffn_Wv"],
                             i["L0_ffn_Wo"]])),
        "wkv": t(np.concatenate([kv[:, 0].reshape(D, CW).T, kv[:, 1].reshape(D, CW).T], 1)),
        "we": t(i["L0_ffn_We"]),
        "wg": t(i["L0_ffn_Wg"]),
        "bcols": t(np.stack([b.reshape(DC, P)[c] for b in columns for c in range(DC)], 1)),
        "brows": t(np.stack([i["L0_attn_bv"], bkv[:, 1].reshape(D), i["L0_xattn_bo"], i["L0_ffn_bv"],
                             i["L0_ffn_bo"], i["L0_ffn_g1"], i["L0_ffn_be1"], i["L0_ffn_g2"],
                             i["L0_ffn_be2"]])),
        "bg": t(i["L0_ffn_bg"]),
        "bexp": t(i["L0_ffn_bexp"]),
    }
    nc = bacc.Bacc("TRN2", target_bir_lowering=False, num_devices=1)
    args = [nc.dram_tensor(n, a.shape, mybir.dt.from_np(a.dtype), kind="ExternalInput").ap()
            for n, a in arrays.items()]
    out = nc.dram_tensor("out", (N, D), F32, kind="ExternalOutput").ap()
    build(nc, *args, out)
    r = run_bass_kernel_spmd(nc, [arrays], core_ids=[0])
    return r.results[0]["out"].reshape(1, N, D)
```

```python
from contextlib import ExitStack

import concourse.bass as bass
from concourse import mybir

F32 = mybir.dt.float32
BF16 = mybir.dt.bfloat16
ALU = mybir.AluOpType
ACT = mybir.ActivationFunctionType
AX = mybir.AxisListType
ds = bass.ds

P = 128
D = 256
DC = D // P
N = 2048
NT = N // P
CH = 512
NCH = N // CH
H = 16
DH = D // H
HG = 4
NG = H // HG
CTX = 1601
CW = 192
NE = 8
EPS = 1e-5
BANK = 512
ROWS = 6 * DH
MROWS = 3
Q_PARTS = (0, 0, 0, 1, 1, 2)
K_PARTS = (0, 1, 2, 0, 1, 0)
W1Q, W1K, W1V, W2Q, W2O, W3Q, W3K, W3V, W3O = range(9)
B1Q, B1K, B2Q, B2K, B3Q, B3K = range(6)
R1V, R2V, R2O, R3V, R3O, RG1, RBE1, RG2, RBE2 = range(9)


def build(nc, x, ctxT, wpack, wkv, we, wg, bcols, brows, bg, bexp, out):
    with ExitStack() as ctx:
        def sb(name, shape, dt=F32):
            return ctx.enter_context(nc.sbuf_tensor(name, shape, dt))

        def sem(name):
            return ctx.enter_context(nc.semaphore(name))

        PS = ctx.enter_context(nc.psum_tensor("PS", [P, 8, BANK], F32))
        xres = sb("xres", [P, NT, D])
        hA = sb("hA", [P, NT, D])
        hT = sb("hT", [P, DC, N])
        W = sb("W", [P, 9, DC, D])
        Wkv = sb("Wkv", [P, 2, 2 * D])
        Wg = sb("Wg", [P, DC, NE])
        bcol = sb("bcol", [P, 12])
        brow = sb("brow", [P, 9, D])
        bgrow = sb("bgrow", [P, NE])
        bexp_sb = sb("bexp_sb", [NE, D])
        ident = sb("ident", [P, P])
        identb = sb("identb", [P, P], BF16)
        stats = sb("stats", [P, NT, 6])
        mv = sb("mv", [P, NT, 2])
        vareps = sb("vareps", [P, NT])
        mhalf = sb("mhalf", [P, NT])
        rstd = sb("rstd", [P, NT])
        ones = sb("ones", [P, NT])
        ARENA = 26500
        arena = sb("arena", [P, ARENA])

        def carve(at, shape, dt=F32):
            n = 1
            for d in shape:
                n *= d
            words = n * (2 if dt == BF16 else 4) // 4
            assert at + words <= ARENA, (at, words)
            v = arena[:, at:at + words]
            if dt == BF16:
                v = v.bitcast(BF16)
            names = "abcd"[:len(shape)]
            if len(shape) > 1:
                v = v.rearrange(f"p ({' '.join(names)}) -> p {' '.join(names)}",
                                **dict(zip(names[1:], shape[1:])))
            return v, at + words

        x_in = [sem(f"x_in{g}") for g in range(NCH)]
        w_in = sem("w_in")
        ctx_in = sem("ctx_in")
        late_in = sem("late_in")
        const_rdy = sem("const_rdy")

        xt = x.rearrange("(t p) d -> p t d", p=P)

        qT, a = carve(0, [DC, N])
        kT, a = carve(a, [DC, N])
        V1, a = carve(a, [NT, D])
        qs, a = carve(a, [2, DC, P])
        P1, a = carve(a, [2, N])
        PT, a = carve(a, [2, NT, P])
        rs = sb("rs", [P, 2])
        nmax = sb("nmax", [P, 2])
        nbias = sb("nbias", [P, 2])
        rr = sb("rr", [P, 2])

        sems = {n: sem("a_" + n) for n in (
            "stat", "mv", "var", "rstd", "h", "pe", "act", "dve", "qs", "s", "mx", "nb", "exp", "tr", "pta",
            "ptd", "z", "rr", "x")}
        var_s = sems["var"]
        stat_s, mv_s, rstd_s, h_s, pe_s, act_s, dve_s = (sems[n] for n in (
            "stat", "mv", "rstd", "h", "pe", "act", "dve"))
        qs_s, s_s, mx_s, nb_s, exp_s, tr_s, pta_s, ptd_s, z_s, rr_s, x_s = (sems[n] for n in (
            "qs", "s", "mx", "nb", "exp", "tr", "pta", "ptd", "z", "rr", "x"))

        units = [("T", n, c, True) for n in range(NCH) for c in range(DC)]
        units += [("K", n, m, True) for n in range(NCH) for m in range(DC)]
        units += [("V", v, 0, False) for v in range(NT // 2)]
        units += [("Q", n, m, m == 0) for n in range(NCH) for m in range(DC)]

        def emptied(u):
            same = sum(1 for w in units[:u + 1] if w[3] == units[u][3])
            return (act_s if units[u][3] else dve_s), same

        LATE = 16 * 11
        with nc.Block() as block:
            @block.sync
            def _(sp):
                for g in range(NCH):
                    sp.dma_start(xres[:, 4 * g:4 * g + 4, :], xt[:, 4 * g:4 * g + 4, :]).then_inc(x_in[g], 16)
                    if g == 0:
                        sp.dma_start(W[:, 0:3], wpack[0:3].rearrange("w (c p) d -> p w c d", p=P)).then_inc(w_in, 16)
                        sp.dma_start(bcol[:, :], bcols).then_inc(w_in, 16)
                        sp.dma_start(brow[:, :, :], brows.partition_broadcast(P)).then_inc(w_in, 16)
                for w in range(3, 9):
                    sp.dma_start(W[:, w], wpack[w].rearrange("(c p) d -> p c d", p=P)).then_inc(late_in, 16)
                sp.dma_start(Wkv[:, 0, :], wkv[0:P, :]).then_inc(late_in, 16)
                sp.dma_start(Wkv[0:CW - P, 1, :], wkv[P:CW, :]).then_inc(late_in, 16)
                sp.dma_start(Wg[:, :, :], wg.rearrange("(c p) e -> p c e", p=P)).then_inc(late_in, 16)
                sp.dma_start(bgrow[:, :], bg.partition_broadcast(P)).then_inc(late_in, 16)
                sp.dma_start(bexp_sb[:, :], bexp).then_inc(late_in, 16)

            @block.gpsimd
            def _(pool):
                pool.memset(ident[:, :], 0.0).then_inc(const_rdy, 1)
                pool.memset(identb[:, :], 0.0).then_inc(const_rdy, 1)
                pool.memset(mhalf[:, :], -0.5).then_inc(const_rdy, 1)
                pool.memset(ones[:, :], 1.0).then_inc(const_rdy, 1)
                pool.wait_ge(const_rdy, 4)
                for m in (ident, identb):
                    pool.affine_select(out=m[:, :], in_=m[:, :], compare_op=ALU.not_equal, fill=1.0,
                                       base=0, pattern=[[-1, P]], channel_multiplier=1).then_inc(const_rdy, 1)
                for g in range(NCH):
                    r = slice(4 * g, 4 * g + 4)
                    pool.wait_ge(mv_s, 4 * g + 4)
                    pool.tensor_scalar(vareps[:, r], mv[:, r, 1], EPS, None, ALU.add).then_inc(var_s, 1)
                    pool.wait_ge(var_s, g + 1)
                    pool.tensor_tensor(rstd[:, r], vareps[:, r], mhalf[:, r], ALU.pow).then_inc(rstd_s, 1)
                pool.wait_ge(act_s, sum(1 for w in units if w[3]))
                pool.wait_ge(dve_s, sum(1 for w in units if not w[3]))

                def q_tile(t, par, first):
                    if not first:
                        pool.wait_ge(s_s, t - 1)
                    pool.tensor_copy(qs[:, par], qT[:, :, ds(t * P, P)]).then_inc(qs_s, 1)

                q_tile(0, 0, True)
                q_tile(1, 1, True)
                with pool.Fori(1, NT // 2) as i:
                    t = 2 * i
                    q_tile(t, 0, False)
                    q_tile(t + 1, 1, False)

            @block.vector
            def _(dve):
                def statistics(g):
                    dve.wait_ge(x_in[g], 16)
                    for t in range(4 * g, 4 * g + 4):
                        dve.bn_stats(stats[:, t, :], xres[:, t, :]).then_inc(stat_s, 1)
                    for t in range(4 * g, 4 * g + 4):
                        dve.wait_ge(stat_s, t + 1)
                        dve.bn_aggr(mv[:, t, :], stats[:, t, :]).then_inc(mv_s, 1)

                def normalize(g):
                    dve.wait_ge(rstd_s, g + 1)
                    for t in range(4 * g, 4 * g + 4):
                        dve.tensor_scalar(hA[:, t, :], xres[:, t, :], mv[:, t, 0:1], rstd[:, t:t + 1],
                                          ALU.subtract, ALU.mult).then_inc(h_s, 1)

                statistics(0)
                for g in range(NCH):
                    if g + 1 < NCH:
                        statistics(g + 1)
                    normalize(g)
                dve.wait_ge(w_in, 48)
                for u, (what, i, m, by_act) in enumerate(units):
                    if by_act:
                        continue
                    dve.wait_ge(pe_s, u + 1)
                    if what == "V":
                        bias = brow[:, R1V, :].unsqueeze(1).to_broadcast([P, 2, D])
                        dve.tensor_tensor(V1[:, 2 * i:2 * i + 2, :],
                                          PS[:, u % 8, :].rearrange("p (t d) -> p t d", t=2), bias,
                                          ALU.add).then_inc(dve_s, 1)
                    else:
                        dve.tensor_scalar(qT[:, m, i * CH:(i + 1) * CH], PS[:, u % 8, :],
                                          bcol[:, 2 * B1Q + m:2 * B1Q + m + 1], None, ALU.add).then_inc(dve_s, 1)

                S = PS[:, 0:4, :].rearrange("p a b -> p (a b)")

                def softmax_max(t, par):
                    dve.wait_ge(s_s, t + 1)
                    dve.tensor_reduce(nmax[:, par:par + 1], S, AX.X, ALU.max, negate=True).then_inc(mx_s, 1)
                    dve.wait_ge(mx_s, t + 1)
                    dve.tensor_scalar(nbias[:, par:par + 1], nmax[:, par:par + 1], D ** -0.5, None,
                                      ALU.mult).then_inc(nb_s, 1)

                def tile(t, par, last):
                    for j in (1, 3):
                        dve.wait_ge(tr_s, 4 * t + j + 1)
                        dve.tensor_copy(PT[:, par, 4 * j:4 * j + 4, :],
                                        PS[:, 4 + j % 2, :].rearrange("p (a b) -> p a b", a=4)).then_inc(ptd_s, 1)
                    if not last:
                        softmax_max(t + 1, 1 - par)
                    dve.wait_ge(exp_s, t + 1)
                    dve.reciprocal(rr[:, par:par + 1], rs[:, par:par + 1]).then_inc(rr_s, 1)
                    dve.wait_ge(rr_s, t + 1)
                    dve.wait_ge(z_s, t + 1)
                    xt_ = xres[:, ds(t, 1), :].rearrange("p a d -> p (a d)")
                    dve.scalar_tensor_tensor(xt_, PS[:, 6 + par, 0:D], rr[:, par:par + 1], xt_,
                                             ALU.mult, ALU.add).then_inc(x_s, 1)

                softmax_max(0, 0)
                tile(0, 0, False)
                tile(1, 1, False)
                with dve.Fori(1, NT // 2 - 1) as i:
                    t = 2 * i
                    tile(t, 0, False)
                    tile(t + 1, 1, False)
                tile(NT - 2, 0, False)
                tile(NT - 1, 1, True)

            @block.scalar
            def _(act):
                act.wait_ge(w_in, 48)
                for u, (what, i, m, by_act) in enumerate(units):
                    if not by_act:
                        continue
                    act.wait_ge(pe_s, u + 1)
                    if what == "T":
                        act.activation(hT[:, m, i * CH:(i + 1) * CH], PS[:, u % 8, :], ACT.Copy).then_inc(act_s, 1)
                    else:
                        to, b = (kT, B1K) if what == "K" else (qT, B1Q)
                        act.activation(to[:, m, i * CH:(i + 1) * CH], PS[:, u % 8, :], ACT.Identity,
                                       bias=bcol[:, 2 * b + m:2 * b + m + 1]).then_inc(act_s, 1)

                S = PS[:, 0:4, :].rearrange("p a b -> p (a b)")

                def exps(t, par, first):
                    act.wait_ge(nb_s, t + 1)
                    if not first:
                        act.wait_ge(tr_s, 4 * t - 4)
                        act.wait_ge(rr_s, t - 1)
                    act.activation(P1[:, par, :], S, ACT.Exp, bias=nbias[:, par:par + 1], scale=D ** -0.5,
                                   accum_out=rs[:, par:par + 1]).then_inc(exp_s, 1)

                def tile(t, par, first, last):
                    for j in (0, 2):
                        act.wait_ge(tr_s, 4 * t + j + 1)
                        act.activation(PT[:, par, 4 * j:4 * j + 4, :],
                                       PS[:, 4 + j % 2, :].rearrange("p (a b) -> p a b", a=4),
                                       ACT.Copy).then_inc(pta_s, 1)
                    if not last:
                        exps(t + 1, 1 - par, first)

                exps(0, 0, True)
                tile(0, 0, True, False)
                tile(1, 1, False, False)
                with act.Fori(1, NT // 2 - 1) as i:
                    t = 2 * i
                    tile(t, 0, False, False)
                    tile(t + 1, 1, False, False)
                tile(NT - 2, 0, False, False)
                tile(NT - 1, 1, False, True)

            @block.tensor
            def _(pe):
                pe.wait_ge(const_rdy, 6)
                pe.wait_ge(w_in, 48)
                for u, (what, i, m, _) in enumerate(units):
                    if u >= 8:
                        pe.wait_ge(*emptied(u - 8))
                    bank = PS[:, u % 8, :]
                    if what == "T":
                        pe.wait_ge(h_s, 4 * i + 4)
                        for j in range(4):
                            mm = pe.transpose(bank[:, j * P:(j + 1) * P], hA[:, 4 * i + j, m * P:(m + 1) * P],
                                              ident[:, :])
                    elif what == "V":
                        for j in range(2):
                            t = 2 * i + j
                            for c in range(DC):
                                mm = pe.matmul(bank[:, j * D:(j + 1) * D], hT[:, c, t * P:(t + 1) * P],
                                               W[:, W1V, c, :], start=(c == 0), stop=(c == DC - 1))
                    else:
                        w = W1K if what == "K" else W1Q
                        pe.wait_ge(*emptied(2 * i + 1))
                        for c in range(DC):
                            mm = pe.matmul(bank, W[:, w, c, m * P:(m + 1) * P], hT[:, c, i * CH:(i + 1) * CH],
                                           start=(c == 0), stop=(c == DC - 1))
                    mm.then_inc(pe_s, 1)
                for u in range(len(units) - 8, len(units)):
                    pe.wait_ge(*emptied(u))

                def scores(t, par, n):
                    if n == 0:
                        pe.wait_ge(qs_s, t + 1)
                    for c in range(DC):
                        mm = pe.matmul(PS[:, n, :], qs[:, par, c, :], kT[:, c, n * CH:(n + 1) * CH],
                                       start=(c == 0), stop=(c == DC - 1))
                    if n == 3:
                        mm.then_inc(s_s, 1)

                def transposes(t, par, j, first):
                    if j == 0:
                        pe.wait_ge(exp_s, t + 1)
                    if j >= 2 or not first:
                        pe.wait_ge(pta_s if j % 2 == 0 else ptd_s, 2 * t + j // 2)
                    for i in range(4):
                        k = 4 * j + i
                        mm = pe.transpose(PS[:, 4 + j % 2, i * P:(i + 1) * P], P1[:, par, k * P:(k + 1) * P],
                                          ident[:, :])
                    mm.then_inc(tr_s, 1)

                def products(t, par, j, first):
                    if j == 0 and not first:
                        pe.wait_ge(x_s, t - 1)
                    pe.wait_ge(pta_s if j % 2 == 0 else ptd_s, 2 * t + j // 2 + 1)
                    for k in range(4 * j, 4 * j + 4):
                        mm = pe.matmul(PS[:, 6 + par, 0:D], PT[:, par, k, :], V1[:, k, :],
                                       start=(k == 0), stop=(k == NT - 1))
                    if j == 3:
                        mm.then_inc(z_s, 1)

                def tile(t, par, first, second, last):
                    for j in range(4):
                        transposes(t, par, j, first)
                        if not last:
                            scores(t + 1, 1 - par, j)
                    for j in range(4):
                        products(t, par, j, first or second)

                for n in range(4):
                    scores(0, 0, n)
                tile(0, 0, True, False, False)
                tile(1, 1, False, True, False)
                with pe.Fori(1, NT // 2 - 1) as i:
                    t = 2 * i
                    tile(t, 0, False, False, False)
                    tile(t + 1, 1, False, False, False)
                tile(NT - 2, 0, False, False, False)
                tile(NT - 1, 1, False, False, True)

        KA, a = carve(0, [HG, N], BF16)
        KB, a = carve(a, [HG, N], BF16)
        Q, a = carve(a, [NCH, HG, CH], BF16)
        V, a = carve(a, [NT, D])
        VG, a = carve(a, [NT, HG, 2 * DH])
        p_at = a
        PX, a = carve(a, [2, HG, CH])
        U, a = carve(a, [CH])
        small_at = a
        mxs, a = carve(a, [2, 16, 4])
        nm, a = carve(a, [16])
        nr, a = carve(a, [16])
        mparts, a = carve(a, [8, 16], BF16)
        rc, a = carve(a, [4, HG])
        mrow, a = carve(a, [P], BF16)
        warm, a = carve(a, [2])
        F, b = carve(p_at, [2, CH])
        R, b = carve(b, [2, CH])
        PRT, b = carve(b, [4, 3, CH], BF16)
        assert b <= ARENA
        ctxT_sb, _ = carve(0, [2, CTX])

        def heads_layer(tag, keys, wq, wo, bq, bk, rv, ro, w_prev):
            cross = keys == CTX
            KT = -(-keys // P)
            sname = lambda n: sem(f"{tag}_{n}")
            qscr = nc.dram_tensor(f"{tag}_q_parts", [3, D, N], BF16).ap()
            kscr = nc.dram_tensor(f"{tag}_k_parts", [3, D, keys], BF16).ap()
            kch = [(n * CH, min(CH, keys - n * CH)) for n in range(-(-keys // CH))]

            units = []
            if w_prev is not None:
                units += [("C", n, c, "act") for n in range(NCH) for c in range(DC)]
                units += [("O", v, 0, "dve") for v in range(NT // 2)]
            kv_units = [("K", n, m, "act") for n in range(len(kch)) for m in range(DC)]
            kv_units += [("V", v, 0, "dve") for v in range(-(-KT // 2))]
            t_units = [("T", n, c, "act") for n in range(NCH) for c in range(DC)]
            q_units = [("Q", n, m, "act") for n in range(NCH) for m in range(DC)]
            units += (kv_units + t_units if cross else t_units + kv_units) + q_units
            split = [u for u in units if u[0] in "KQ"]
            pe_s, act_s, dve_s, stat_s, mv_s, var_s, rstd_s, h_s, p1_s, r1_s, p2_s, p3_s, one_s = (
                sname(n) for n in ("pe", "act", "dve", "stat", "mv", "var", "rstd", "h", "p1", "r1",
                                   "p2", "p3", "one"))
            st_s = [sname(f"st{i}") for i in range(4)]
            kin = sname("ctx") if cross else None
            aq = [(0, KT // 2), (KT // 2, KT)]
            ka_in = [sname(f"ka{i}") for i in range(len(aq))]
            kb_in = sname("kb")
            q_in = [sname(f"q{i}") for i in range(NCH)]

            def stored(sp, j):
                for i in range(max(0, j - 3), j + 1):
                    sp.wait_ge(st_s[i % 4], 16 * (i // 4 + 1))

            def load_k(sp, g, to, lo, hi, loaded):
                for b, part in enumerate(K_PARTS):
                    sp.dma_start(to[b * DH:(b + 1) * DH, :, lo:hi],
                                 kscr[part, g * HG * DH:(g + 1) * HG * DH, lo:hi].rearrange("(h d) t -> d h t", h=HG)
                                 ).then_inc(loaded, 16)

            def load_q(sp, g, c):
                for b, part in enumerate(Q_PARTS):
                    sp.dma_start(Q[b * DH:(b + 1) * DH, c],
                                 qscr[part, g * HG * DH:(g + 1) * HG * DH, c * CH:(c + 1) * CH]
                                 .rearrange("(h d) t -> d h t", h=HG)).then_inc(q_in[c], 16)

            def emptied(u):
                same = sum(1 for w in units[:u + 1] if w[3] == units[u][3])
                return (act_s if units[u][3] == "act" else dve_s), same

            def index(what, i, m):
                return next(n for n, w in enumerate(units) if w[:3] == (what, i, m))

            with nc.Block() as block:
                @block.sync
                def _(sp):
                    if cross:
                        sp.wait_ge(late_in, LATE)
                        sp.dma_start(ctxT_sb[:, 0, :], ctxT[0:P, :]).then_inc(kin, 16)
                        sp.dma_start(ctxT_sb[0:CW - P, 1, :], ctxT[P:CW, :]).then_inc(kin, 16)
                    for j, (what, n, m, _) in enumerate(split):
                        scr = kscr if what == "K" else qscr
                        at, size = kch[n] if what == "K" else (n * CH, CH)
                        sp.wait_ge(p3_s, j + 1)
                        sp.dma_start(scr[:, m * P:(m + 1) * P, at:at + size].rearrange("a p t -> p a t"),
                                     PRT[:, j % 4, :, 0:size]).then_inc(st_s[j % 4], 16)
                        if j == len(split) - 6:
                            stored(sp, j - 2)
                            load_k(sp, 0, KB, 0, keys, kb_in)
                    stored(sp, len(split) - 1)

                @block.gpsimd
                def _(pool):
                    for g in range(NCH):
                        r = slice(4 * g, 4 * g + 4)
                        pool.wait_ge(mv_s, 4 * g + 4)
                        pool.tensor_scalar(vareps[:, r], mv[:, r, 1], EPS, None, ALU.add).then_inc(var_s, 1)
                        pool.wait_ge(var_s, g + 1)
                        pool.tensor_tensor(rstd[:, r], vareps[:, r], mhalf[:, r], ALU.pow).then_inc(rstd_s, 1)
                    pool.memset(VG[:, :, :, DH:2 * DH], 1.0).then_inc(one_s, 1)

                @block.vector
                def _(dve):
                    dve.wait_ge(late_in, LATE)

                    def statistics(g):
                        if w_prev is not None:
                            dve.wait_ge(dve_s, 2 * g + 2)
                        for t in range(4 * g, 4 * g + 4):
                            dve.bn_stats(stats[:, t, :], xres[:, t, :]).then_inc(stat_s, 1)
                        for t in range(4 * g, 4 * g + 4):
                            dve.wait_ge(stat_s, t + 1)
                            dve.bn_aggr(mv[:, t, :], stats[:, t, :]).then_inc(mv_s, 1)

                    def normalize(g):
                        dve.wait_ge(rstd_s, g + 1)
                        for t in range(4 * g, 4 * g + 4):
                            dve.tensor_scalar(hA[:, t, :], xres[:, t, :], mv[:, t, 0:1], rstd[:, t:t + 1],
                                              ALU.subtract, ALU.mult).then_inc(h_s, 1)

                    def layernorm():
                        statistics(0)
                        for g in range(NCH):
                            if g + 1 < NCH:
                                statistics(g + 1)
                            normalize(g)

                    def second_part(j):
                        size = kch[split[j][1]][1] if split[j][0] == "K" else CH
                        dve.wait_ge(p2_s, j + 1)
                        dve.tensor_tensor(PRT[:, j % 4, 2, 0:size], R[:, j % 2, 0:size],
                                          PRT[:, j % 4, 1, 0:size], ALU.subtract).then_inc(p3_s, 1)

                    if cross:
                        layernorm()
                    j = 0
                    for u, (what, i, m, by) in enumerate(units):
                        if not cross and what == "T" and (i, m) == (0, 0):
                            layernorm()
                        if what in "KQ":
                            size = kch[i][1] if what == "K" else CH
                            dve.wait_ge(p1_s, j + 1)
                            if j >= 2:
                                dve.wait_ge(p3_s, j - 1)
                            dve.tensor_tensor(R[:, j % 2, 0:size], F[:, j % 2, 0:size],
                                              PRT[:, j % 4, 0, 0:size], ALU.subtract).then_inc(r1_s, 1)
                            if j:
                                second_part(j - 1)
                            j += 1
                        elif what == "O":
                            dve.wait_ge(pe_s, u + 1)
                            x2 = xres[:, 2 * i:2 * i + 2, :]
                            dve.tensor_tensor(x2, PS[:, u % 8, :].rearrange("p (t d) -> p t d", t=2), x2,
                                              ALU.add).then_inc(dve_s, 1)
                        elif what == "V":
                            dve.wait_ge(pe_s, u + 1)
                            for k in range(2):
                                t = 2 * i + k
                                rows = min(P, keys - t * P)
                                if rows <= 0:
                                    continue
                                last = dve.tensor_tensor(V[0:rows, t, :], PS[0:rows, u % 8, k * D:(k + 1) * D],
                                                         brow[0:rows, rv, :], ALU.add)
                            last.then_inc(dve_s, 1)
                    second_part(len(split) - 1)

                @block.scalar
                def _(act):
                    def first_cut(j):
                        size = kch[split[j][1]][1] if split[j][0] == "K" else CH
                        act.wait_ge(r1_s, j + 1)
                        act.activation(PRT[:, j % 4, 1, 0:size], R[:, j % 2, 0:size], ACT.Copy).then_inc(p2_s, 1)

                    j = 0
                    for u, (what, i, m, by) in enumerate(units):
                        if by != "act":
                            continue
                        act.wait_ge(pe_s, u + 1)
                        if what in "TC":
                            act.activation(hT[:, m, i * CH:(i + 1) * CH], PS[:, u % 8, :], ACT.Copy).then_inc(act_s, 1)
                            continue
                        size = kch[i][1] if what == "K" else CH
                        col = 2 * (bk if what == "K" else bq) + m
                        if j >= 2:
                            act.wait_ge(r1_s, j - 1)
                        if j >= 4:
                            act.wait_ge(st_s[j % 4], 16 * (j // 4))
                        act.activation(F[:, j % 2, 0:size], PS[:, u % 8, 0:size], ACT.Identity,
                                       bias=bcol[:, col:col + 1]).then_inc(act_s, 1)
                        act.wait_ge(*emptied(u))
                        act.activation(PRT[:, j % 4, 0, 0:size], F[:, j % 2, 0:size], ACT.Copy).then_inc(p1_s, 1)
                        if j:
                            first_cut(j - 1)
                        j += 1
                    first_cut(j - 1)

                @block.tensor
                def _(pe):
                    if cross:
                        pe.wait_ge(late_in, LATE)
                        pe.wait_ge(kin, 32)
                    for u, (what, i, m, _) in enumerate(units):
                        if u >= 8:
                            pe.wait_ge(*emptied(u - 8))
                        bank = PS[:, u % 8, :]
                        if what in "TC":
                            if what == "T":
                                pe.wait_ge(h_s, 4 * i + 4)
                            source = hA if what == "T" else CTXO
                            for j in range(4):
                                mm = pe.transpose(bank[:, j * P:(j + 1) * P],
                                                  source[:, 4 * i + j, m * P:(m + 1) * P], ident[:, :])
                        elif what == "O":
                            pe.wait_ge(*emptied(index("C", i // 2, 1)))
                            for j in range(2):
                                t = 2 * i + j
                                for c in range(DC):
                                    mm = pe.matmul(bank[:, j * D:(j + 1) * D], hT[:, c, t * P:(t + 1) * P],
                                                   W[:, w_prev, c, :], start=(c == 0), stop=(c == DC - 1))
                        elif what == "V":
                            if not cross:
                                pe.wait_ge(*emptied(index("T", i // 2, 1)))
                            for j in range(2):
                                t = 2 * i + j
                                rows = min(P, keys - t * P)
                                if rows <= 0:
                                    continue
                                for c in range(DC):
                                    k = P if c == 0 or not cross else CW - P
                                    lhs = (ctxT_sb if cross else hT)[0:k, c, t * P:t * P + rows]
                                    rhs = Wkv[0:k, c, D:2 * D] if cross else W[:, W3V, c, :]
                                    mm = pe.matmul(bank[0:rows, j * D:(j + 1) * D], lhs, rhs,
                                                   start=(c == 0), stop=(c == DC - 1))
                        elif what == "K" and cross:
                            at, size = kch[i]
                            for c in range(DC):
                                k = P if c == 0 else CW - P
                                mm = pe.matmul(bank[:, 0:size], Wkv[0:k, c, m * P:(m + 1) * P],
                                               ctxT_sb[0:k, c, at:at + size], start=(c == 0), stop=(c == DC - 1))
                        else:
                            w = W3K if what == "K" else wq
                            pe.wait_ge(*emptied(index("T", i, 1)))
                            for c in range(DC):
                                mm = pe.matmul(bank, W[:, w, c, m * P:(m + 1) * P], hT[:, c, i * CH:(i + 1) * CH],
                                               start=(c == 0), stop=(c == DC - 1))
                        mm.then_inc(pe_s, 1)

            SLOTS = NCH * KT
            UNITS = 64
            AHEAD = 80
            quarter = [keys * i // 4 for i in range(5)]

            def until(i):
                return i // KT * UNITS + (i % KT) * UNITS // KT

            s_s, exp_s, mx_s, md_s, nm_s, mp_s, mt_s, mc_s, pv_s, u_s, ut_s, un_s, rc_s, vg_s, xb_s, ka1_s, cut_s = (
                sname(n) for n in ("s", "exp", "mx", "md", "nm", "mp", "mt", "mc", "pv", "u", "ut", "un",
                                   "rc", "vg", "xb", "ka_one", "cut"))
            mrow_in = sname("mrow")
            zero_s = sname("zero")

            def turn_slot(q):
                return next(i for i in range(SLOTS + 1) if until(i) + AHEAD >= (q + 1) * UNITS + 6) - 1

            turns = {turn_slot(q): q for q in range(1, 5)}
            outs = {c * KT + 2: c - 1 for c in range(NCH)}

            def slot_units(i, last):
                return [("unit", n) for n in range(until(i) + AHEAD, until(i + 1) + AHEAD)
                        if not (last and n >= NCH * UNITS)]

            def slot_turned(i, first, last):
                entries = []
                if i in turns and not (last and turns[i] >= NCH):
                    entries.append(("turn", turns[i]))
                if i in outs and not (first and outs[i] < 0):
                    entries.append(("out", outs[i]))
                return entries

            def group_ring(first, last):
                ring = [e for i in range(SLOTS) for e in slot_units(i, last) + slot_turned(i, first, last)]
                return ring + [("out", NCH - 1)] * last

            prologue = [("unit", n) for n in range(AHEAD)]
            prologue.insert(UNITS + 8, ("turn", 0))
            kinds = {"first": (True, False), "middle": (False, False), "last": (False, True)}
            rings = {k: group_ring(*v) for k, v in kinds.items()}
            starts = {"first": len(prologue), "middle": len(prologue) + len(rings["first"])}
            starts["last"] = starts["middle"]
            assert len(rings["middle"]) % 3 == 0
            of_group_before = [(what, n - (NCH * UNITS if what == "unit" else NCH))
                               for what, n in rings["middle"][-3:]]
            assert rings["first"][-3:] == rings["middle"][-3:]

            def ring_bank(kind, r):
                return (4, 5, 7)[(r + (starts[kind] if kind != "prologue" else 0)) % 3]

            def bank_free(pe, kind, r, base, chunks):
                if kind == "prologue":
                    if r < 3:
                        return
                    what, n = prologue[r - 3]
                elif r >= 3:
                    what, n = rings[kind][r - 3]
                else:
                    what, n = (prologue[-3:] if kind == "first" else of_group_before)[r]
                if what == "unit":
                    pe.wait_ge(md_s, base + n + 1)
                elif what == "turn":
                    pe.wait_ge(mc_s, chunks + n + 1)
                else:
                    pe.wait_ge(un_s, chunks + n + 1)

            with nc.Block() as block:
                @block.sync
                def _(sp):
                    def load_a(g, n):
                        load_k(sp, g, KA, aq[n][0] * P, min(aq[n][1] * P, keys), ka_in[n])

                    def minus_max(n):
                        sp.wait_ge(mc_s, n + 1)
                        if n >= NCH:
                            sp.wait_ge(s_s, 2 * KT * (n - NCH + 1))
                        for r in range(MROWS):
                            sp.dma_start(Q[ROWS + r:ROWS + r + 1, n % NCH].rearrange("p h (t q) -> p (h t) q", t=4),
                                         mrow[16 * r:16 * r + 16, :]).then_inc(mrow_in, 16)

                    load_q(sp, 0, 0)
                    for n in range(len(aq)):
                        load_a(0, n)
                    for c in range(1, NCH):
                        load_q(sp, 0, c)
                    minus_max(0)
                    for g in range(NG):
                        more = g + 1 < NG
                        minus_max(NCH * g + 1)
                        if more:
                            sp.wait_ge(mx_s, g * NCH * UNITS + 2 * UNITS)
                            load_k(sp, g + 1, KB, 0, keys, kb_in)
                            sp.wait_ge(s_s, 2 * KT * (NCH * g + 1))
                            load_q(sp, g + 1, 0)
                        minus_max(NCH * g + 2)
                        if more:
                            sp.wait_ge(s_s, 2 * KT * (NCH * g + 2))
                            load_q(sp, g + 1, 1)
                        minus_max(NCH * g + 3)
                        if more:
                            sp.wait_ge(s_s, 2 * KT * (NCH * g + 3))
                            load_q(sp, g + 1, 2)
                            sp.wait_ge(s_s, 2 * KT * (NCH * g + 3) + 2 * aq[0][1])
                            load_a(g + 1, 0)
                            minus_max(NCH * g + 4)
                            sp.wait_ge(s_s, 2 * KT * (NCH * g + 4))
                            load_a(g + 1, 1)
                            load_q(sp, g + 1, 3)

                @block.gpsimd
                def _(pool):
                    pool.memset(KA[ROWS:ROWS + MROWS, :, :], 1.0).then_inc(ka1_s, 1)
                    pool.wait_ge(ka1_s, 1)

                    def v_piece(g, n, first):
                        lo, hi = aq[n]
                        if not first:
                            pool.wait_ge(pv_s, KT * (NCH * g - 1) + hi)
                        whole = min(hi, keys // P)
                        for a_, b_, rows in ((lo, whole, P), (whole, hi, keys % P)):
                            if b_ > a_:
                                pool.tensor_copy(
                                    VG[0:rows, a_:b_, :, 0:DH],
                                    V[0:rows, a_:b_, ds(g * HG * DH, HG * DH)].rearrange("p t (h d) -> p t h d", h=HG)
                                ).then_inc(vg_s, 1)

                    def minus_parts(n):
                        pool.wait_ge(nm_s, n + 1)
                        pool.tensor_tensor(mparts[:, 0, :], nm[:, :], ones[:, :], ALU.mult).then_inc(cut_s, 1)
                        pool.wait_ge(cut_s, 3 * n + 1)
                        pool.tensor_tensor(nr[:, :], nm[:, :], mparts[:, 0, :], ALU.subtract).then_inc(cut_s, 1)
                        pool.wait_ge(cut_s, 3 * n + 2)
                        pool.tensor_tensor(mparts[:, 1, :], nr[:, :], ones[:, :], ALU.mult).then_inc(cut_s, 1)
                        pool.wait_ge(cut_s, 3 * n + 3)
                        pool.tensor_tensor(mparts[:, 2, :], nr[:, :], mparts[:, 1, :], ALU.subtract).then_inc(mp_s, 1)

                    for n in range(len(aq)):
                        v_piece(0, n, True)
                    base = xres if cross else hA
                    for t in range(NT):
                        pool.tensor_tensor(base[:, t, :], base[:, t, :], brow[:, ro, :], ALU.add).then_inc(xb_s, 1)
                    pool.wait_ge(zero_s, 1)
                    minus_parts(0)
                    with pool.Fori(0, NG - 1) as g:
                        for q in range(1, NCH + 1):
                            minus_parts(g * NCH + q)
                        for n in range(len(aq)):
                            v_piece(g + 1, n, False)
                    for q in range(1, NCH):
                        minus_parts((NG - 1) * NCH + q)

                def copies(n):
                    return sum((min(hi, keys // P) > lo) + (hi > keys // P) for lo, hi in aq[:n])

                @block.vector
                def _(dve):
                    def entry(kind, r, what, n, base, g):
                        chunks = g * NCH
                        bank = PS[:, ring_bank(kind, r), :]
                        if what == "unit":
                            size = quarter[n % 4 + 1] - quarter[n % 4]
                            slot = n // UNITS % 2
                            dve.wait_ge(mx_s, base + n + 1)
                            dve.tensor_reduce(mxs[:, slot, n % UNITS // 4, n % 4:n % 4 + 1], bank[:, 0:size],
                                              AX.X, ALU.max).then_inc(md_s, 1)
                            if n % UNITS == UNITS - 1:
                                dve.wait_ge(md_s, base + n + 1)
                                dve.tensor_reduce(nm[:, :], mxs[:, slot], AX.X, ALU.max, negate=True).then_inc(nm_s, 1)
                        elif what == "out":
                            t4 = bank.rearrange("p (t h e) -> p t h e", t=4, h=HG)
                            dve.wait_ge(ut_s, chunks + n + 1)
                            if n == NCH - 1:
                                dve.wait_ge(un_s, chunks + n)
                            dve.reciprocal(rc[:, :, :], t4[:, :, :, DH]).then_inc(rc_s, 1)
                            dve.wait_ge(rc_s, chunks + n + 1)
                            c, of = (n, g) if n >= 0 else (NCH - 1, g - 1)
                            to = CTXO[:, 4 * c:4 * c + 4, ds(of * HG * DH, HG * DH)]
                            dve.tensor_tensor(to.rearrange("p t (h d) -> p t h d", h=HG), t4[:, :, :, 0:DH],
                                              rc[:, :, :].unsqueeze(3).to_broadcast([P, 4, HG, DH]),
                                              ALU.mult).then_inc(un_s, 1)

                    def group(g, kind):
                        for r, (what, n) in enumerate(rings[kind]):
                            entry(kind, r, what, n, g * NCH * UNITS, g)

                    dve.memset(mparts[:, :, :], 0.0).then_inc(zero_s, 1)
                    for r, (what, n) in enumerate(prologue):
                        entry("prologue", r, what, n, 0, 0)
                    group(0, "first")
                    with dve.Fori(1, NG - 1) as g:
                        group(g, "middle")
                    group(NG - 1, "last")

                @block.scalar
                def _(act):
                    act.activation(warm[:, 0:1], ident[:, 0:1], ACT.Exp).then_inc(exp_s, 1)
                    act.activation(warm[:, 1:2], ident[:, 0:1], ACT.Exp).then_inc(exp_s, 1)

                    def turned(n, bank):
                        act.wait_ge(mt_s, n + 1)
                        act.activation(mrow[0:16 * MROWS, :], PS[0:16 * MROWS, bank, 0:P // 2].bitcast(BF16),
                                       ACT.Copy).then_inc(mc_s, 1)

                    def sums(n):
                        act.wait_ge(pv_s, KT * (n + 1))
                        act.activation(U[:, :], PS[:, 6, :], ACT.Copy).then_inc(u_s, 1)

                    def group(g, kind):
                        chunks = g * NCH
                        for i in range(SLOTS):
                            kt = i % KT
                            rows = min(P, keys - kt * P)
                            for pair in range(2):
                                act.wait_ge(s_s, chunks * 2 * KT + 2 * i + pair + 1)
                                act.activation(PX[0:rows, i % 2, 2 * pair:2 * pair + 2, :],
                                               PS[0:rows, 2 * pair:2 * pair + 2, :], ACT.Exp,
                                               scale=DH ** -0.5).then_inc(exp_s, 1)
                            if ("turn", turns.get(i)) in rings[kind]:
                                r = rings[kind].index(("turn", turns[i]))
                                turned(chunks + turns[i], ring_bank(kind, r))
                            if kt == 0 and (i or kind != "first"):
                                sums(chunks + i // KT - 1)

                    turned(0, ring_bank("prologue", prologue.index(("turn", 0))))
                    group(0, "first")
                    with act.Fori(1, NG - 1) as g:
                        group(g, "middle")
                    group(NG - 1, "last")
                    sums(NG * NCH - 1)

                @block.tensor
                def _(pe):
                    def entry(kind, r, what, n, base, g):
                        chunks = g * NCH
                        bank = PS[:, ring_bank(kind, r), :]
                        if what == "unit":
                            q = n // UNITS
                            head, tile, k = n % UNITS // 16, n % 16 // 4, n % 4
                            if n % UNITS == 0:
                                pe.wait_ge(q_in[q % NCH], (g + 1 + q // NCH) * 16 * len(Q_PARTS))
                                if q % NCH == 0:
                                    pe.wait_ge(kb_in, (g + 1 + q // NCH) * 16 * len(K_PARTS))
                                if q == 2:
                                    for m in ka_in:
                                        pe.wait_ge(m, (g + 1) * 16 * len(K_PARTS))
                            bank_free(pe, kind, r, base, chunks)
                            source = KA if q in (2, 3) else KB
                            lo, hi = quarter[k], quarter[k + 1]
                            pe.matmul(bank[:, 0:hi - lo], Q[0:ROWS, q % NCH, head, tile * P:(tile + 1) * P],
                                      source[0:ROWS, head, lo:hi], start=True, stop=True).then_inc(mx_s, 1)
                        elif what == "turn":
                            pe.wait_ge(mp_s, chunks + n + 1)
                            bank_free(pe, kind, r, base, chunks)
                            pe.transpose(bank[:, 0:P // 2].bitcast(BF16),
                                         mparts[:, :, :].rearrange("p a b -> p (a b)"), identb[:, :]).then_inc(mt_s, 1)
                        else:
                            pe.wait_ge(u_s, chunks + n + 1)
                            bank_free(pe, kind, r, base, chunks)
                            for t in range(4):
                                mm = pe.transpose(bank[:, t * P:(t + 1) * P], U[:, t * P:(t + 1) * P], ident[:, :])
                            mm.then_inc(ut_s, 1)

                    def scores(g, i, pair):
                        chunks = g * NCH
                        c, kt = divmod(i, KT)
                        rows = min(P, keys - kt * P)
                        if kt == 0 and pair == 0:
                            pe.wait_ge(mrow_in, 16 * MROWS * (chunks + c + 1))
                        if c == 0 and pair == 0:
                            for n, (lo, _) in enumerate(aq):
                                if kt == lo:
                                    pe.wait_ge(ka_in[n], (g + 1) * 16 * len(K_PARTS))
                        pe.wait_ge(exp_s, chunks * 2 * KT + 2 * i + pair + 1)
                        for h in (2 * pair, 2 * pair + 1):
                            mm = pe.matmul(PS[0:rows, h, :], KA[0:ROWS + MROWS, h, kt * P:kt * P + rows],
                                           Q[0:ROWS + MROWS, c, h, :], start=True, stop=True)
                        mm.then_inc(s_s, 1)

                    def products(g, i):
                        chunks = g * NCH
                        c, kt = divmod(i, KT)
                        rows = min(P, keys - kt * P)
                        if c == 0:
                            for n, (lo, _) in enumerate(aq):
                                if kt == lo:
                                    pe.wait_ge(vg_s, g * copies(len(aq)) + copies(n + 1))
                        if kt == 0 and not (c == 0 and isinstance(g, int) and g == 0):
                            pe.wait_ge(u_s, chunks + c)
                        pe.wait_ge(exp_s, chunks * 2 * KT + 2 * i + 4)
                        for h in range(HG):
                            mm = pe.matmul(PS[32 * h:32 * h + 32, 6, :], VG[0:rows, kt, h, :],
                                           PX[0:rows, i % 2, h, :], start=(kt == 0), stop=(kt == KT - 1))
                        mm.then_inc(pv_s, 1)

                    def group(g, kind):
                        base = g * NCH * UNITS
                        first, last = kinds[kind]
                        r = 0
                        for i in range(SLOTS):
                            units, turned = slot_units(i, last), slot_turned(i, first, last)
                            steps = [lambda: scores(g, i, 0), lambda: scores(g, i, 1)]
                            if i or not first:
                                steps.append(lambda: products(g, i - 1))
                            cuts = (0, 1, 3, len(units))
                            for k, do in enumerate(steps):
                                do()
                                for what, n in units[cuts[k]:cuts[k + 1]]:
                                    entry(kind, r, what, n, base, g)
                                    r += 1
                            if len(steps) == 2:
                                for what, n in units[3:]:
                                    entry(kind, r, what, n, base, g)
                                    r += 1
                            for what, n in turned:
                                entry(kind, r, what, n, base, g)
                                r += 1
                        if last:
                            products(g, SLOTS - 1)
                            entry(kind, r, "out", NCH - 1, base, g)

                    pe.wait_ge(one_s, 1)
                    for r, (what, n) in enumerate(prologue):
                        entry("prologue", r, what, n, 0, 0)
                    pe.wait_ge(ka1_s, 1)
                    group(0, "first")
                    with pe.Fori(1, NG - 1) as g:
                        group(g, "middle")
                    group(NG - 1, "last")
            return un_s

        CTXO = sb("CTXO", [P, NT, D])
        heads_layer("c", CTX, W2Q, W2O, B2Q, B2K, R2V, R2O, None)
        heads_layer("s", N, W3Q, W3O, B3Q, B3K, R3V, RBE1, W2O)

        We, a = carve(0, [DC, NE, D])
        AO, a = carve(a, [NT, D])
        YT, a = carve(a, [DC, N])
        MO, a = carve(a, [NT, D])
        wT, a = carve(a, [NCH, CH])
        small = {}
        for name in ("lg", "sh", "ex", "pr", "q1", "o1", "p2", "q2", "o2", "wt", "oo"):
            small[name], a = carve(a, [NT, NE])
        for name in ("mx", "sm", "rc", "m1", "a1", "m2", "a2"):
            small[name], a = carve(a, [NT])
        rev, a = carve(a, [NE])
        stats2, a = carve(a, [NT, 6])
        mv2, a = carve(a, [NT, 2])
        rstd2, a = carve(a, [NT])
        units = [("C", n, c, "act") for n in range(NCH) for c in range(DC)]
        units += [("O", v, 0, "dve") for v in range(NT // 2)]
        for n in range(NCH):
            units += [("T", n, c, "act") for c in range(DC)] + [("G", n, 0, "dve")]
        for n in range(NCH):
            units += [("R", n, 0, "act")] + [("B", v, 0, "act") for v in (2 * n, 2 * n + 1)]
            units += [("M", t, e, "dve") for t in range(4 * n, 4 * n + 4) for e in range(NE // 2)]
        fsem = {n: sem("f_" + n) for n in (
            "we", "pe", "act", "dve", "stat", "mv", "var", "rstd", "n", "ng", "y", "g", "ex", "w", "mo", "stat2",
            "mv2", "rstd2", "n2", "ng2", "res", "o", "out", "rev")}
        pe_s, act_s, dve_s = fsem["pe"], fsem["act"], fsem["dve"]

        def emptied(u):
            same = sum(1 for w in units[:u + 1] if w[3] == units[u][3])
            return (act_s if units[u][3] == "act" else dve_s), same

        def index(what, i, m=0):
            return next(n for n, w in enumerate(units) if w[:3] == (what, i, m))

        def brows4(r):
            return brow[:, r, :].unsqueeze(1).to_broadcast([P, 4, D])

        with nc.Block() as block:
            @block.sync
            def _(sp):
                sp.dma_start(We[:, 0, :, :], we[:, 0:P, :].rearrange("e p f -> p e f")).then_inc(fsem["we"], 16)
                sp.dma_start(We[:, 1, :, :], we[:, P:D, :].rearrange("e p f -> p e f")).then_inc(fsem["we"], 16)
                o = out.rearrange("(t p) d -> p t d", p=P)
                for g in range(NCH):
                    sp.wait_ge(fsem["o"], g + 1)
                    sp.dma_start(o[:, 4 * g:4 * g + 4, :], MO[:, 4 * g:4 * g + 4, :]).then_inc(fsem["out"], 16)
                sp.wait_ge(fsem["out"], 16 * NCH)

            @block.gpsimd
            def _(pool):
                for e in range(NE):
                    pool.memset(rev[:, e:e + 1], float(NE - e)).then_inc(fsem["rev"], 1)
                def reciprocal_std(n, g, mvs, src, to):
                    r = slice(4 * g, 4 * g + 4)
                    pool.wait_ge(mvs, 4 * g + 4)
                    pool.tensor_scalar(vareps[:, r], src[:, r, 1], EPS, None, ALU.add).then_inc(fsem["var"], 1)
                    pool.wait_ge(fsem["var"], n + 1)
                    pool.tensor_tensor(to[:, r], vareps[:, r], mhalf[:, r], ALU.pow).then_inc(fsem["rstd"], 1)

                def gain(g, to, row, normalized, done):
                    r = slice(4 * g, 4 * g + 4)
                    pool.wait_ge(normalized, 4 * g + 4)
                    pool.tensor_tensor(to[:, r, :], to[:, r, :], brows4(row), ALU.mult).then_inc(done, 1)

                for g in range(NCH):
                    reciprocal_std(g, g, fsem["mv"], mv, rstd)
                    if g:
                        gain(g - 1, AO, RG1, fsem["n"], fsem["ng"])
                gain(NCH - 1, AO, RG1, fsem["n"], fsem["ng"])
                for g in range(NCH):
                    r = slice(4 * g, 4 * g + 4)
                    pool.wait_ge(fsem["y"], g + 1)
                    pool.tensor_tensor(xres[:, r, :], xres[:, r, :], hA[:, r, :], ALU.add).then_inc(fsem["res"], 1)
                    pool.wait_ge(fsem["res"], 2 * g + 1)
                    pool.tensor_tensor(xres[:, r, :], xres[:, r, :], brows4(RBE2), ALU.add).then_inc(fsem["res"], 1)
                for g in range(NCH):
                    pool.wait_ge(fsem["rstd"], NCH + g)
                    reciprocal_std(NCH + g, g, fsem["mv2"], mv2, rstd2)
                    gain(g, MO, RG2, fsem["n2"], fsem["ng2"])

            @block.vector
            def _(dve):
                def attention_output(g):
                    for v in (2 * g, 2 * g + 1):
                        u = index("O", v)
                        dve.wait_ge(pe_s, u + 1)
                        bias = brow[:, R3O, :].unsqueeze(1).to_broadcast([P, 2, D])
                        dve.tensor_tensor(AO[:, 2 * v:2 * v + 2, :], PS[:, u % 8, :].rearrange("p (t d) -> p t d", t=2),
                                          bias, ALU.add).then_inc(dve_s, 1)
                    dve.wait_ge(dve_s, 2 * g + 2)
                    for t in range(4 * g, 4 * g + 4):
                        dve.bn_stats(stats[:, t, :], AO[:, t, :]).then_inc(fsem["stat"], 1)
                    for t in range(4 * g, 4 * g + 4):
                        dve.wait_ge(fsem["stat"], t + 1)
                        dve.bn_aggr(mv[:, t, :], stats[:, t, :]).then_inc(fsem["mv"], 1)

                def normalize(g, to, m, r, rdy, s):
                    dve.wait_ge(fsem["rstd"], rdy)
                    for t in range(4 * g, 4 * g + 4):
                        dve.tensor_scalar(to[:, t, :], to[:, t, :], m[:, t, 0:1], r[:, t:t + 1],
                                          ALU.subtract, ALU.mult).then_inc(s, 1)

                def experts_input(g):
                    r = slice(4 * g, 4 * g + 4)
                    dve.wait_ge(fsem["ng"], g + 1)
                    dve.tensor_tensor(hA[:, r, :], hA[:, r, :], AO[:, r, :], ALU.add).then_inc(fsem["y"], 1)

                def gate(g):
                    r = slice(4 * g, 4 * g + 4)
                    u = index("G", g)
                    n = [16 * g]
                    gs = fsem["g"]

                    def chain(ins):
                        ins.then_inc(gs, 1)
                        n[0] += 1
                        dve.wait_ge(gs, n[0])

                    def b(name):
                        return small[name][:, r].unsqueeze(2).to_broadcast([P, 4, NE])

                    s = {k: v[:, r] for k, v in small.items()}
                    revb = rev[:, :].unsqueeze(1).to_broadcast([P, 4, NE])
                    dve.wait_ge(pe_s, u + 1)
                    dve.tensor_tensor(s["lg"], PS[:, u % 8, 0:4 * NE].rearrange("p (t e) -> p t e", t=4),
                                      bgrow[:, :].unsqueeze(1).to_broadcast([P, 4, NE]), ALU.add).then_inc(dve_s, 1)
                    dve.wait_ge(*emptied(u))
                    chain(dve.tensor_reduce(s["mx"], s["lg"], AX.X, ALU.max))
                    chain(dve.tensor_tensor(s["sh"], s["lg"], b("mx"), ALU.subtract))
                    dve.wait_ge(fsem["ex"], g + 1)
                    chain(dve.tensor_reduce(s["sm"], s["ex"], AX.X, ALU.add))
                    chain(dve.reciprocal(s["rc"], s["sm"]))
                    chain(dve.tensor_tensor(s["pr"], s["ex"], b("rc"), ALU.mult))
                    chain(dve.tensor_reduce(s["m1"], s["pr"], AX.X, ALU.max))
                    chain(dve.tensor_tensor(s["q1"], s["pr"], b("m1"), ALU.is_equal))
                    chain(dve.tensor_tensor(s["o2"], s["q1"], revb, ALU.mult))
                    chain(dve.tensor_reduce(s["a1"], s["o2"], AX.X, ALU.max))
                    chain(dve.tensor_tensor(s["o1"], s["o2"], b("a1"), ALU.is_equal))
                    chain(dve.scalar_tensor_tensor(s["p2"], s["o1"], -2.0, s["pr"], ALU.mult, ALU.add))
                    chain(dve.tensor_reduce(s["m2"], s["p2"], AX.X, ALU.max))
                    chain(dve.tensor_tensor(s["q2"], s["p2"], b("m2"), ALU.is_equal))
                    chain(dve.tensor_tensor(s["oo"], s["q2"], revb, ALU.mult))
                    chain(dve.tensor_reduce(s["a2"], s["oo"], AX.X, ALU.max))
                    chain(dve.tensor_tensor(s["q1"], s["oo"], b("a2"), ALU.is_equal))
                    assert n[0] == 16 * g + 16
                    dve.tensor_tensor(s["q2"], s["q1"], s["o1"], ALU.add).then_inc(fsem["w"], 1)
                    dve.wait_ge(fsem["w"], 2 * g + 1)
                    dve.tensor_tensor(s["wt"], s["q2"], s["pr"], ALU.mult).then_inc(fsem["w"], 1)

                mo = [0]

                def experts(t):
                    for e in range(NE // 2):
                        u = index("M", t, e)
                        dve.wait_ge(pe_s, u + 1)
                        if e == 0:
                            dve.wait_ge(*emptied(index("B", t // 2)))
                        for k in range(2):
                            if e or k:
                                dve.wait_ge(fsem["mo"], mo[0])
                            ins = dve.scalar_tensor_tensor(MO[:, t, :], PS[:, u % 8, k * D:(k + 1) * D],
                                                           small["wt"][:, t, 2 * e + k:2 * e + k + 1], MO[:, t, :],
                                                           ALU.mult, ALU.add)
                            if k == 0:
                                ins.then_inc(fsem["mo"], 1)
                                mo[0] += 1
                            else:
                                ins.then_inc(dve_s, 1)
                                dve.wait_ge(*emptied(u))

                def experts_stats(g):
                    for t in range(4 * g, 4 * g + 4):
                        dve.bn_stats(stats2[:, t, :], MO[:, t, :]).then_inc(fsem["stat2"], 1)
                    for t in range(4 * g, 4 * g + 4):
                        dve.wait_ge(fsem["stat2"], t + 1)
                        dve.bn_aggr(mv2[:, t, :], stats2[:, t, :]).then_inc(fsem["mv2"], 1)

                def finish(g):
                    r = slice(4 * g, 4 * g + 4)
                    dve.wait_ge(fsem["ng2"], g + 1)
                    dve.wait_ge(fsem["res"], 2 * g + 2)
                    dve.tensor_tensor(MO[:, r, :], MO[:, r, :], xres[:, r, :], ALU.add).then_inc(fsem["o"], 1)

                for g in range(NCH):
                    attention_output(g)
                    if g:
                        normalize(g - 1, AO, mv, rstd, g, fsem["n"])
                    if g > 1:
                        experts_input(g - 2)
                normalize(NCH - 1, AO, mv, rstd, NCH, fsem["n"])
                experts_input(NCH - 2)
                experts_input(NCH - 1)
                dve.wait_ge(fsem["rev"], NE)
                for g in range(NCH):
                    gate(g)
                for g in range(NCH):
                    dve.wait_ge(fsem["w"], 2 * g + 2)
                    for t in range(4 * g, 4 * g + 4):
                        experts(t)
                    experts_stats(g)
                    if g:
                        finish(g - 1)
                    normalize(g, MO, mv2, rstd2, NCH + g + 1, fsem["n2"])
                finish(NCH - 1)

            @block.scalar
            def _(act):
                for u, (what, i, m, by) in enumerate(units):
                    if what == "G":
                        act.wait_ge(fsem["g"], 16 * i + 2)
                        act.activation(small["ex"][:, 4 * i:4 * i + 4], small["sh"][:, 4 * i:4 * i + 4],
                                       ACT.Exp).then_inc(fsem["ex"], 1)
                    if by != "act":
                        continue
                    act.wait_ge(pe_s, u + 1)
                    if what == "C":
                        act.activation(hT[:, m, i * CH:(i + 1) * CH], PS[:, u % 8, :], ACT.Copy).then_inc(act_s, 1)
                    elif what == "T":
                        act.activation(YT[:, m, i * CH:(i + 1) * CH], PS[:, u % 8, :], ACT.Copy).then_inc(act_s, 1)
                    elif what == "R":
                        act.activation(wT[0:NE, i, :], PS[0:NE, u % 8, :], ACT.Copy).then_inc(act_s, 1)
                    else:
                        act.activation(MO[:, 2 * i:2 * i + 2, :], PS[:, u % 8, :].rearrange("p (t d) -> p t d", t=2),
                                       ACT.Copy).then_inc(act_s, 1)

            @block.tensor
            def _(pe):
                for u, (what, i, m, _) in enumerate(units):
                    if u >= 8:
                        pe.wait_ge(*emptied(u - 8))
                    bank = PS[:, u % 8, :]
                    if what in "CT":
                        if what == "T":
                            pe.wait_ge(fsem["y"], i + 1)
                        source = hA if what == "T" else CTXO
                        for j in range(4):
                            mm = pe.transpose(bank[:, j * P:(j + 1) * P], source[:, 4 * i + j, m * P:(m + 1) * P],
                                              ident[:, :])
                    elif what == "O":
                        pe.wait_ge(*emptied(index("C", i // 2, 1)))
                        for j in range(2):
                            t = 2 * i + j
                            for c in range(DC):
                                mm = pe.matmul(bank[:, j * D:(j + 1) * D], hT[:, c, t * P:(t + 1) * P],
                                               W[:, W3O, c, :], start=(c == 0), stop=(c == DC - 1))
                    elif what == "G":
                        pe.wait_ge(*emptied(index("T", i, 1)))
                        for j in range(4):
                            t = 4 * i + j
                            for c in range(DC):
                                mm = pe.matmul(bank[:, j * NE:(j + 1) * NE], YT[:, c, t * P:(t + 1) * P],
                                               Wg[:, c, :], start=(c == 0), stop=(c == DC - 1))
                    elif what == "R":
                        pe.wait_ge(fsem["w"], 2 * i + 2)
                        for j in range(4):
                            mm = pe.transpose(bank[0:NE, j * P:(j + 1) * P], small["wt"][:, 4 * i + j, :], ident[:, :])
                    elif what == "B":
                        pe.wait_ge(*emptied(index("R", i // 2)))
                        for j in range(2):
                            t = 2 * i + j
                            mm = pe.matmul(bank[:, j * D:(j + 1) * D], wT[0:NE, t // 4, t % 4 * P:(t % 4 + 1) * P],
                                           bexp_sb[:, :], start=True, stop=True)
                    else:
                        if (i, m) == (0, 0):
                            pe.wait_ge(fsem["we"], 32)
                        for c in range(DC):
                            mm = pe.matmul(bank, YT[:, c, i * P:(i + 1) * P],
                                           We[:, c, 2 * m:2 * m + 2, :].rearrange("p e f -> p (e f)"),
                                           start=(c == 0), stop=(c == DC - 1))
                    mm.then_inc(pe_s, 1)


def kernel(**inputs):
    import numpy as np
    import concourse.bacc as bacc
    from concourse.bass_utils import run_bass_kernel_spmd

    i = {k: np.asarray(v) for k, v in inputs.items()}
    t = np.ascontiguousarray
    kv = i["L0_xattn_Wkv"].reshape(H, 2, DH, CW)
    bkv = i["L0_xattn_bkv"].reshape(H, 2, DH)
    columns = [i["L0_attn_bq"], i["L0_attn_bk"], i["L0_xattn_bq"], bkv[:, 0].reshape(D), i["L0_ffn_bq"],
               i["L0_ffn_bk"]]
    arrays = {
        "x": t(i["x"][0]),
        "ctxT": t(i["ctx_768"][0].T),
        "wpack": t(np.stack([i["L0_attn_Wq"].T, i["L0_attn_Wk"].T, i["L0_attn_Wv"].T, i["L0_xattn_Wq"].T,
                             i["L0_xattn_Wo"].T, i["L0_ffn_Wq"], i["L0_ffn_Wk"], i["L0_ffn_Wv"],
                             i["L0_ffn_Wo"]])),
        "wkv": t(np.concatenate([kv[:, 0].reshape(D, CW).T, kv[:, 1].reshape(D, CW).T], 1)),
        "we": t(i["L0_ffn_We"]),
        "wg": t(i["L0_ffn_Wg"]),
        "bcols": t(np.stack([b.reshape(DC, P)[c] for b in columns for c in range(DC)], 1)),
        "brows": t(np.stack([i["L0_attn_bv"], bkv[:, 1].reshape(D), i["L0_xattn_bo"], i["L0_ffn_bv"],
                             i["L0_ffn_bo"], i["L0_ffn_g1"], i["L0_ffn_be1"], i["L0_ffn_g2"],
                             i["L0_ffn_be2"]])),
        "bg": t(i["L0_ffn_bg"]),
        "bexp": t(i["L0_ffn_bexp"]),
    }
    nc = bacc.Bacc("TRN2", target_bir_lowering=False, num_devices=1)
    args = [nc.dram_tensor(n, a.shape, mybir.dt.from_np(a.dtype), kind="ExternalInput").ap()
            for n, a in arrays.items()]
    out = nc.dram_tensor("out", (N, D), F32, kind="ExternalOutput").ap()
    build(nc, *args, out)
    r = run_bass_kernel_spmd(nc, [arrays], core_ids=[0])
    return r.results[0]["out"].reshape(1, N, D)
```

```python
from contextlib import ExitStack

import concourse.bass as bass
from concourse import mybir

F32 = mybir.dt.float32
BF16 = mybir.dt.bfloat16
ALU = mybir.AluOpType
ACT = mybir.ActivationFunctionType
AX = mybir.AxisListType
ds = bass.ds

P = 128
D = 256
DC = D // P
N = 2048
NT = N // P
CH = 512
NCH = N // CH
H = 16
DH = D // H
HG = 4
NG = H // HG
CTX = 1601
CW = 192
NE = 8
EPS = 1e-5
BANK = 512
ROWS = 6 * DH
MROWS = 3
Q_PARTS = (0, 0, 0, 1, 1, 2)
K_PARTS = (0, 1, 2, 0, 1, 0)
W1Q, W1K, W1V, W2Q, W2O, W3Q, W3K, W3V, W3O = range(9)
B1Q, B1K, B2Q, B2K, B3Q, B3K = range(6)
R1V, R2V, R2O, R3V, R3O, RG1, RBE1, RG2, RBE2 = range(9)


def build(nc, x, ctxT, wpack, wkv, we, wg, bcols, brows, bg, bexp, out):
    with ExitStack() as ctx:
        def sb(name, shape, dt=F32):
            return ctx.enter_context(nc.sbuf_tensor(name, shape, dt))

        def sem(name):
            return ctx.enter_context(nc.semaphore(name))

        PS = ctx.enter_context(nc.psum_tensor("PS", [P, 8, BANK], F32))
        xres = sb("xres", [P, NT, D])
        hA = sb("hA", [P, NT, D])
        hT = sb("hT", [P, DC, N])
        W = sb("W", [P, 9, DC, D])
        Wkv = sb("Wkv", [P, 2, 2 * D])
        Wg = sb("Wg", [P, DC, NE])
        bcol = sb("bcol", [P, 12])
        brow = sb("brow", [P, 9, D])
        bgrow = sb("bgrow", [P, NE])
        bexp_sb = sb("bexp_sb", [NE, D])
        ident = sb("ident", [P, P])
        identb = sb("identb", [P, P], BF16)
        stats = sb("stats", [P, NT, 6])
        mv = sb("mv", [P, NT, 2])
        vareps = sb("vareps", [P, NT])
        mhalf = sb("mhalf", [P, NT])
        rstd = sb("rstd", [P, NT])
        ones = sb("ones", [P, NT])
        CTXO = sb("CTXO", [P, NT, D])
        ctxT_sb = CTXO[:, :, :].rearrange("p t d -> p (t d)")[:, 0:2 * CTX].rearrange("p (c t) -> p c t", c=2)
        ARENA = 26500
        arena = sb("arena", [P, ARENA])

        def carve(at, shape, dt=F32):
            n = 1
            for d in shape:
                n *= d
            words = n * (2 if dt == BF16 else 4) // 4
            assert at + words <= ARENA, (at, words)
            v = arena[:, at:at + words]
            if dt == BF16:
                v = v.bitcast(BF16)
            names = "abcd"[:len(shape)]
            if len(shape) > 1:
                v = v.rearrange(f"p ({' '.join(names)}) -> p {' '.join(names)}",
                                **dict(zip(names[1:], shape[1:])))
            return v, at + words

        x_in = [sem(f"x_in{g}") for g in range(NCH)]
        w_in = sem("w_in")
        v_in = sem("v_in")
        late_in = sem("late_in")
        const_rdy = sem("const_rdy")

        xt = x.rearrange("(t p) d -> p t d", p=P)

        qT, a = carve(0, [DC, N])
        kT, a = carve(a, [DC, N])
        V1, a = carve(a, [NT, D])
        qs, a = carve(a, [2, DC, P])
        P1, a = carve(a, [2, N])
        PT, a = carve(a, [2, NT, P])
        rs = sb("rs", [P, 2])
        nmax = sb("nmax", [P, 2])
        nbias = sb("nbias", [P, 2])
        rr = sb("rr", [P, 2])

        sems = {n: sem("a_" + n) for n in (
            "stat", "mv", "var", "rstd", "h", "pe", "act", "dve", "qs", "s", "mx", "nb", "exp", "tr", "pta",
            "ptd", "z", "rr", "x")}
        var_s = sems["var"]
        stat_s, mv_s, rstd_s, h_s, pe_s, act_s, dve_s = (sems[n] for n in (
            "stat", "mv", "rstd", "h", "pe", "act", "dve"))
        qs_s, s_s, mx_s, nb_s, exp_s, tr_s, pta_s, ptd_s, z_s, rr_s, x_s = (sems[n] for n in (
            "qs", "s", "mx", "nb", "exp", "tr", "pta", "ptd", "z", "rr", "x"))

        units = []
        for what, n in (("T", 0), ("K", 0), ("T", 1), ("T", 2), ("K", 1), ("T", 3), ("K", 2), ("K", 3)):
            units += [(what, n, m, True) for m in range(DC)]
        units += [("Q", n, m, m == 0) for n in range(NCH) for m in range(DC)]
        v_first = len(units)
        assert v_first % 8 == 0
        units += [("V", v, 0, False) for v in range(NT // 2)]

        def unit_bank(u):
            return u % 8 if u < v_first else 4 + u % 4

        def bank_before(u):
            if u >= v_first:
                return u - 4
            return u - 8 if u >= 8 else None

        def index(what, i, m):
            return next(n for n, w in enumerate(units) if w[:3] == (what, i, m))

        def emptied(u):
            same = sum(1 for w in units[:u + 1] if w[3] == units[u][3])
            return (act_s if units[u][3] else dve_s), same

        LATE = 16 * 13
        with nc.Block() as block:
            @block.sync
            def _(sp):
                def load_x(g):
                    sp.dma_start(xres[:, 4 * g:4 * g + 4, :], xt[:, 4 * g:4 * g + 4, :]).then_inc(x_in[g], 16)

                load_x(0)
                sp.dma_start(W[:, 0:2], wpack[0:2].rearrange("w (c p) d -> p w c d", p=P)).then_inc(w_in, 16)
                load_x(1)
                sp.dma_start(bcol[:, :], bcols).then_inc(w_in, 16)
                for g in range(2, NCH):
                    load_x(g)
                sp.dma_start(W[:, 2], wpack[2].rearrange("(c p) d -> p c d", p=P)).then_inc(v_in, 16)
                sp.dma_start(brow[:, :, :], brows.partition_broadcast(P)).then_inc(v_in, 16)
                sp.dma_start(Wkv[:, 0, :], wkv[0:P, :]).then_inc(late_in, 16)
                sp.dma_start(Wkv[0:CW - P, 1, :], wkv[P:CW, :]).then_inc(late_in, 16)
                sp.dma_start(ctxT_sb[:, 0, :], ctxT[0:P, :]).then_inc(late_in, 16)
                sp.dma_start(ctxT_sb[0:CW - P, 1, :], ctxT[P:CW, :]).then_inc(late_in, 16)
                for w in range(3, 9):
                    sp.dma_start(W[:, w], wpack[w].rearrange("(c p) d -> p c d", p=P)).then_inc(late_in, 16)
                sp.dma_start(Wg[:, :, :], wg.rearrange("(c p) e -> p c e", p=P)).then_inc(late_in, 16)
                sp.dma_start(bgrow[:, :], bg.partition_broadcast(P)).then_inc(late_in, 16)
                sp.dma_start(bexp_sb[:, :], bexp).then_inc(late_in, 16)

            @block.gpsimd
            def _(pool):
                pool.memset(ident[:, :], 0.0).then_inc(const_rdy, 1)
                pool.memset(identb[:, :], 0.0).then_inc(const_rdy, 1)
                pool.memset(mhalf[:, :], -0.5).then_inc(const_rdy, 1)
                pool.memset(ones[:, :], 1.0).then_inc(const_rdy, 1)
                pool.wait_ge(const_rdy, 4)
                for m in (ident, identb):
                    pool.affine_select(out=m[:, :], in_=m[:, :], compare_op=ALU.not_equal, fill=1.0,
                                       base=0, pattern=[[-1, P]], channel_multiplier=1).then_inc(const_rdy, 1)
                for g in range(NCH):
                    r = slice(4 * g, 4 * g + 4)
                    pool.wait_ge(mv_s, 4 * g + 4)
                    pool.tensor_scalar(vareps[:, r], mv[:, r, 1], EPS, None, ALU.add).then_inc(var_s, 1)
                    pool.wait_ge(var_s, g + 1)
                    pool.tensor_tensor(rstd[:, r], vareps[:, r], mhalf[:, r], ALU.pow).then_inc(rstd_s, 1)
                def q_emptied(i):
                    pool.wait_ge(*emptied(index("Q", i, 0)))
                    pool.wait_ge(*emptied(index("Q", i, 1)))


                def q_tile(t, par, first):
                    if not first:
                        pool.wait_ge(s_s, t - 1)
                    pool.tensor_copy(qs[:, par], qT[:, :, ds(t * P, P)]).then_inc(qs_s, 1)

                q_emptied(0)
                q_tile(0, 0, True)
                q_tile(1, 1, True)
                q_emptied(NCH - 1)
                with pool.Fori(1, NT // 2) as i:
                    t = 2 * i
                    q_tile(t, 0, False)
                    q_tile(t + 1, 1, False)

            @block.vector
            def _(dve):
                def statistics(g):
                    dve.wait_ge(x_in[g], 16)
                    for t in range(4 * g, 4 * g + 4):
                        dve.bn_stats(stats[:, t, :], xres[:, t, :]).then_inc(stat_s, 1)
                    for t in range(4 * g, 4 * g + 4):
                        dve.wait_ge(stat_s, t + 1)
                        dve.bn_aggr(mv[:, t, :], stats[:, t, :]).then_inc(mv_s, 1)

                def normalize(g):
                    dve.wait_ge(rstd_s, g + 1)
                    for t in range(4 * g, 4 * g + 4):
                        dve.tensor_scalar(hA[:, t, :], xres[:, t, :], mv[:, t, 0:1], rstd[:, t:t + 1],
                                          ALU.subtract, ALU.mult).then_inc(h_s, 1)

                statistics(0)
                normalize(0)
                statistics(1)
                for g in range(1, NCH):
                    if g + 1 < NCH:
                        statistics(g + 1)
                    normalize(g)
                def unit(u):
                    _, i, m, _ = units[u]
                    dve.wait_ge(pe_s, u + 1)
                    if u >= v_first:
                        bias = brow[:, R1V, :].unsqueeze(1).to_broadcast([P, 2, D])
                        dve.tensor_tensor(V1[:, 2 * i:2 * i + 2, :],
                                          PS[:, unit_bank(u), :].rearrange("p (t d) -> p t d", t=2), bias,
                                          ALU.add).then_inc(dve_s, 1)
                    else:
                        dve.tensor_scalar(qT[:, m, i * CH:(i + 1) * CH], PS[:, unit_bank(u), :],
                                          bcol[:, 2 * B1Q + m:2 * B1Q + m + 1], None, ALU.add).then_inc(dve_s, 1)

                dve.wait_ge(w_in, 32)
                for u in range(v_first):
                    if not units[u][3]:
                        unit(u)

                S = PS[:, 0:4, :].rearrange("p a b -> p (a b)")

                def softmax_max(t, par):
                    dve.wait_ge(s_s, t + 1)
                    dve.tensor_reduce(nmax[:, par:par + 1], S, AX.X, ALU.max, negate=True).then_inc(mx_s, 1)
                    dve.wait_ge(mx_s, t + 1)
                    dve.tensor_scalar(nbias[:, par:par + 1], nmax[:, par:par + 1], D ** -0.5, None,
                                      ALU.mult).then_inc(nb_s, 1)

                def tile(t, par, last):
                    for j in (1, 3):
                        dve.wait_ge(tr_s, 4 * t + j + 1)
                        dve.tensor_copy(PT[:, par, 4 * j:4 * j + 4, :],
                                        PS[:, 4 + j % 2, :].rearrange("p (a b) -> p a b", a=4)).then_inc(ptd_s, 1)
                    if not last:
                        softmax_max(t + 1, 1 - par)
                    dve.wait_ge(exp_s, t + 1)
                    dve.reciprocal(rr[:, par:par + 1], rs[:, par:par + 1]).then_inc(rr_s, 1)
                    dve.wait_ge(rr_s, t + 1)
                    dve.wait_ge(z_s, t + 1)
                    xt_ = xres[:, ds(t, 1), :].rearrange("p a d -> p (a d)")
                    dve.scalar_tensor_tensor(xt_, PS[:, 6 + par, 0:D], rr[:, par:par + 1], xt_,
                                             ALU.mult, ALU.add).then_inc(x_s, 1)

                softmax_max(0, 0)
                dve.wait_ge(v_in, 32)
                for u in range(v_first, len(units)):
                    unit(u)
                tile(0, 0, False)
                tile(1, 1, False)
                with dve.Fori(1, NT // 2 - 1) as i:
                    t = 2 * i
                    tile(t, 0, False)
                    tile(t + 1, 1, False)
                tile(NT - 2, 0, False)
                tile(NT - 1, 1, True)

            @block.scalar
            def _(act):
                for u, (what, i, m, by_act) in enumerate(units):
                    if not by_act:
                        continue
                    act.wait_ge(pe_s, u + 1)
                    if what == "T":
                        act.activation(hT[:, m, i * CH:(i + 1) * CH], PS[:, u % 8, :], ACT.Copy).then_inc(act_s, 1)
                    else:
                        act.wait_ge(w_in, 32)
                        to, b = (kT, B1K) if what == "K" else (qT, B1Q)
                        act.activation(to[:, m, i * CH:(i + 1) * CH], PS[:, u % 8, :], ACT.Identity,
                                       bias=bcol[:, 2 * b + m:2 * b + m + 1]).then_inc(act_s, 1)

                S = PS[:, 0:4, :].rearrange("p a b -> p (a b)")

                def exps(t, par, first):
                    act.wait_ge(nb_s, t + 1)
                    if not first:
                        act.wait_ge(tr_s, 4 * t - 4)
                        act.wait_ge(rr_s, t - 1)
                    act.activation(P1[:, par, :], S, ACT.Exp, bias=nbias[:, par:par + 1], scale=D ** -0.5,
                                   accum_out=rs[:, par:par + 1]).then_inc(exp_s, 1)

                def tile(t, par, first, last):
                    for j in (0, 2):
                        act.wait_ge(tr_s, 4 * t + j + 1)
                        act.activation(PT[:, par, 4 * j:4 * j + 4, :],
                                       PS[:, 4 + j % 2, :].rearrange("p (a b) -> p a b", a=4),
                                       ACT.Copy).then_inc(pta_s, 1)
                    if not last:
                        exps(t + 1, 1 - par, first)

                exps(0, 0, True)
                tile(0, 0, True, False)
                tile(1, 1, False, False)
                with act.Fori(1, NT // 2 - 1) as i:
                    t = 2 * i
                    tile(t, 0, False, False)
                    tile(t + 1, 1, False, False)
                tile(NT - 2, 0, False, False)
                tile(NT - 1, 1, False, True)

            @block.tensor
            def _(pe):
                pe.wait_ge(const_rdy, 6)
                def unit(u):
                    what, i, m, _ = units[u]
                    if bank_before(u) is not None:
                        pe.wait_ge(*emptied(bank_before(u)))
                    bank = PS[:, unit_bank(u), :]
                    if what == "T":
                        pe.wait_ge(h_s, 4 * i + 4)
                        for j in range(4):
                            mm = pe.transpose(bank[:, j * P:(j + 1) * P], hA[:, 4 * i + j, m * P:(m + 1) * P],
                                              ident[:, :])
                    elif what == "V":
                        for j in range(2):
                            t = 2 * i + j
                            for c in range(DC):
                                mm = pe.matmul(bank[:, j * D:(j + 1) * D], hT[:, c, t * P:(t + 1) * P],
                                               W[:, W1V, c, :], start=(c == 0), stop=(c == DC - 1))
                    else:
                        w = W1K if what == "K" else W1Q
                        pe.wait_ge(w_in, 32)
                        pe.wait_ge(*emptied(index("T", i, 1)))
                        for c in range(DC):
                            mm = pe.matmul(bank, W[:, w, c, m * P:(m + 1) * P], hT[:, c, i * CH:(i + 1) * CH],
                                           start=(c == 0), stop=(c == DC - 1))
                    mm.then_inc(pe_s, 1)

                def scores(t, par, n):
                    if n == 0:
                        pe.wait_ge(qs_s, t + 1)
                    for c in range(DC):
                        mm = pe.matmul(PS[:, n, :], qs[:, par, c, :], kT[:, c, n * CH:(n + 1) * CH],
                                       start=(c == 0), stop=(c == DC - 1))
                    if n == 3:
                        mm.then_inc(s_s, 1)

                def transposes(t, par, j, first):
                    if j == 0:
                        pe.wait_ge(exp_s, t + 1)
                    if j >= 2 or not first:
                        pe.wait_ge(pta_s if j % 2 == 0 else ptd_s, 2 * t + j // 2)
                    for i in range(4):
                        k = 4 * j + i
                        mm = pe.transpose(PS[:, 4 + j % 2, i * P:(i + 1) * P], P1[:, par, k * P:(k + 1) * P],
                                          ident[:, :])
                    mm.then_inc(tr_s, 1)

                def products(t, par, j, first):
                    if j == 0 and not first:
                        pe.wait_ge(x_s, t - 1)
                    pe.wait_ge(pta_s if j % 2 == 0 else ptd_s, 2 * t + j // 2 + 1)
                    for k in range(4 * j, 4 * j + 4):
                        mm = pe.matmul(PS[:, 6 + par, 0:D], PT[:, par, k, :], V1[:, k, :],
                                       start=(k == 0), stop=(k == NT - 1))
                    if j == 3:
                        mm.then_inc(z_s, 1)

                def tile(t, par, first, second, last):
                    for j in range(4):
                        transposes(t, par, j, first)
                        if not last:
                            scores(t + 1, 1 - par, j)
                    for j in range(4):
                        products(t, par, j, first or second)

                for u in range(v_first):
                    unit(u)
                for u in range(v_first - 8, v_first - 4):
                    pe.wait_ge(*emptied(u))
                for n in range(4):
                    scores(0, 0, n)
                pe.wait_ge(v_in, 32)
                for u in range(v_first, len(units)):
                    unit(u)
                for u in range(len(units) - 4, len(units)):
                    pe.wait_ge(*emptied(u))
                tile(0, 0, True, False, False)
                tile(1, 1, False, True, False)
                with pe.Fori(1, NT // 2 - 1) as i:
                    t = 2 * i
                    tile(t, 0, False, False, False)
                    tile(t + 1, 1, False, False, False)
                tile(NT - 2, 0, False, False, False)
                tile(NT - 1, 1, False, False, True)

        KA, a = carve(0, [HG, N], BF16)
        KB, a = carve(a, [HG, N], BF16)
        Q, a = carve(a, [NCH, HG, CH], BF16)
        V, a = carve(a, [NT, D])
        VG, a = carve(a, [NT, HG, 2 * DH])
        p_at = a
        PX, a = carve(a, [2, HG, CH])
        U, a = carve(a, [CH])
        a += 512
        mxs, a = carve(a, [2, 16, 4])
        nm, a = carve(a, [16])
        nr, a = carve(a, [16])
        mparts, a = carve(a, [8, 16], BF16)
        rc, a = carve(a, [4, HG])
        mrow, a = carve(a, [P], BF16)
        warm, a = carve(a, [2])
        F, b = carve(p_at, [2, CH])
        R, b = carve(b, [2, CH])
        PRT, b = carve(b, [4, 3, CH], BF16)
        assert b <= ARENA - 512

        def heads_layer(tag, keys, wq, bq, bk, rv, ro, w_prev):
            cross = keys == CTX
            KT = -(-keys // P)
            sname = lambda n: sem(f"{tag}_{n}")
            qscr = nc.dram_tensor(f"{tag}_q_parts", [3, D, N], BF16).ap()
            kscr = nc.dram_tensor(f"{tag}_k_parts", [3, D, keys], BF16).ap()
            kch = [(n * CH, min(CH, keys - n * CH)) for n in range(-(-keys // CH))]

            units = []
            if w_prev is not None:
                for n in range(NCH + 1):
                    if n < NCH:
                        units += [("C", n, c, "act") for c in range(DC)]
                    if n:
                        units += [("O", v, 0, "dve") for v in (2 * n - 2, 2 * n - 1)]
            k_units = [("K", n, m, "act") for n in range(len(kch)) for m in range(DC)]
            t_units = [("T", n, c, "act") for n in range(NCH) for c in range(DC)]
            q_units = [("Q", n, m, "act") for n in range(NCH) for m in range(DC)]
            if cross:
                units += k_units + [("V", v, 0, "act") for v in range(4)]
                units += t_units
            else:
                units += t_units[:2 * DC]
                for n in range(2, NCH):
                    units += k_units[DC * (n - 2):DC * (n - 1)] + t_units[DC * n:DC * (n + 1)]
                units += k_units[DC * (NCH - 2):]
            units += q_units
            v_units, v_mid = -(-KT // 2), 4 if cross else 0
            v_end = min(3, v_units - v_mid)
            bank_shift = len(units)
            units += [("V", v, 0, "next") for v in range(v_mid, v_mid + v_end)]

            def bank_of(u):
                return PS[:, (u - bank_shift) % 8, :]

            def v_copies(act, v, bank):
                for k in range(2):
                    t = 2 * v + k
                    rows = min(P, keys - t * P)
                    if rows > 0:
                        copied = act.activation(V[0:rows, t, :], bank[0:rows, k * D:(k + 1) * D], ACT.Copy)
                return copied

            def v_products(pe, v, bank):
                for k in range(2):
                    t = 2 * v + k
                    rows = min(P, keys - t * P)
                    for c in range(DC if rows > 0 else 0):
                        dims = P if c == 0 or not cross else CW - P
                        lhs = (ctxT_sb if cross else hT)[0:dims, c, t * P:t * P + rows]
                        rhs = Wkv[0:dims, c, D:2 * D] if cross else W[:, W3V, c, :]
                        mm = pe.matmul(bank[0:rows, k * D:(k + 1) * D], lhs, rhs, start=(c == 0), stop=(c == DC - 1))
                return mm
            split = [u for u in units if u[0] in "KQ"]
            pe_s, act_s, dve_s, stat_s, mv_s, var_s, rstd_s, h_s, p1_s, r1_s, p2_s, p3_s, one_s = (
                sname(n) for n in ("pe", "act", "dve", "stat", "mv", "var", "rstd", "h", "p1", "r1",
                                   "p2", "p3", "one"))
            st_s = [sname(f"st{i}") for i in range(4)]
            aq = [(0, KT // 2), (KT // 2, KT)]
            ka_in = [sname(f"ka{i}") for i in range(len(aq))]
            kb_in = sname("kb")
            q_in = [sname(f"q{i}") for i in range(NCH)]

            def stored(sp, j):
                for i in range(max(0, j - 3), j + 1):
                    sp.wait_ge(st_s[i % 4], 16 * (i // 4 + 1))

            def load_k(sp, g, to, lo, hi, loaded, blocks=range(6)):
                for b in blocks:
                    part = K_PARTS[b]
                    sp.dma_start(to[b * DH:(b + 1) * DH, :, lo:hi],
                                 kscr[part, g * HG * DH:(g + 1) * HG * DH, lo:hi].rearrange("(h d) t -> d h t", h=HG)
                                 ).then_inc(loaded, 16)

            def load_q(sp, g, c, blocks=range(6)):
                for b in blocks:
                    part = Q_PARTS[b]
                    sp.dma_start(Q[b * DH:(b + 1) * DH, c],
                                 qscr[part, g * HG * DH:(g + 1) * HG * DH, c * CH:(c + 1) * CH]
                                 .rearrange("(h d) t -> d h t", h=HG)).then_inc(q_in[c], 16)

            def emptied(u):
                same = sum(1 for w in units[:u + 1] if w[3] == units[u][3])
                return (act_s if units[u][3] == "act" else dve_s), same

            def index(what, i, m):
                return next(n for n, w in enumerate(units) if w[:3] == (what, i, m))

            with nc.Block() as block:
                @block.sync
                def _(sp):
                    for j, (what, n, m, _) in enumerate(split):
                        k = j - len(k_units) - 1
                        if k == 0:
                            stored(sp, len(k_units) - 1)
                        if k == 3:
                            stored(sp, len(k_units))
                        if 0 <= k < 3:
                            load_k(sp, 0, KB, 0, keys, kb_in, (2 * k, 2 * k + 1))
                        if 3 <= k < 6:
                            load_q(sp, 0, 0, (2 * k - 6, 2 * k - 5))
                        scr = kscr if what == "K" else qscr
                        at, size = kch[n] if what == "K" else (n * CH, CH)
                        sp.wait_ge(p3_s, j + 1)
                        sp.dma_start(scr[:, m * P:(m + 1) * P, at:at + size].rearrange("a p t -> p a t"),
                                     PRT[:, j % 4, :, 0:size]).then_inc(st_s[j % 4], 16)

                @block.gpsimd
                def _(pool):
                    for g in range(NCH):
                        r = slice(4 * g, 4 * g + 4)
                        pool.wait_ge(mv_s, 4 * g + 4)
                        pool.tensor_scalar(vareps[:, r], mv[:, r, 1], EPS, None, ALU.add).then_inc(var_s, 1)
                        pool.wait_ge(var_s, g + 1)
                        pool.tensor_tensor(rstd[:, r], vareps[:, r], mhalf[:, r], ALU.pow).then_inc(rstd_s, 1)
                    pool.memset(VG[:, :, :, DH:2 * DH], 1.0).then_inc(one_s, 1)

                @block.vector
                def _(dve):
                    dve.wait_ge(late_in, LATE)

                    def statistics(g):
                        if w_prev is not None:
                            dve.wait_ge(dve_s, 2 * g + 2)
                        for t in range(4 * g, 4 * g + 4):
                            dve.bn_stats(stats[:, t, :], xres[:, t, :]).then_inc(stat_s, 1)
                        for t in range(4 * g, 4 * g + 4):
                            dve.wait_ge(stat_s, t + 1)
                            dve.bn_aggr(mv[:, t, :], stats[:, t, :]).then_inc(mv_s, 1)

                    def normalize(g):
                        dve.wait_ge(rstd_s, g + 1)
                        for t in range(4 * g, 4 * g + 4):
                            dve.tensor_scalar(hA[:, t, :], xres[:, t, :], mv[:, t, 0:1], rstd[:, t:t + 1],
                                              ALU.subtract, ALU.mult).then_inc(h_s, 1)

                    pieces = [(statistics, 0), (statistics, 1), (normalize, 0), (statistics, 2), (normalize, 1),
                              (statistics, 3), (normalize, 2), (normalize, 3)]

                    def second_part(j):
                        size = kch[split[j][1]][1] if split[j][0] == "K" else CH
                        dve.wait_ge(p2_s, j + 1)
                        dve.tensor_tensor(PRT[:, j % 4, 2, 0:size], R[:, j % 2, 0:size],
                                          PRT[:, j % 4, 1, 0:size], ALU.subtract).then_inc(p3_s, 1)

                    j = 0
                    for u, (what, i, m, by) in enumerate(units):
                        if what in "KQ":
                            size = kch[i][1] if what == "K" else CH
                            dve.wait_ge(p1_s, j + 1)
                            if j >= 2:
                                dve.wait_ge(p3_s, j - 1)
                            dve.tensor_tensor(R[:, j % 2, 0:size], F[:, j % 2, 0:size],
                                              PRT[:, j % 4, 0, 0:size], ALU.subtract).then_inc(r1_s, 1)
                            if j:
                                second_part(j - 1)
                            if cross and what == "K":
                                piece, g = pieces[j]
                                piece(g)
                            j += 1
                        elif what == "O":
                            dve.wait_ge(pe_s, u + 1)
                            x2 = xres[:, 2 * i:2 * i + 2, :]
                            dve.tensor_tensor(x2, bank_of(u).rearrange("p (t d) -> p t d", t=2), x2,
                                              ALU.add).then_inc(dve_s, 1)
                            if i % 2:
                                statistics(i // 2)
                                if i > 1:
                                    normalize(i // 2 - 1)
                            if i == NT // 2 - 1:
                                normalize(NCH - 1)
                    second_part(len(split) - 1)

                @block.scalar
                def _(act):
                    def first_cut(j):
                        size = kch[split[j][1]][1] if split[j][0] == "K" else CH
                        act.wait_ge(r1_s, j + 1)
                        act.activation(PRT[:, j % 4, 1, 0:size], R[:, j % 2, 0:size], ACT.Copy).then_inc(p2_s, 1)

                    j = 0
                    for u, (what, i, m, by) in enumerate(units):
                        if by != "act":
                            continue
                        act.wait_ge(pe_s, u + 1)
                        if what == "V":
                            v_copies(act, i, bank_of(u)).then_inc(act_s, 1)
                            continue
                        if what in "TC":
                            act.activation(hT[:, m, i * CH:(i + 1) * CH], bank_of(u), ACT.Copy).then_inc(act_s, 1)
                            continue
                        size = kch[i][1] if what == "K" else CH
                        col = 2 * (bk if what == "K" else bq) + m
                        if j >= 2:
                            act.wait_ge(r1_s, j - 1)
                        if j >= 4:
                            act.wait_ge(st_s[j % 4], 16 * (j // 4))
                        act.activation(F[:, j % 2, 0:size], bank_of(u)[:, 0:size], ACT.Identity,
                                       bias=bcol[:, col:col + 1]).then_inc(act_s, 1)
                        act.wait_ge(*emptied(u))
                        act.activation(PRT[:, j % 4, 0, 0:size], F[:, j % 2, 0:size], ACT.Copy).then_inc(p1_s, 1)
                        if j:
                            first_cut(j - 1)
                        j += 1
                    first_cut(j - 1)

                @block.tensor
                def _(pe):
                    if cross:
                        pe.wait_ge(late_in, LATE)
                    for u, (what, i, m, _) in enumerate(units):
                        if u >= 8:
                            pe.wait_ge(*emptied(u - 8))
                        bank = bank_of(u)
                        if what in "TC":
                            if what == "T":
                                pe.wait_ge(h_s, 4 * i + 4)
                            source = hA if what == "T" else CTXO
                            for j in range(4):
                                mm = pe.transpose(bank[:, j * P:(j + 1) * P],
                                                  source[:, 4 * i + j, m * P:(m + 1) * P], ident[:, :])
                        elif what == "O":
                            pe.wait_ge(*emptied(index("C", i // 2, 1)))
                            for j in range(2):
                                t = 2 * i + j
                                for c in range(DC):
                                    mm = pe.matmul(bank[:, j * D:(j + 1) * D], hT[:, c, t * P:(t + 1) * P],
                                                   W[:, w_prev, c, :], start=(c == 0), stop=(c == DC - 1))
                        elif what == "V":
                            mm = v_products(pe, i, bank)
                        elif what == "K" and cross:
                            at, size = kch[i]
                            for c in range(DC):
                                k = P if c == 0 else CW - P
                                mm = pe.matmul(bank[:, 0:size], Wkv[0:k, c, m * P:(m + 1) * P],
                                               ctxT_sb[0:k, c, at:at + size], start=(c == 0), stop=(c == DC - 1))
                        else:
                            w = W3K if what == "K" else wq
                            pe.wait_ge(*emptied(index("T", i, 1)))
                            for c in range(DC):
                                mm = pe.matmul(bank, W[:, w, c, m * P:(m + 1) * P], hT[:, c, i * CH:(i + 1) * CH],
                                               start=(c == 0), stop=(c == DC - 1))
                        mm.then_inc(pe_s, 1)

            SLOTS = NCH * KT
            UNITS = 64
            AHEAD = 84
            quarter = [keys * i // 4 for i in range(5)]

            def until(i):
                return i // KT * UNITS + (i % KT) * UNITS // KT

            s_s, exp_s, mx_s, md_s, nm_s, mp_s, mt_s, mc_s, pv_s, u_s, ut_s, un_s, rc_s, vg_s, xb_s, ka1_s, cut_s = (
                sname(n) for n in ("s", "exp", "mx", "md", "nm", "mp", "mt", "mc", "pv", "u", "ut", "un",
                                   "rc", "vg", "xb", "ka_one", "cut"))
            mrow_in = sname("mrow")
            zero_s = sname("zero")
            vmm_s, v_s = sname("vmm"), sname("v")

            def turn_slot(q):
                return next(i for i in range(SLOTS + 1) if until(i) + AHEAD >= (q + 1) * UNITS + 6) - 1

            turns = {turn_slot(q): q for q in range(1, 5)}
            outs = {c * KT + 2: c - 1 for c in range(NCH)}

            def slot_units(i, last):
                return [("unit", n) for n in range(until(i) + AHEAD, until(i + 1) + AHEAD)
                        if not (last and n >= NCH * UNITS)]

            def slot_turned(i, first, last):
                entries = []
                if i in turns and not (last and turns[i] >= NCH):
                    entries.append(("turn", turns[i]))
                if i in outs and not (first and outs[i] < 0):
                    entries.append(("out", outs[i]))
                return entries

            def group_ring(first, last):
                ring = [e for i in range(SLOTS) for e in slot_units(i, last) + slot_turned(i, first, last)]
                return ring + [("out", NCH - 1)] * last

            prologue = [("unit", n) for n in range(AHEAD)]
            prologue.insert(UNITS + 8, ("turn", 0))
            kinds = {"first": (True, False), "middle": (False, False), "last": (False, True)}
            rings = {k: group_ring(*v) for k, v in kinds.items()}
            starts = {"first": len(prologue), "middle": len(prologue) + len(rings["first"])}
            starts["last"] = starts["middle"]
            assert len(rings["middle"]) % 3 == 0
            of_group_before = [(what, n - (NCH * UNITS if what == "unit" else NCH))
                               for what, n in rings["middle"][-3:]]
            assert rings["first"][-3:] == rings["middle"][-3:]

            def ring_bank(kind, r):
                return (4, 5, 7)[(r + (starts[kind] if kind != "prologue" else 0)) % 3]

            def bank_free(pe, kind, r, base, chunks):
                if kind == "prologue":
                    if r < 3:
                        return
                    what, n = prologue[r - 3]
                elif r >= 3:
                    what, n = rings[kind][r - 3]
                else:
                    what, n = (prologue[-3:] if kind == "first" else of_group_before)[r]
                if what == "unit":
                    pe.wait_ge(md_s, base + n + 1)
                elif what == "turn":
                    pe.wait_ge(mc_s, chunks + n + 1)
                else:
                    pe.wait_ge(un_s, chunks + n + 1)

            with nc.Block() as block:
                @block.sync
                def _(sp):
                    def load_a(g, n):
                        load_k(sp, g, KA, aq[n][0] * P, min(aq[n][1] * P, keys), ka_in[n])

                    def minus_max(n):
                        sp.wait_ge(mc_s, n + 1)
                        if n >= NCH:
                            sp.wait_ge(s_s, 2 * KT * (n - NCH + 1))
                        for r in range(MROWS):
                            sp.dma_start(Q[ROWS + r:ROWS + r + 1, n % NCH].rearrange("p h (t q) -> p (h t) q", t=4),
                                         mrow[16 * r:16 * r + 16, :]).then_inc(mrow_in, 16)

                    for n in range(len(aq)):
                        load_a(0, n)
                    stored(sp, len(split) - 1)
                    for c in range(1, NCH):
                        load_q(sp, 0, c)
                    minus_max(0)
                    for g in range(NG):
                        more = g + 1 < NG
                        minus_max(NCH * g + 1)
                        if more:
                            sp.wait_ge(mx_s, g * NCH * UNITS + 2 * UNITS)
                            load_k(sp, g + 1, KB, 0, keys, kb_in)
                            sp.wait_ge(s_s, 2 * KT * (NCH * g + 1))
                            load_q(sp, g + 1, 0)
                        minus_max(NCH * g + 2)
                        if more:
                            sp.wait_ge(s_s, 2 * KT * (NCH * g + 2))
                            load_q(sp, g + 1, 1)
                        minus_max(NCH * g + 3)
                        if more:
                            sp.wait_ge(s_s, 2 * KT * (NCH * g + 3))
                            load_q(sp, g + 1, 2)
                            sp.wait_ge(s_s, 2 * KT * (NCH * g + 3) + 2 * aq[0][1])
                            load_a(g + 1, 0)
                            minus_max(NCH * g + 4)
                            sp.wait_ge(s_s, 2 * KT * (NCH * g + 4))
                            load_a(g + 1, 1)
                            load_q(sp, g + 1, 3)

                @block.gpsimd
                def _(pool):
                    pool.memset(KA[ROWS:ROWS + MROWS, :, :], 1.0).then_inc(ka1_s, 1)
                    pool.wait_ge(ka1_s, 1)

                    def v_piece(g, n, first):
                        lo, hi = aq[n]
                        if not first:
                            pool.wait_ge(pv_s, KT * (NCH * g - 1) + hi)
                        whole = min(hi, keys // P)
                        for a_, b_, rows in ((lo, whole, P), (whole, hi, keys % P)):
                            if b_ > a_:
                                cols = ds(g * HG * DH, HG * DH)
                                bias = brow[0:rows, rv, cols].rearrange("p (h d) -> p h d", h=HG)
                                pool.tensor_tensor(
                                    VG[0:rows, a_:b_, :, 0:DH],
                                    V[0:rows, a_:b_, cols].rearrange("p t (h d) -> p t h d", h=HG),
                                    bias.unsqueeze(1).to_broadcast([rows, b_ - a_, HG, DH]), ALU.add).then_inc(vg_s, 1)

                    def minus_parts(n):
                        pool.wait_ge(nm_s, n + 1)
                        pool.tensor_tensor(mparts[:, 0, :], nm[:, :], ones[:, :], ALU.mult).then_inc(cut_s, 1)
                        pool.wait_ge(cut_s, 3 * n + 1)
                        pool.tensor_tensor(nr[:, :], nm[:, :], mparts[:, 0, :], ALU.subtract).then_inc(cut_s, 1)
                        pool.wait_ge(cut_s, 3 * n + 2)
                        pool.tensor_tensor(mparts[:, 1, :], nr[:, :], ones[:, :], ALU.mult).then_inc(cut_s, 1)
                        pool.wait_ge(cut_s, 3 * n + 3)
                        pool.tensor_tensor(mparts[:, 2, :], nr[:, :], mparts[:, 1, :], ALU.subtract).then_inc(mp_s, 1)

                    base = xres if cross else hA
                    for t in range(NT):
                        pool.tensor_tensor(base[:, t, :], base[:, t, :], brow[:, ro, :], ALU.add).then_inc(xb_s, 1)
                    pool.wait_ge(v_s, v_units - v_mid)
                    for n in range(len(aq)):
                        v_piece(0, n, True)
                    pool.wait_ge(zero_s, 1)
                    minus_parts(0)
                    with pool.Fori(0, NG - 1) as g:
                        for q in range(1, NCH + 1):
                            minus_parts(g * NCH + q)
                        for n in range(len(aq)):
                            v_piece(g + 1, n, False)
                    for q in range(1, NCH):
                        minus_parts((NG - 1) * NCH + q)

                def copies(n):
                    return sum((min(hi, keys // P) > lo) + (hi > keys // P) for lo, hi in aq[:n])

                @block.vector
                def _(dve):
                    def entry(kind, r, what, n, base, g):
                        chunks = g * NCH
                        bank = PS[:, ring_bank(kind, r), :]
                        if what == "unit":
                            size = quarter[n % 4 + 1] - quarter[n % 4]
                            slot = n // UNITS % 2
                            dve.wait_ge(mx_s, base + n + 1)
                            dve.tensor_reduce(mxs[:, slot, n % UNITS // 4, n % 4:n % 4 + 1], bank[:, 0:size],
                                              AX.X, ALU.max).then_inc(md_s, 1)
                            if n % UNITS == UNITS - 1:
                                dve.wait_ge(md_s, base + n + 1)
                                dve.tensor_reduce(nm[:, :], mxs[:, slot], AX.X, ALU.max, negate=True).then_inc(nm_s, 1)
                        elif what == "out":
                            t4 = bank.rearrange("p (t h e) -> p t h e", t=4, h=HG)
                            dve.wait_ge(ut_s, chunks + n + 1)
                            if n == NCH - 1:
                                dve.wait_ge(un_s, chunks + n)
                            dve.reciprocal(rc[:, :, :], t4[:, :, :, DH]).then_inc(rc_s, 1)
                            dve.wait_ge(rc_s, chunks + n + 1)
                            c, of = (n, g) if n >= 0 else (NCH - 1, g - 1)
                            to = CTXO[:, 4 * c:4 * c + 4, ds(of * HG * DH, HG * DH)]
                            dve.tensor_tensor(to.rearrange("p t (h d) -> p t h d", h=HG), t4[:, :, :, 0:DH],
                                              rc[:, :, :].unsqueeze(3).to_broadcast([P, 4, HG, DH]),
                                              ALU.mult).then_inc(un_s, 1)

                    def group(g, kind):
                        for r, (what, n) in enumerate(rings[kind]):
                            entry(kind, r, what, n, g * NCH * UNITS, g)

                    dve.memset(mparts[:, :, :], 0.0).then_inc(zero_s, 1)
                    for r, (what, n) in enumerate(prologue):
                        entry("prologue", r, what, n, 0, 0)
                    group(0, "first")
                    with dve.Fori(1, NG - 1) as g:
                        group(g, "middle")
                    group(NG - 1, "last")

                @block.scalar
                def _(act):
                    for k in range(v_units - v_mid):
                        if k >= v_end:
                            act.wait_ge(vmm_s, k - v_end + 1)
                        v_copies(act, v_mid + k, PS[:, k % 4, :]).then_inc(v_s, 1)
                    act.activation(warm[:, 0:1], ident[:, 0:1], ACT.Exp).then_inc(exp_s, 1)
                    act.activation(warm[:, 1:2], ident[:, 0:1], ACT.Exp).then_inc(exp_s, 1)

                    def turned(n, bank):
                        act.wait_ge(mt_s, n + 1)
                        act.activation(mrow[0:16 * MROWS, :], PS[0:16 * MROWS, bank, 0:P // 2].bitcast(BF16),
                                       ACT.Copy).then_inc(mc_s, 1)

                    def sums(n):
                        act.wait_ge(pv_s, KT * (n + 1))
                        act.activation(U[:, :], PS[:, 6, :], ACT.Copy).then_inc(u_s, 1)

                    def group(g, kind):
                        chunks = g * NCH
                        for i in range(SLOTS):
                            kt = i % KT
                            rows = min(P, keys - kt * P)
                            for pair in range(2):
                                act.wait_ge(s_s, chunks * 2 * KT + 2 * i + pair + 1)
                                act.activation(PX[0:rows, i % 2, 2 * pair:2 * pair + 2, :],
                                               PS[0:rows, 2 * pair:2 * pair + 2, :], ACT.Exp,
                                               scale=DH ** -0.5).then_inc(exp_s, 1)
                            if ("turn", turns.get(i)) in rings[kind]:
                                r = rings[kind].index(("turn", turns[i]))
                                turned(chunks + turns[i], ring_bank(kind, r))
                            if kt == 0 and (i or kind != "first"):
                                sums(chunks + i // KT - 1)

                    turned(0, ring_bank("prologue", prologue.index(("turn", 0))))
                    group(0, "first")
                    with act.Fori(1, NG - 1) as g:
                        group(g, "middle")
                    group(NG - 1, "last")
                    sums(NG * NCH - 1)

                @block.tensor
                def _(pe):
                    def entry(kind, r, what, n, base, g):
                        chunks = g * NCH
                        bank = PS[:, ring_bank(kind, r), :]
                        if what == "unit":
                            q = n // UNITS
                            head, tile, k = n % UNITS // 16, n % 16 // 4, n % 4
                            if n % UNITS == 0:
                                pe.wait_ge(q_in[q % NCH], (g + 1 + q // NCH) * 16 * len(Q_PARTS))
                                if q % NCH == 0:
                                    pe.wait_ge(kb_in, (g + 1 + q // NCH) * 16 * len(K_PARTS))
                                if q == 2:
                                    for m in ka_in:
                                        pe.wait_ge(m, (g + 1) * 16 * len(K_PARTS))
                            bank_free(pe, kind, r, base, chunks)
                            source = KA if q in (2, 3) else KB
                            lo, hi = quarter[k], quarter[k + 1]
                            pe.matmul(bank[:, 0:hi - lo], Q[0:ROWS, q % NCH, head, tile * P:(tile + 1) * P],
                                      source[0:ROWS, head, lo:hi], start=True, stop=True).then_inc(mx_s, 1)
                        elif what == "turn":
                            pe.wait_ge(mp_s, chunks + n + 1)
                            bank_free(pe, kind, r, base, chunks)
                            pe.transpose(bank[:, 0:P // 2].bitcast(BF16),
                                         mparts[:, :, :].rearrange("p a b -> p (a b)"), identb[:, :]).then_inc(mt_s, 1)
                        else:
                            pe.wait_ge(u_s, chunks + n + 1)
                            bank_free(pe, kind, r, base, chunks)
                            for t in range(4):
                                mm = pe.transpose(bank[:, t * P:(t + 1) * P], U[:, t * P:(t + 1) * P], ident[:, :])
                            mm.then_inc(ut_s, 1)

                    def scores(g, i, pair):
                        chunks = g * NCH
                        c, kt = divmod(i, KT)
                        rows = min(P, keys - kt * P)
                        if kt == 0 and pair == 0:
                            pe.wait_ge(mrow_in, 16 * MROWS * (chunks + c + 1))
                        if c == 0 and pair == 0:
                            for n, (lo, _) in enumerate(aq):
                                if kt == lo:
                                    pe.wait_ge(ka_in[n], (g + 1) * 16 * len(K_PARTS))
                        pe.wait_ge(exp_s, chunks * 2 * KT + 2 * i + pair + 1)
                        for h in (2 * pair, 2 * pair + 1):
                            mm = pe.matmul(PS[0:rows, h, :], KA[0:ROWS + MROWS, h, kt * P:kt * P + rows],
                                           Q[0:ROWS + MROWS, c, h, :], start=True, stop=True)
                        mm.then_inc(s_s, 1)

                    def products(g, i):
                        chunks = g * NCH
                        c, kt = divmod(i, KT)
                        rows = min(P, keys - kt * P)
                        if c == 0:
                            for n, (lo, _) in enumerate(aq):
                                if kt == lo:
                                    pe.wait_ge(vg_s, g * copies(len(aq)) + copies(n + 1))
                        if kt == 0 and not (c == 0 and isinstance(g, int) and g == 0):
                            pe.wait_ge(u_s, chunks + c)
                        pe.wait_ge(exp_s, chunks * 2 * KT + 2 * i + 4)
                        for h in range(HG):
                            mm = pe.matmul(PS[32 * h:32 * h + 32, 6, :], VG[0:rows, kt, h, :],
                                           PX[0:rows, i % 2, h, :], start=(kt == 0), stop=(kt == KT - 1))
                        mm.then_inc(pv_s, 1)

                    def group(g, kind):
                        base = g * NCH * UNITS
                        first, last = kinds[kind]
                        r = 0
                        for i in range(SLOTS):
                            units, turned = slot_units(i, last), slot_turned(i, first, last)
                            steps = [lambda: scores(g, i, 0), lambda: scores(g, i, 1)]
                            if i or not first:
                                steps.append(lambda: products(g, i - 1))
                            cuts = (0, 1, 3, len(units))
                            for k, do in enumerate(steps):
                                do()
                                for what, n in units[cuts[k]:cuts[k + 1]]:
                                    entry(kind, r, what, n, base, g)
                                    r += 1
                            if len(steps) == 2:
                                for what, n in units[3:]:
                                    entry(kind, r, what, n, base, g)
                                    r += 1
                            for what, n in turned:
                                entry(kind, r, what, n, base, g)
                                r += 1
                        if last:
                            products(g, SLOTS - 1)
                            entry(kind, r, "out", NCH - 1, base, g)

                    pe.wait_ge(one_s, 1)
                    for r, (what, n) in enumerate(prologue):
                        if r % 4 == 0 and r // 4 < v_units - v_mid - v_end:
                            k = v_end + r // 4
                            pe.wait_ge(v_s, k - 3)
                            v_products(pe, v_mid + k, PS[:, k % 4, :]).then_inc(vmm_s, 1)
                        entry("prologue", r, what, n, 0, 0)
                    pe.wait_ge(ka1_s, 1)
                    group(0, "first")
                    with pe.Fori(1, NG - 1) as g:
                        group(g, "middle")
                    group(NG - 1, "last")
            return un_s

        heads_layer("c", CTX, W2Q, B2Q, B2K, R2V, R2O, None)
        heads_layer("s", N, W3Q, B3Q, B3K, R3V, RBE1, W2O)

        We, a = carve(0, [DC, NE, D])
        AO, a = carve(a, [NT, D])
        YT, a = carve(a, [DC, N])
        MO, a = carve(a, [NT, D])
        wT, a = carve(a, [NCH, CH])
        small = {}
        for name in ("lg", "sh", "ex", "pr", "q1", "o1", "p2", "q2", "o2", "wt", "oo"):
            small[name], a = carve(a, [NT, NE])
        for name in ("mx", "sm", "rc", "m1", "a1", "m2", "a2"):
            small[name], a = carve(a, [NT])
        rev, a = carve(a, [NE])
        stats2, a = carve(a, [NT, 6])
        mv2, a = carve(a, [NT, 2])
        var2, a = carve(a, [NT])
        rstd2, a = carve(a, [NT])
        mr, a = carve(a, [NT])
        nb, a = carve(a, [NT])
        mr2, a = carve(a, [NT])
        nb2, a = carve(a, [NT])
        units = []
        for n in range(NCH + 1):
            if n < NCH:
                units += [("C", n, c, "act") for c in range(DC)]
            if n:
                units += [("O", v, 0, "dve") for v in (2 * n - 2, 2 * n - 1)]

        units += [("T", 0, c, "act") for c in range(DC)] + [("G", 0, 0, "dve")]
        for t in range(NT):
            n = t // 4
            units += [("M", t, e, "dve") for e in range(NE // 2 - 1)]
            if t % 4 == 0:
                units += [("R", n, 0, "act")]
            if t % 4 == 2 and n + 1 < NCH:
                units += [("T", n + 1, c, "act") for c in range(DC)]
            units += [("M", t, NE // 2 - 1, "dve")]
            if t % 4 == 0:
                units += [("B", v, 0, "act") for v in (2 * n, 2 * n + 1)]
            if t % 4 == 2 and n + 1 < NCH:
                units += [("G", n + 1, 0, "dve")]
        fsem = {n: sem("f_" + n) for n in (
            "we", "pe", "act", "dve", "stat", "mv", "chain", "nb", "n", "ng", "y", "g", "ex", "w", "mo", "stat2",
            "mv2", "n2", "ng2", "res", "o", "out", "rev")}
        LAG = 3
        pe_s, act_s, dve_s = fsem["pe"], fsem["act"], fsem["dve"]

        def emptied(u):
            same = sum(1 for w in units[:u + 1] if w[3] == units[u][3])
            return (act_s if units[u][3] == "act" else dve_s), same

        def index(what, i, m=0):
            return next(n for n, w in enumerate(units) if w[:3] == (what, i, m))

        def brows4(r):
            return brow[:, r, :].unsqueeze(1).to_broadcast([P, 4, D])

        with nc.Block() as block:
            @block.sync
            def _(sp):
                sp.dma_start(We[:, 0, :, :], we[:, 0:P, :].rearrange("e p f -> p e f")).then_inc(fsem["we"], 16)
                sp.dma_start(We[:, 1, :, :], we[:, P:D, :].rearrange("e p f -> p e f")).then_inc(fsem["we"], 16)
                o = out.rearrange("(t p) d -> p t d", p=P)
                for t in range(0, NT, 2):
                    sp.wait_ge(fsem["o"], t + 2)
                    sp.dma_start(o[:, t:t + 2, :], MO[:, t:t + 2, :]).then_inc(fsem["out"], 16)
                sp.wait_ge(fsem["out"], 16 * (NT // 2))

            @block.gpsimd
            def _(pool):
                for e in range(NE):
                    pool.memset(rev[:, e:e + 1], float(NE - e)).then_inc(fsem["rev"], 1)
                def scale_and_bias(n, r, aggregated, count, m, v, to, by, minus):
                    chain = fsem["chain"]
                    pool.wait_ge(aggregated, count)
                    pool.tensor_scalar(v[:, r], m[:, r, 1], EPS, None, ALU.add).then_inc(chain, 1)
                    pool.wait_ge(chain, 3 * n + 1)
                    pool.tensor_tensor(to[:, r], v[:, r], mhalf[:, r], ALU.pow).then_inc(chain, 1)
                    pool.wait_ge(chain, 3 * n + 2)
                    pool.tensor_tensor(by[:, r], m[:, r, 0], to[:, r], ALU.mult).then_inc(chain, 1)
                    pool.wait_ge(chain, 3 * n + 3)
                    pool.tensor_scalar(minus[:, r], by[:, r], -1.0, None, ALU.mult).then_inc(fsem["nb"], 1)

                for g in range(NCH):
                    scale_and_bias(g, slice(4 * g, 4 * g + 4), fsem["mv"], 4 * g + 4, mv, vareps, rstd, mr, nb)
                for g in range(NCH):
                    r = slice(4 * g, 4 * g + 4)
                    pool.wait_ge(fsem["y"], g + 1)
                    pool.tensor_tensor(xres[:, r, :], xres[:, r, :], hA[:, r, :], ALU.add).then_inc(fsem["res"], 1)
                    pool.wait_ge(fsem["res"], 2 * g + 1)
                    pool.tensor_tensor(xres[:, r, :], xres[:, r, :], brows4(RBE2), ALU.add).then_inc(fsem["res"], 1)
                for t in range(NT):
                    scale_and_bias(NCH + t, slice(t, t + 1), fsem["mv2"], t + 1, mv2, var2, rstd2, mr2, nb2)

            @block.vector
            def _(dve):
                def attention_output(g):
                    for v in (2 * g, 2 * g + 1):
                        u = index("O", v)
                        dve.wait_ge(pe_s, u + 1)
                        bias = brow[:, R3O, :].unsqueeze(1).to_broadcast([P, 2, D])
                        dve.tensor_tensor(AO[:, 2 * v:2 * v + 2, :], PS[:, u % 8, :].rearrange("p (t d) -> p t d", t=2),
                                          bias, ALU.add).then_inc(dve_s, 1)
                    dve.wait_ge(dve_s, 2 * g + 2)
                    for t in range(4 * g, 4 * g + 4):
                        dve.bn_stats(stats[:, t, :], AO[:, t, :]).then_inc(fsem["stat"], 1)
                    for t in range(4 * g, 4 * g + 4):
                        dve.wait_ge(fsem["stat"], t + 1)
                        dve.bn_aggr(mv[:, t, :], stats[:, t, :]).then_inc(fsem["mv"], 1)

                def experts_input(g):
                    r = slice(4 * g, 4 * g + 4)
                    dve.wait_ge(fsem["n"], 4 * g + 4)
                    dve.tensor_tensor(AO[:, r, :], AO[:, r, :], brows4(RG1), ALU.mult).then_inc(fsem["ng"], 1)
                    dve.wait_ge(fsem["ng"], g + 1)
                    dve.tensor_tensor(hA[:, r, :], hA[:, r, :], AO[:, r, :], ALU.add).then_inc(fsem["y"], 1)

                def gate(g):
                    r = slice(4 * g, 4 * g + 4)
                    u = index("G", g)
                    n = [16 * g]
                    gs = fsem["g"]

                    def chain(ins):
                        ins.then_inc(gs, 1)
                        n[0] += 1
                        dve.wait_ge(gs, n[0])

                    def b(name):
                        return small[name][:, r].unsqueeze(2).to_broadcast([P, 4, NE])

                    s = {k: v[:, r] for k, v in small.items()}
                    revb = rev[:, :].unsqueeze(1).to_broadcast([P, 4, NE])
                    dve.wait_ge(pe_s, u + 1)
                    dve.tensor_tensor(s["lg"], PS[:, u % 8, 0:4 * NE].rearrange("p (t e) -> p t e", t=4),
                                      bgrow[:, :].unsqueeze(1).to_broadcast([P, 4, NE]), ALU.add).then_inc(dve_s, 1)
                    dve.wait_ge(*emptied(u))
                    chain(dve.tensor_reduce(s["mx"], s["lg"], AX.X, ALU.max))
                    chain(dve.tensor_tensor(s["sh"], s["lg"], b("mx"), ALU.subtract))
                    dve.wait_ge(fsem["ex"], g + 1)
                    chain(dve.tensor_reduce(s["sm"], s["ex"], AX.X, ALU.add))
                    chain(dve.reciprocal(s["rc"], s["sm"]))
                    chain(dve.tensor_tensor(s["pr"], s["ex"], b("rc"), ALU.mult))
                    chain(dve.tensor_reduce(s["m1"], s["pr"], AX.X, ALU.max))
                    chain(dve.tensor_tensor(s["q1"], s["pr"], b("m1"), ALU.is_equal))
                    chain(dve.tensor_tensor(s["o2"], s["q1"], revb, ALU.mult))
                    chain(dve.tensor_reduce(s["a1"], s["o2"], AX.X, ALU.max))
                    chain(dve.tensor_tensor(s["o1"], s["o2"], b("a1"), ALU.is_equal))
                    chain(dve.scalar_tensor_tensor(s["p2"], s["o1"], -2.0, s["pr"], ALU.mult, ALU.add))
                    chain(dve.tensor_reduce(s["m2"], s["p2"], AX.X, ALU.max))
                    chain(dve.tensor_tensor(s["q2"], s["p2"], b("m2"), ALU.is_equal))
                    chain(dve.tensor_tensor(s["oo"], s["q2"], revb, ALU.mult))
                    chain(dve.tensor_reduce(s["a2"], s["oo"], AX.X, ALU.max))
                    chain(dve.tensor_tensor(s["q1"], s["oo"], b("a2"), ALU.is_equal))
                    assert n[0] == 16 * g + 16
                    dve.tensor_tensor(s["q2"], s["q1"], s["o1"], ALU.add).then_inc(fsem["w"], 1)
                    dve.wait_ge(fsem["w"], 2 * g + 1)
                    dve.tensor_tensor(s["wt"], s["q2"], s["pr"], ALU.mult).then_inc(fsem["w"], 1)

                mo = [0]

                def experts(t):
                    for e in range(NE // 2):
                        u = index("M", t, e)
                        dve.wait_ge(pe_s, u + 1)
                        if e == 0:
                            dve.wait_ge(*emptied(index("B", t // 2)))
                        for k in range(2):
                            if e or k:
                                dve.wait_ge(fsem["mo"], mo[0])
                            ins = dve.scalar_tensor_tensor(MO[:, t, :], PS[:, u % 8, k * D:(k + 1) * D],
                                                           small["wt"][:, t, 2 * e + k:2 * e + k + 1], MO[:, t, :],
                                                           ALU.mult, ALU.add)
                            if k == 0:
                                ins.then_inc(fsem["mo"], 1)
                                mo[0] += 1
                            else:
                                ins.then_inc(dve_s, 1)
                                dve.wait_ge(*emptied(u))

                def experts_stats(t):
                    dve.wait_ge(dve_s, emptied(index("M", t, NE // 2 - 1))[1])
                    dve.bn_stats(stats2[:, t, :], MO[:, t, :]).then_inc(fsem["stat2"], 1)
                    dve.wait_ge(fsem["stat2"], t + 1)
                    dve.bn_aggr(mv2[:, t, :], stats2[:, t, :]).then_inc(fsem["mv2"], 1)

                def finish(t):
                    dve.wait_ge(fsem["n2"], t + 1)
                    dve.tensor_tensor(MO[:, t, :], MO[:, t, :], brow[:, RG2, :], ALU.mult).then_inc(fsem["ng2"], 1)
                    dve.wait_ge(fsem["ng2"], t + 1)
                    dve.wait_ge(fsem["res"], 2 * (t // 4) + 2)
                    dve.tensor_tensor(MO[:, t, :], MO[:, t, :], xres[:, t, :], ALU.add).then_inc(fsem["o"], 1)

                attention_output(0)
                attention_output(1)
                experts_input(0)
                attention_output(2)
                experts_input(1)
                attention_output(3)
                dve.wait_ge(fsem["rev"], NE)
                gate(0)
                experts_input(2)
                for t in range(NT):
                    if t % 4 == 0:
                        dve.wait_ge(fsem["w"], 2 * (t // 4) + 2)
                    experts(t)
                    experts_stats(t)
                    if t == 0:
                        experts_input(3)
                    if t % 4 == 2 and t // 4 + 1 < NCH:
                        gate(t // 4 + 1)
                    if t >= LAG:
                        finish(t - LAG)
                for t in range(NT - LAG, NT):
                    finish(t)

            @block.scalar
            def _(act):
                def normalize(r, to, scale, bias, counted, s):
                    act.wait_ge(fsem["nb"], counted)
                    for t in r:
                        act.activation(to[:, t, :], to[:, t, :], ACT.Identity, bias=bias[:, t:t + 1],
                                       scale=scale[:, t:t + 1]).then_inc(s, 1)

                def normalize_attention(g):
                    normalize(range(4 * g, 4 * g + 4), AO, rstd, nb, g + 1, fsem["n"])

                def normalize_experts(t):
                    normalize(range(t, t + 1), MO, rstd2, nb2, NCH + t + 1, fsem["n2"])

                for u, (what, i, m, by) in enumerate(units):
                    if what == "G":
                        act.wait_ge(fsem["g"], 16 * i + 2)
                        act.activation(small["ex"][:, 4 * i:4 * i + 4], small["sh"][:, 4 * i:4 * i + 4],
                                       ACT.Exp).then_inc(fsem["ex"], 1)
                    if what == "M" and m == NE // 2 - 1 and i >= LAG - 1:
                        normalize_experts(i - LAG + 1)
                    if by != "act":
                        continue
                    if (what, i, m) == ("R", 0, 0):
                        normalize_attention(2)
                    if (what, i, m) == ("R", 0, 0):
                        normalize_attention(3)
                    act.wait_ge(pe_s, u + 1)
                    if what == "C":
                        act.activation(hT[:, m, i * CH:(i + 1) * CH], PS[:, u % 8, :], ACT.Copy).then_inc(act_s, 1)
                        if m == DC - 1 and i >= 2:
                            normalize_attention(i - 2)
                    elif what == "T":
                        act.activation(YT[:, m, i * CH:(i + 1) * CH], PS[:, u % 8, :], ACT.Copy).then_inc(act_s, 1)
                    elif what == "R":
                        act.activation(wT[0:NE, i, :], PS[0:NE, u % 8, :], ACT.Copy).then_inc(act_s, 1)
                    else:
                        act.activation(MO[:, 2 * i:2 * i + 2, :], PS[:, u % 8, :].rearrange("p (t d) -> p t d", t=2),
                                       ACT.Copy).then_inc(act_s, 1)

                for t in range(NT - LAG + 1, NT):
                    normalize_experts(t)

            @block.tensor
            def _(pe):
                for u, (what, i, m, _) in enumerate(units):
                    if u >= 8:
                        pe.wait_ge(*emptied(u - 8))
                    bank = PS[:, u % 8, :]
                    if what in "CT":
                        if what == "T":
                            pe.wait_ge(fsem["y"], i + 1)
                        source = hA if what == "T" else CTXO
                        for j in range(4):
                            mm = pe.transpose(bank[:, j * P:(j + 1) * P], source[:, 4 * i + j, m * P:(m + 1) * P],
                                              ident[:, :])
                    elif what == "O":
                        pe.wait_ge(*emptied(index("C", i // 2, 1)))
                        for j in range(2):
                            t = 2 * i + j
                            for c in range(DC):
                                mm = pe.matmul(bank[:, j * D:(j + 1) * D], hT[:, c, t * P:(t + 1) * P],
                                               W[:, W3O, c, :], start=(c == 0), stop=(c == DC - 1))
                    elif what == "G":
                        pe.wait_ge(*emptied(index("T", i, 1)))
                        for j in range(4):
                            t = 4 * i + j
                            for c in range(DC):
                                mm = pe.matmul(bank[:, j * NE:(j + 1) * NE], YT[:, c, t * P:(t + 1) * P],
                                               Wg[:, c, :], start=(c == 0), stop=(c == DC - 1))
                    elif what == "R":
                        pe.wait_ge(fsem["w"], 2 * i + 2)
                        for j in range(4):
                            mm = pe.transpose(bank[0:NE, j * P:(j + 1) * P], small["wt"][:, 4 * i + j, :], ident[:, :])
                    elif what == "B":
                        pe.wait_ge(*emptied(index("R", i // 2)))
                        for j in range(2):
                            t = 2 * i + j
                            mm = pe.matmul(bank[:, j * D:(j + 1) * D], wT[0:NE, t // 4, t % 4 * P:(t % 4 + 1) * P],
                                           bexp_sb[:, :], start=True, stop=True)
                    else:
                        if (i, m) == (0, 0):
                            pe.wait_ge(fsem["we"], 32)
                        for c in range(DC):
                            mm = pe.matmul(bank, YT[:, c, i * P:(i + 1) * P],
                                           We[:, c, 2 * m:2 * m + 2, :].rearrange("p e f -> p (e f)"),
                                           start=(c == 0), stop=(c == DC - 1))
                    mm.then_inc(pe_s, 1)


def kernel(**inputs):
    import numpy as np
    import concourse.bacc as bacc
    from concourse.bass_utils import run_bass_kernel_spmd

    i = {k: np.asarray(v) for k, v in inputs.items()}
    t = np.ascontiguousarray
    kv = i["L0_xattn_Wkv"].reshape(H, 2, DH, CW)
    bkv = i["L0_xattn_bkv"].reshape(H, 2, DH)
    columns = [i["L0_attn_bq"], i["L0_attn_bk"], i["L0_xattn_bq"], bkv[:, 0].reshape(D), i["L0_ffn_bq"],
               i["L0_ffn_bk"]]
    arrays = {
        "x": t(i["x"][0]),
        "ctxT": t(i["ctx_768"][0].T),
        "wpack": t(np.stack([i["L0_attn_Wq"].T, i["L0_attn_Wk"].T, i["L0_attn_Wv"].T, i["L0_xattn_Wq"].T,
                             i["L0_xattn_Wo"].T, i["L0_ffn_Wq"], i["L0_ffn_Wk"], i["L0_ffn_Wv"],
                             i["L0_ffn_Wo"]])),
        "wkv": t(np.concatenate([kv[:, 0].reshape(D, CW).T, kv[:, 1].reshape(D, CW).T], 1)),
        "we": t(i["L0_ffn_We"]),
        "wg": t(i["L0_ffn_Wg"]),
        "bcols": t(np.stack([b.reshape(DC, P)[c] for b in columns for c in range(DC)], 1)),
        "brows": t(np.stack([i["L0_attn_bv"], bkv[:, 1].reshape(D), i["L0_xattn_bo"], i["L0_ffn_bv"],
                             i["L0_ffn_bo"], i["L0_ffn_g1"], i["L0_ffn_be1"], i["L0_ffn_g2"],
                             i["L0_ffn_be2"]])),
        "bg": t(i["L0_ffn_bg"]),
        "bexp": t(i["L0_ffn_bexp"]),
    }
    nc = bacc.Bacc("TRN2", target_bir_lowering=False, num_devices=1)
    args = [nc.dram_tensor(n, a.shape, mybir.dt.from_np(a.dtype), kind="ExternalInput").ap()
            for n, a in arrays.items()]
    out = nc.dram_tensor("out", (N, D), F32, kind="ExternalOutput").ap()
    build(nc, *args, out)
    r = run_bass_kernel_spmd(nc, [arrays], core_ids=[0])
    return r.results[0]["out"].reshape(1, N, D)
```
